# Optimizing a Trainium2 kernel written in Bass

```python
import numpy as np
import jax
import jax.numpy as jnp

def _softmax(x, axis=-1):
    return jax.nn.softmax(x, axis=axis)

def _gelu(x):
    return jax.nn.gelu(x, approximate=True)

def _silu(x):
    return jax.nn.silu(x)

def _sigmoid(x):
    return jax.nn.sigmoid(x)

def _layernorm(x, axis=-1, eps=1e-05):
    m = jnp.mean(x, axis=axis, keepdims=True)
    v = jnp.var(x, axis=axis, keepdims=True)
    return (x - m) / jnp.sqrt(v + eps)

def _scatter_add(tgt, idx, src, axis=0):
    return tgt.at[idx].add(src)

def _segment_sum(src, seg, n):
    return jax.ops.segment_sum(src, seg, n)
kernel_name = 'mk_cond_seq_d2_seqx_r4_205206'

def setup_inputs(seed: int=0):
    np.random.seed(seed)
    _w = jnp.asarray

    def _rec_inputs():
        import jax
        import jax.numpy as jnp
        _rk = jax.random.key(seed)
        x = -0.000125 + 0.9999 * jax.random.normal(jax.random.fold_in(_rk, 1), (64, 64, 256), jnp.float32)
        _lenS = 64 - jax.random.randint(jax.random.fold_in(_rk, 7), (64,), 0, max(1, 64 // 4) + 1, jnp.int32)
        _lenS2 = 64 - jax.random.randint(jax.random.fold_in(_rk, 8), (64,), 0, max(1, 64 // 4) + 1, jnp.int32)
        itok_B_0_15 = jax.random.randint(jax.random.fold_in(_rk, 11), (64,), 0, 16, jnp.int32)
        itok_B_6_14 = jax.random.randint(jax.random.fold_in(_rk, 12), (64,), 6, 15, jnp.int32)
        return (x, itok_B_0_15, itok_B_6_14)
    x, itok_B_0_15, itok_B_6_14 = _rec_inputs()

    def _L0_cond_setup():
        import jax, jax.numpy as jnp
        import numpy as np
        B, S, D = (32, 256, 256)
        A = 64
        E = 16
        LN_EPS = 1e-05
        key = jax.random.key(seed)
        ks = jax.random.split(key, 10)
        s = lambda fan_in: 1.0 / np.sqrt(fan_in)
        return {'hidden_states': jax.random.normal(ks[0], (B, S, D), dtype=jnp.float32), 'domain_id': jax.random.randint(ks[1], (B,), 0, E, dtype=jnp.int64), 'down_W': jax.random.uniform(ks[2], (A, D), jnp.float32, -s(D), s(D)), 'down_b': jax.random.uniform(ks[3], (A,), jnp.float32, -s(D), s(D)), 'up_W': jax.random.uniform(ks[4], (D, A), jnp.float32, -s(A), s(A)), 'up_b': jax.random.uniform(ks[5], (D,), jnp.float32, -s(A), s(A)), 'expert_W': jax.random.uniform(ks[6], (E, A, A), jnp.float32, -s(A), s(A)), 'expert_b': jax.random.uniform(ks[7], (E, A), jnp.float32, -s(A), s(A)), 'domain_emb': jax.random.normal(ks[8], (E, A), dtype=jnp.float32), 'ln_gamma': jnp.ones((D,), jnp.float32), 'ln_beta': jnp.zeros((D,), jnp.float32)}
    _L0_cond_all = _L0_cond_setup()
    _L0_cond_in = {k: v for k, v in _L0_cond_all.items() if k in ('down_W', 'down_b', 'up_W', 'up_b', 'expert_W', 'expert_b', 'domain_emb', 'ln_gamma', 'ln_beta')}
    del _L0_cond_all

    def _L1_cond_setup():
        import jax, jax.numpy as jnp
        import numpy as np
        D = 256
        E = 8
        FF = 1024
        TOPK = 2
        S = 32
        SE = 64
        SH = 128
        B, T = (2, 512)

        def _forward(x, subject_ids, ln_g, ln_b, subj_emb, hyp_w1, hyp_b1, hyp_w2, hyp_b2, sty_w1, sty_b1, sty_w2, sty_b2, router_w, exp_w1, exp_b1, exp_w2, exp_b2):
            mu = x.mean(-1, keepdims=True)
            var = x.var(-1, keepdims=True)
            h = (x - mu) * jax.lax.rsqrt(var + 1e-05) * ln_g + ln_b
            m_t = h.mean(1, keepdims=True)
            v_t = h.var(1, keepdims=True)
            h_norm = (h - m_t) * jax.lax.rsqrt(v_t + 1e-08)
            se = subj_emb[subject_ids]
            hyp = jax.nn.relu(se @ hyp_w1 + hyp_b1) @ hyp_w2 + hyp_b2
            sty = jax.nn.relu(hyp @ sty_w1 + sty_b1) @ sty_w2 + sty_b2
            gamma, beta = jnp.split(sty, 2, axis=-1)
            gamma = jax.nn.softplus(gamma) + 1e-08
            h = h_norm * gamma[:, None, :] + beta[:, None, :]
            h_flat = h.reshape(-1, D)
            probs = jax.nn.softmax(h_flat @ router_w, axis=-1)
            gates, idx = jax.lax.top_k(probs, TOPK)
            gates = gates / gates.sum(-1, keepdims=True)
            N = h_flat.shape[0]
            combine = jnp.zeros((N, E), h_flat.dtype).at[jnp.arange(N)[:, None], idx].add(gates)
            hid = jax.nn.relu(jnp.einsum('nd,edf->nef', h_flat, exp_w1) + exp_b1)
            eout = jnp.einsum('nef,efd->ned', hid, exp_w2) + exp_b2
            y = jnp.einsum('ned,ne->nd', eout, combine)
            return x + y.reshape(x.shape)
        key = jax.random.key(seed)
        ks = jax.random.split(key, 16)
        n = lambda k, sh, s=0.02: jax.random.normal(k, sh, dtype=jnp.float32) * s
        return {'x': jax.random.normal(ks[0], (B, T, D), dtype=jnp.float32), 'subject_ids': jax.random.randint(ks[1], (B,), 0, S), 'ln_g': jnp.ones((D,), jnp.float32), 'ln_b': jnp.zeros((D,), jnp.float32), 'subj_emb': n(ks[2], (S, SE)), 'hyp_w1': n(ks[3], (SE, SH), 1.0 / np.sqrt(SE)), 'hyp_b1': jnp.zeros((SH,), jnp.float32), 'hyp_w2': n(ks[4], (SH, SH), 1.0 / np.sqrt(SH)), 'hyp_b2': jnp.zeros((SH,), jnp.float32), 'sty_w1': n(ks[5], (SH, SH // 2), 1.0 / np.sqrt(SH)), 'sty_b1': jnp.zeros((SH // 2,), jnp.float32), 'sty_w2': n(ks[6], (SH // 2, 2 * D), 1.0 / np.sqrt(SH // 2)), 'sty_b2': jnp.zeros((2 * D,), jnp.float32), 'router_w': n(ks[7], (D, E), 1.0 / np.sqrt(D)), 'exp_w1': n(ks[8], (E, D, FF), 1.0 / np.sqrt(D)), 'exp_b1': jnp.zeros((E, FF), jnp.float32), 'exp_w2': n(ks[9], (E, FF, D), 1.0 / np.sqrt(FF)), 'exp_b2': jnp.zeros((E, D), jnp.float32)}
    _L1_cond_all = _L1_cond_setup()
    _L1_cond_in = {k: v for k, v in _L1_cond_all.items() if k in ('ln_g', 'ln_b', 'subj_emb', 'hyp_w1', 'hyp_b1', 'hyp_w2', 'hyp_b2', 'sty_w1', 'sty_b1', 'sty_w2', 'sty_b2', 'router_w', 'exp_w1', 'exp_b1', 'exp_w2', 'exp_b2')}
    del _L1_cond_all
    return {'x': x, 'itok_B_0_15': itok_B_0_15, 'itok_B_6_14': itok_B_6_14, 'L0_cond_down_W': _L0_cond_in['down_W'], 'L0_cond_down_b': _L0_cond_in['down_b'], 'L0_cond_up_W': _L0_cond_in['up_W'], 'L0_cond_up_b': _L0_cond_in['up_b'], 'L0_cond_expert_W': _L0_cond_in['expert_W'], 'L0_cond_expert_b': _L0_cond_in['expert_b'], 'L0_cond_domain_emb': _L0_cond_in['domain_emb'], 'L0_cond_ln_gamma': _L0_cond_in['ln_gamma'], 'L0_cond_ln_beta': _L0_cond_in['ln_beta'], 'L1_cond_ln_g': _L1_cond_in['ln_g'], 'L1_cond_ln_b': _L1_cond_in['ln_b'], 'L1_cond_subj_emb': _L1_cond_in['subj_emb'], 'L1_cond_hyp_w1': _L1_cond_in['hyp_w1'], 'L1_cond_hyp_b1': _L1_cond_in['hyp_b1'], 'L1_cond_hyp_w2': _L1_cond_in['hyp_w2'], 'L1_cond_hyp_b2': _L1_cond_in['hyp_b2'], 'L1_cond_sty_w1': _L1_cond_in['sty_w1'], 'L1_cond_sty_b1': _L1_cond_in['sty_b1'], 'L1_cond_sty_w2': _L1_cond_in['sty_w2'], 'L1_cond_sty_b2': _L1_cond_in['sty_b2'], 'L1_cond_router_w': _L1_cond_in['router_w'], 'L1_cond_exp_w1': _L1_cond_in['exp_w1'], 'L1_cond_exp_b1': _L1_cond_in['exp_b1'], 'L1_cond_exp_w2': _L1_cond_in['exp_w2'], 'L1_cond_exp_b2': _L1_cond_in['exp_b2']}

def reference(x, itok_B_0_15, itok_B_6_14, L0_cond_down_W, L0_cond_down_b, L0_cond_up_W, L0_cond_up_b, L0_cond_expert_W, L0_cond_expert_b, L0_cond_domain_emb, L0_cond_ln_gamma, L0_cond_ln_beta, L1_cond_ln_g, L1_cond_ln_b, L1_cond_subj_emb, L1_cond_hyp_w1, L1_cond_hyp_b1, L1_cond_hyp_w2, L1_cond_hyp_b2, L1_cond_sty_w1, L1_cond_sty_b1, L1_cond_sty_w2, L1_cond_sty_b2, L1_cond_router_w, L1_cond_exp_w1, L1_cond_exp_b1, L1_cond_exp_w2, L1_cond_exp_b2):
    import jax
    import jax.numpy as jnp

    def _L0_cond_ref(hidden_states, domain_id, down_W, down_b, up_W, up_b, expert_W, expert_b, domain_emb, ln_gamma, ln_beta):
        import jax, jax.numpy as jnp
        import numpy as np
        B, S, D = (32, 256, 256)
        A = 64
        E = 16
        LN_EPS = 1e-05
        residual = hidden_states
        hidden = jnp.einsum('bsd,ad->bsa', hidden_states, down_W) + down_b
        hidden = jax.nn.gelu(hidden, approximate=False)
        valid = (domain_id >= 0) & (domain_id < E)
        idx = jnp.clip(domain_id, 0, E - 1)
        Wsel = expert_W[idx]
        bsel = expert_b[idx]
        expert_out = jnp.einsum('bsa,boa->bso', hidden, Wsel) + bsel[:, None, :]
        domain_output = jnp.where(valid[:, None, None], expert_out, hidden)
        hidden = domain_output + domain_emb[idx][:, None, :]
        hidden = jnp.einsum('bsa,da->bsd', hidden, up_W) + up_b
        x = hidden + residual
        mu = jnp.mean(x, axis=-1, keepdims=True)
        var = jnp.mean(jnp.square(x - mu), axis=-1, keepdims=True)
        return (x - mu) * jax.lax.rsqrt(var + LN_EPS) * ln_gamma + ln_beta

    def _L1_cond_ref(x, subject_ids, ln_g, ln_b, subj_emb, hyp_w1, hyp_b1, hyp_w2, hyp_b2, sty_w1, sty_b1, sty_w2, sty_b2, router_w, exp_w1, exp_b1, exp_w2, exp_b2):
        import jax, jax.numpy as jnp
        import numpy as np
        D = 256
        E = 8
        FF = 1024
        TOPK = 2
        S = 32
        SE = 64
        SH = 128
        B, T = (2, 512)

        def _forward(x, subject_ids, ln_g, ln_b, subj_emb, hyp_w1, hyp_b1, hyp_w2, hyp_b2, sty_w1, sty_b1, sty_w2, sty_b2, router_w, exp_w1, exp_b1, exp_w2, exp_b2):
            mu = x.mean(-1, keepdims=True)
            var = x.var(-1, keepdims=True)
            h = (x - mu) * jax.lax.rsqrt(var + 1e-05) * ln_g + ln_b
            m_t = h.mean(1, keepdims=True)
            v_t = h.var(1, keepdims=True)
            h_norm = (h - m_t) * jax.lax.rsqrt(v_t + 1e-08)
            se = subj_emb[subject_ids]
            hyp = jax.nn.relu(se @ hyp_w1 + hyp_b1) @ hyp_w2 + hyp_b2
            sty = jax.nn.relu(hyp @ sty_w1 + sty_b1) @ sty_w2 + sty_b2
            gamma, beta = jnp.split(sty, 2, axis=-1)
            gamma = jax.nn.softplus(gamma) + 1e-08
            h = h_norm * gamma[:, None, :] + beta[:, None, :]
            h_flat = h.reshape(-1, D)
            probs = jax.nn.softmax(h_flat @ router_w, axis=-1)
            gates, idx = jax.lax.top_k(probs, TOPK)
            gates = gates / gates.sum(-1, keepdims=True)
            N = h_flat.shape[0]
            combine = jnp.zeros((N, E), h_flat.dtype).at[jnp.arange(N)[:, None], idx].add(gates)
            hid = jax.nn.relu(jnp.einsum('nd,edf->nef', h_flat, exp_w1) + exp_b1)
            eout = jnp.einsum('nef,efd->ned', hid, exp_w2) + exp_b2
            y = jnp.einsum('ned,ne->nd', eout, combine)
            return x + y.reshape(x.shape)
        return _forward(x, subject_ids, ln_g, ln_b, subj_emb, hyp_w1, hyp_b1, hyp_w2, hyp_b2, sty_w1, sty_b1, sty_w2, sty_b2, router_w, exp_w1, exp_b1, exp_w2, exp_b2)
    x = _L0_cond_ref(x, itok_B_0_15, L0_cond_down_W, L0_cond_down_b, L0_cond_up_W, L0_cond_up_b, L0_cond_expert_W, L0_cond_expert_b, L0_cond_domain_emb, L0_cond_ln_gamma, L0_cond_ln_beta)
    x = _L1_cond_ref(x, itok_B_6_14, L1_cond_ln_g, L1_cond_ln_b, L1_cond_subj_emb, L1_cond_hyp_w1, L1_cond_hyp_b1, L1_cond_hyp_w2, L1_cond_hyp_b2, L1_cond_sty_w1, L1_cond_sty_b1, L1_cond_sty_w2, L1_cond_sty_b2, L1_cond_router_w, L1_cond_exp_w1, L1_cond_exp_b1, L1_cond_exp_w2, L1_cond_exp_b2)
    return x

_drawn_inputs = setup_inputs


def setup_inputs(seed=0):
    import zlib

    import numpy as np

    out = dict(_drawn_inputs(seed))
    spreads = {'L0_cond_ln_gamma': (1.0, 0.2),
     'L0_cond_ln_beta': (0.0, 0.1),
     'L1_cond_ln_g': (1.0, 0.6),
     'L1_cond_ln_b': (0.0, 0.8),
     'L1_cond_hyp_b1': (0.0, 0.1),
     'L1_cond_hyp_b2': (0.0, 0.1),
     'L1_cond_sty_b1': (0.0, 0.1),
     'L1_cond_sty_b2': (0.0, 0.1),
     'L1_cond_exp_b1': (0.0, 0.1),
     'L1_cond_exp_b2': (0.0, 0.1)}
    factors = {'L0_cond_down_b': 3.027}
    for name, (base, spread) in spreads.items():
        noise = np.random.default_rng([zlib.crc32(name.encode()), seed]).standard_normal(out[name].shape)
        drawn = base * np.exp(spread * noise) if base else spread * noise
        out[name] = jnp.asarray(drawn.astype(out[name].dtype))
    for name, factor in factors.items():
        out[name] = (out[name] * factor).astype(out[name].dtype)
    return out
```

```python
from contextlib import ExitStack

import concourse.bass as bass
from concourse import mybir

F32 = mybir.dt.float32
F16 = mybir.dt.float16
I32 = mybir.dt.int32
U32 = mybir.dt.uint32
ALU = mybir.AluOpType
ACT = mybir.ActivationFunctionType
AX = mybir.AxisListType.X

P = 128
ITEMS, T, D = 64, 64, 256
A, ADAPTERS = 64, 16
SUBJECTS, SE, SH = 32, 64, 128
EXPERTS, FF = 8, 1024
TOKENS = ITEMS * T
DC = D // P
FC = FF // P
GROUP = 512
GROUPS = TOKENS // GROUP
GT = GROUP // P
GI = GROUP // T
NT = TOKENS // P
TILES = 2 * TOKENS // P + EXPERTS - 1
NONE_ROW = 32
CHUNK = 1024
CHUNKS = 2 * EXPERTS * DC * FF // CHUNK
W2_AT = EXPERTS * DC * FF
STAGES = 3
WSCALE = 256.0
RING = 8
ZROWS = 8

LN_G, LN_B, HYP_B1, HYP_B2, STY_B2, B1 = 0, DC, 2 * DC, 2 * DC + 1, 2 * DC + 2, 4 * DC + 2
FEATURE_COLS = B1 + EXPERTS * FC


class At:

    def __init__(self, h, c=0):
        self.g = h * 2 + c
        self.par = c % 2
        self.half = h + c // 2


def wait(eng, sem, value):
    if not isinstance(value, int) or value > 0:
        eng.wait_ge(sem, value)


def wait_apart(eng, sem, value, held):
    if not isinstance(value, int):
        eng.wait_ge(held, 1)
    wait(eng, sem, value)


def upto(g, n, most):
    return min(g + n, most) if isinstance(g, int) else g + n


def bcast(ap, axis, shape):
    return ap.unsqueeze(axis).broadcast_to(shape)


def build(nc, x, ids, subject_ids, down_w, down_b, up_w, up_b, adapter_w, adapter_b, domain_emb,
          gamma0, beta0, subj_emb, hyp_w1, hyp_w2, sty_w1, sty_b1, sty_w2, feature, router_w,
          expert_w, exp_b2, out):
    x_rows = x.rearrange("(g t p) d -> g p t d", t=GT, p=P)
    out_rows = out.rearrange("(g t p) d -> g p t d", t=GT, p=P)

    residual = nc.dram_tensor("residual", (TOKENS, D), F32, kind="Internal").ap()
    residual_rows = residual.rearrange("(g t p) d -> g p t d", t=GT, p=P)
    slots_in = nc.dram_tensor("slots_in", (TILES * P, 2 * D), F16, kind="Internal").ap()
    slots_out = nc.dram_tensor("slots_out", (TILES * P, D), F32, kind="Internal").ap()
    slots_clear = slots_in.rearrange("(p r) d -> p (r d)", p=P)

    with ExitStack() as whole:
        def sem(name):
            return whole.enter_context(nc.semaphore(name))

        def keep(name, shape, dt):
            return whole.enter_context(nc.sbuf_tensor(name, shape, dt))

        w_high = keep("w_high", [P, CHUNKS * CHUNK], F16)
        w_low = keep("w_low", [P, CHUNKS * CHUNK], F16)
        feat = keep("feat", [P, FEATURE_COLS], F32)
        ident16 = keep("ident16", [P, P], F16)
        slot_of = keep("slot_of", [P, 2, NT], U32)
        gate = keep("gate", [P, 2, NT], F32)
        tile_expert = keep("tile_expert", [1, TILES], I32)
        banks = whole.enter_context(nc.psum_tensor("banks", [P, 8, 512], F32))

        dense(nc, sem, locals())
        experts(nc, sem, locals())
        combine(nc, sem, locals())


def dense(nc, sem, env):
    (x_rows, ids, subject_ids, down_w, down_b, up_w, up_b, adapter_w, adapter_b, domain_emb, gamma0,
     beta0, subj_emb, hyp_w1, hyp_w2, sty_w1, sty_b1, sty_w2, feature, router_w, expert_w,
     residual_rows, slots_in, slots_clear) = (env[n] for n in (
         "x_rows", "ids", "subject_ids", "down_w", "down_b", "up_w", "up_b", "adapter_w",
         "adapter_b", "domain_emb", "gamma0", "beta0", "subj_emb", "hyp_w1", "hyp_w2", "sty_w1",
         "sty_b1", "sty_w2", "feature", "router_w", "expert_w", "residual_rows", "slots_in",
         "slots_clear"))
    w_high, w_low, feat, ident16, slot_of, gate, tile_expert, banks = (env[n] for n in (
        "w_high", "w_low", "feat", "ident16", "slot_of", "gate", "tile_expert", "banks"))

    with ExitStack() as ctx:
        def sb(name, shape, dt=F32):
            return ctx.enter_context(nc.sbuf_tensor(name, shape, dt))

        ident = sb("ident", [P, P])
        minus_half = sb("minus_half", [P, GI * DC])
        part_no = sb("part_no", [P, 1])
        place_weight = sb("place_weight", [P, EXPERTS])
        tile_start = sb("tile_start", [P, NT])
        tile_no = sb("tile_no", [1, TILES])
        dw = sb("dw", [P, DC, A])
        ab = sb("ab", [A, 2])
        uw = sb("uw", [A + 1, D])
        g0 = sb("g0", [P, D])
        b0 = sb("b0", [P, D])
        rw = sb("rw", [P, DC, EXPERTS])
        item_gamma = sb("item_gamma", [P, DC, ITEMS])
        item_beta = sb("item_beta", [P, DC, ITEMS])
        item_add = sb("item_add", [A, ITEMS])
        lg = sb("lg", [P, NT, EXPERTS])

        h_pair = sb("h_pair", [P, NT, 2, D], F16)
        stage = sb("stage", [P, STAGES, CHUNK])
        xb = sb("xb", [P, 2, GT, D])
        nb = sb("nb", [P, GT, D])
        xT = sb("xT", [P, DC, GROUP])
        hT = sb("hT", [P, DC, GROUP])
        act = sb("act", [A, GROUP])
        dom = sb("dom", [A + 1, GROUP])
        wnow = sb("wnow", [A, GI * A])
        stats0 = sb("stats0", [P, GT, 6])
        mv0 = sb("mv0", [P, GT, 2])
        rs0 = sb("rs0", [P, GT])
        stats1 = sb("stats1", [P, GT, 6])
        mv1 = sb("mv1", [P, GT, 2])
        rs1 = sb("rs1", [P, GT])
        statsT = sb("statsT", [P, DC * GI, 6])
        msum = sb("msum", [P, DC * GI])
        mdiff = sb("mdiff", [P, DC * GI])
        var4 = sb("var4", [P, DC * GI])
        rsT = sb("rsT", [P, DC * GI])
        aff_a = sb("aff_a", [P, DC, GI])
        aff_c = sb("aff_c", [P, DC, GI])

        table = w_low[0:NONE_ROW + 1, 16 * CHUNK:24 * CHUNK].bitcast(F32)
        wsel = w_low[0:A, 24 * CHUNK:32 * CHUNK].bitcast(F32)
        wsel_io = wsel.rearrange("a (i o) -> a i o", o=A)
        scratch = w_high[:, 24 * CHUNK:32 * CHUNK].bitcast(F32)
        at = [0]

        def scr(rows, cols):
            at[0] += cols
            return scratch[0:rows, at[0] - cols:at[0]]

        idf = scr(NONE_ROW + 1, ITEMS)
        sidf = scr(SUBJECTS, ITEMS)
        idc = scr(NONE_ROW + 1, ITEMS)
        hot_w = scr(NONE_ROW + 1, ITEMS)
        hot_e = scr(ADAPTERS, ITEMS)
        hot_s = scr(SUBJECTS, ITEMS)
        t_ab = scr(ADAPTERS, A)
        t_de = scr(ADAPTERS, A)
        t_se = scr(SUBJECTS, SE)
        hw1 = scr(SE, SH)
        hw2 = scr(SH, SH)
        sw1 = scr(SH, SH // 2)
        sw2 = scr(SH // 2, 2 * D)
        se_sb = scr(SE, ITEMS)
        hy1 = scr(SH, ITEMS)
        hy2 = scr(SH, ITEMS)
        st1 = scr(SH // 2, ITEMS)
        style = scr(P, DC * ITEMS)
        absz = scr(P, DC * ITEMS)
        expz = scr(P, DC * ITEMS)
        lnz = scr(P, DC * ITEMS)
        ids_i = scr(NONE_ROW + 1, ITEMS).bitcast(I32)
        sids_i = scr(SUBJECTS, ITEMS).bitcast(I32)
        zero_rows = h_pair[:, 24:32].rearrange("p t k d -> p (t k d)")[:, 0:ZROWS * 2 * D]

        rt = xb[:, :, :, :].rearrange("p a t d -> p (a t d)")
        rt2 = nb[:, :, :].rearrange("p t d -> p (t d)")
        W = NT * EXPERTS

        def grid(k):
            src = rt[:, k * W:(k + 1) * W] if k < 8 else rt2[:, (k - 8) * W:(k - 7) * W]
            return src.rearrange("p (j e) -> p j e", e=EXPERTS)

        def line(k):
            return stage[:, 0, k * NT:(k + 1) * NT]

        earlier = stage[:, 1, 2 * P:3 * P]
        ones = stage[:, 1, 3 * P:4 * P]
        zeros = stage[:, 1, 4 * P:4 * P + W]

        ps_x = banks[:, 0:2, :]
        ps_u = banks[:, 2:4, :].rearrange("p a b -> p (a b)").rearrange("p (t d) -> p t d", d=D)
        ps_h = banks[:, 4:6, :].rearrange("p a b -> p (a b)").rearrange("p (t d) -> p t d", d=D)
        ps_down = banks[0:A, 6, :]
        ps_lg = banks[:, 6, 0:GT * EXPERTS].rearrange("p (t e) -> p t e", e=EXPERTS)
        ps_dom = banks[0:A, 7, :]

        ids_loaded, table_loaded, consts_loaded = sem("ids_loaded"), sem("table_loaded"), sem("consts_loaded")
        table_cleared, pool_consts, cleared_zero = sem("table_cleared"), sem("pool_consts"), sem("cleared_zero")
        slots_cleared = sem("slots_cleared")
        ids_float, hot_ready, select_done, select_copied = (
            sem("ids_float"), sem("hot_ready"), sem("select_done"), sem("select_copied"))
        net_done, net_ready, style_step = sem("net_done"), sem("net_ready"), sem("style_step")
        lnz_ready, dom_row = sem("lnz_ready"), sem("dom_row")
        x_loaded = [sem("x_loaded0"), sem("x_loaded1")]
        res_stored = [sem("res_stored0"), sem("res_stored1")]
        stage_loaded = [sem(f"stage_loaded{s}") for s in range(STAGES)]
        (xT_done, xT_ready, down_done, act_ready, adapt_done, dom_ready, up_done, s_ready, st0_ready,
         mv0_ready, ve0_ready, rs0_ready, n0_ready, n0g_ready, x1_ready, st1_ready, mv1_ready,
         ve1_ready, rs1_ready, n_ready, nT_done, hT_ready) = (sem(n) for n in (
             "xT_done", "xT_ready", "down_done", "act_ready", "adapt_done", "dom_ready", "up_done",
             "s_ready", "st0_ready", "mv0_ready", "ve0_ready", "rs0_ready", "n0_ready", "n0g_ready",
             "x1_ready", "st1_ready", "mv1_ready", "ve1_ready", "rs1_ready", "n_ready", "nT_done",
             "hT_ready"))
        (stT_ready, item_step, var4_ready, rsT_ready, aff_a_ready, aff_c_ready, scaled_ready,
         h_ready, logits_done, logits_copied, back_done, high_ready, low_ready) = (sem(n) for n in (
             "stT_ready", "item_step", "var4_ready", "rsT_ready", "aff_a_ready", "aff_c_ready",
             "scaled_ready", "h_ready", "logits_done", "logits_copied", "back_done", "high_ready",
             "low_ready"))
        wnow_ready, route_consts = sem("wnow_ready"), sem("route_consts")
        w_high_ready, w_low_ready = sem("w_high_ready"), sem("w_low_ready")
        route_step, exp_in, exp_out, mask_ready, rank_done = (
            sem("route_step"), sem("exp_in"), sem("exp_out"), sem("mask_ready"), sem("rank_done"))
        slots_known, scattered = sem("slots_known"), sem("scattered")
        N_CONSTS = 16

        def iterations(eng, body, looped=GROUPS // 2):
            body(At(0, 0))
            body(At(0, 1))
            with eng.Fori(1, looped) as h:
                body(At(h, 0))
                body(At(h, 1))
            for i in range(2 * looped, GROUPS + 2):
                body(At(i // 2, i % 2))

        def back(i, n):
            if isinstance(i.g, int):
                g = i.g - n
                return At(g // 2, g % 2) if 0 <= g < GROUPS else None
            return At(i.half, i.par - n)

        def chunks(i):
            if isinstance(i.g, int) and i.g >= GROUPS:
                first = STAGES * GROUPS + (i.g - GROUPS) * 4
                return [(q, q % STAGES, q // STAGES) for q in range(first, first + 4)]
            return [(i.g * STAGES + s, s, i.g) for s in range(STAGES)]

        with nc.Block() as block:

            @block.sync
            def _(sp):
                def load_x(i):
                    sp.dma_start(xb[:, i.par], x_rows[i.g] if isinstance(i.g, int)
                                 else x_rows[bass.ds(i.g, 1)].rearrange("o p t d -> (o p) t d")
                                 ).then_inc(x_loaded[i.par], 16)

                def load_weights(i):
                    for q, slot, turn in chunks(i):
                        wait(sp, w_low_ready, q - STAGES + 1)
                        src = expert_w[q] if isinstance(q, int) else expert_w[bass.ds(q, 1)].rearrange("o p c -> (o p) c")
                        sp.dma_start(stage[:, slot], src).then_inc(stage_loaded[slot], 16)

                sp.dma_start(ids_i, ids.partition_broadcast(NONE_ROW + 1).rearrange("q o n -> q (o n)")).then_inc(ids_loaded, 16)
                sp.dma_start(sids_i, subject_ids.partition_broadcast(SUBJECTS).rearrange("q o n -> q (o n)")).then_inc(ids_loaded, 16)
                load_x(At(0, 0))
                load_x(At(0, 1))
                for dst, src in ((dw[:], down_w), (ab[:, 0:1], down_b), (ab[:, 1:2], sty_b1),
                                 (uw[0:A], up_w), (uw[A:A + 1], up_b), (feat[:], feature),
                                 (t_ab, adapter_b), (t_de, domain_emb), (t_se, subj_emb),
                                 (hw1, hyp_w1), (hw2, hyp_w2), (sw1, sty_w1), (sw2, sty_w2),
                                 (rw[:], router_w),
                                 (g0[:], gamma0.partition_broadcast(P).rearrange("q o n -> q (o n)")),
                                 (b0[:], beta0.partition_broadcast(P).rearrange("q o n -> q (o n)"))):
                    sp.dma_start(dst, src).then_inc(consts_loaded, 16)
                sp.wait_ge(table_cleared, 2)
                sp.dma_start(table[0:ADAPTERS], adapter_w).then_inc(table_loaded, 16)
                sp.wait_ge(cleared_zero, 1)
                for r in range(0, TILES, ZROWS):
                    n = min(ZROWS, TILES - r)
                    sp.dma_start(slots_clear[:, r * 2 * D:(r + n) * 2 * D],
                                 zero_rows[:, 0:n * 2 * D]).then_inc(slots_cleared, 16)

                def body(i):
                    load_weights(i)
                    if (s2 := back(i, 1)) is not None:
                        sp.wait_ge(x1_ready, s2.g + 1)
                        sp.dma_start(residual_rows[s2.g] if isinstance(s2.g, int)
                                     else residual_rows[bass.ds(s2.g, 1)].rearrange("o p t d -> (o p) t d"),
                                     xb[:, s2.par]).then_inc(res_stored[s2.par], 16)
                        if not isinstance(i.g, int) or i.g + 1 < GROUPS:
                            wait_apart(sp, n_ready, s2.g + 1, ids_loaded)
                            sp.wait_ge(res_stored[s2.par], (s2.half + 1) * 16)
                            load_x(At(s2.half + 1, s2.par))

                iterations(sp, body, GROUPS // 2 - 1)
                for par in range(2):
                    sp.wait_ge(res_stored[par], GROUPS // 2 * 16)

            @block.gpsimd
            def _(pool):
                nc.gpsimd.memset(table[:], 0.0).then_inc(table_cleared, 1)
                pool.wait_ge(table_cleared, 1)
                row = table[NONE_ROW:NONE_ROW + 1].rearrange("r (o a) -> r o a", a=A)
                nc.gpsimd.affine_select(out=row, in_=row, compare_op=ALU.not_equal, fill=1.0, base=0,
                                        pattern=[[1, A], [-1, A]], channel_multiplier=0).then_inc(table_cleared, 1)
                pool.wait_ge(table_cleared, 2)
                nc.gpsimd.iota(part_no[:], [[0, 1]], base=0, channel_multiplier=1,
                               allow_small_or_imprecise_dtypes=True).then_inc(pool_consts, 1)
                nc.gpsimd.memset(ident[:], 0.0).then_inc(pool_consts, 1)
                pool.wait_ge(pool_consts, 2)
                nc.gpsimd.affine_select(out=ident[:], in_=ident[:], compare_op=ALU.not_equal, fill=1.0, base=0,
                                        pattern=[[-1, P]], channel_multiplier=1).then_inc(pool_consts, 1)
                nc.gpsimd.memset(minus_half[:], -0.5).then_inc(pool_consts, 1)
                nc.gpsimd.memset(zero_rows, 0.0).then_inc(cleared_zero, 1)
                pool.wait_ge(pool_consts, 3)
                nc.gpsimd.tensor_copy(ident16[:], ident[:]).then_inc(pool_consts, 1)
                for dst, pattern, base in ((place_weight[:], [[-1, EXPERTS]], EXPERTS),
                                           (tile_start[:], [[P, NT]], 0), (tile_no[:], [[1, TILES]], 0)):
                    nc.gpsimd.iota(dst, pattern, base=base, channel_multiplier=0,
                                   allow_small_or_imprecise_dtypes=True).then_inc(pool_consts, 1)

                def rstd(g, mv, mv_sem, rs, ve_sem, rs_sem):
                    wait_apart(pool, mv_sem, g + 1, select_copied)
                    nc.gpsimd.tensor_scalar(rs[:], mv[:, :, 1], 1e-5, None, ALU.add).then_inc(ve_sem, 1)
                    pool.wait_ge(ve_sem, g + 1)
                    nc.gpsimd.tensor_tensor(rs[:], rs[:], minus_half[:, 0:GT], ALU.pow).then_inc(rs_sem, 1)

                def body(i):
                    s1, s2, s3 = back(i, 0), back(i, 1), back(i, 2)
                    if s1 is not None:
                        wait(pool, adapt_done, s1.g)
                        nc.gpsimd.tensor_copy(wnow[:], wsel[:, bass.ds(s1.g * GI * A, GI * A)]).then_inc(wnow_ready, 1)
                    if s2 is not None:
                        rstd(s2.g, mv0, mv0_ready, rs0, ve0_ready, rs0_ready)
                    if s3 is not None:
                        pool.wait_ge(var4_ready, s3.g + 1)
                        nc.gpsimd.tensor_tensor(rsT[:], var4[:], minus_half[:], ALU.pow).then_inc(rsT_ready, 1)
                    if s2 is not None:
                        pool.wait_ge(n0g_ready, s2.g + 1)
                        nc.gpsimd.tensor_tensor(xb[:, s2.par], xb[:, s2.par], bcast(b0[:], 1, [P, GT, D]),
                                                ALU.add).then_inc(x1_ready, 1)
                        rstd(s2.g, mv1, mv1_ready, rs1, ve1_ready, rs1_ready)

                pool.wait_ge(select_copied, A // 8)
                iterations(pool, body)
                pool.wait_ge(w_low_ready, CHUNKS)
                nc.gpsimd.memset(earlier, 0.0).then_inc(route_consts, 1)
                nc.gpsimd.memset(ones, 1.0).then_inc(route_consts, 1)
                nc.gpsimd.memset(zeros, 0.0).then_inc(route_consts, 1)
                pool.wait_ge(route_consts, 1)
                nc.gpsimd.affine_select(out=earlier, in_=earlier, compare_op=ALU.is_ge, fill=1.0, base=0,
                                        pattern=[[-1, P]], channel_multiplier=1).then_inc(route_consts, 1)
                pool.wait_ge(slots_known, 1)
                pool.wait_ge(high_ready, GROUPS)
                pool.wait_ge(low_ready, GROUPS)
                pool.wait_ge(slots_cleared, 16 * -(-TILES // ZROWS))
                for j in range(NT):
                    for k in range(2):
                        nc.gpsimd.indirect_dma_start(
                            out=slots_in, out_offset=bass.IndirectOffsetOnAxis(ap=slot_of[:, k, j:j + 1], axis=0),
                            in_=h_pair[:, j].rearrange("p k d -> p (k d)"), in_offset=None).then_inc(scattered, 16)
                pool.wait_ge(scattered, 16 * 2 * NT)

            @block.tensor
            def _(pe):
                def setup():
                    pe.wait_ge(consts_loaded, 16 * N_CONSTS)
                    pe.wait_ge(hot_ready, 3)
                    nc.tensor.matmul(banks[0:A, 6, 0:ITEMS], t_ab, hot_w[0:ADAPTERS], start=True, stop=False)
                    nc.tensor.matmul(banks[0:A, 6, 0:ITEMS], t_de, hot_e, start=False, stop=True)
                    nc.tensor.matmul(banks[0:SE, 7, 0:ITEMS], t_se, hot_s, start=True, stop=True).then_inc(net_done, 1)
                    pe.wait_ge(table_loaded, 16)
                    for b in range(A // 8):
                        wait(pe, select_copied, b - 1)
                        for k in range(8):
                            o = b * 8 + k
                            last = nc.tensor.matmul(banks[0:A, b % 2, k * ITEMS:(k + 1) * ITEMS],
                                                    table[:, o * A:(o + 1) * A], hot_w, start=True, stop=True)
                        last.then_inc(select_done, 1)
                    for w, src, bank, n, k in ((hw1, se_sb, 6, SH, 1), (hw2, hy1, 7, SH, 2), (sw1, hy2, 6, SH // 2, 3)):
                        pe.wait_ge(net_ready, k + 1)
                        nc.tensor.matmul(banks[0:n, bank, 0:ITEMS], w, src, start=True, stop=True).then_inc(net_done, 1)
                    pe.wait_ge(net_ready, 5)
                    for c in range(2 * DC):
                        last = nc.tensor.matmul(banks[:, 7, c * ITEMS:(c + 1) * ITEMS], sw2[:, c * P:(c + 1) * P],
                                                st1, start=True, stop=True)
                    last.then_inc(net_done, 1)

                def into_features(i):
                    pe.wait_ge(x_loaded[i.par], (i.half + 1) * 16)
                    wait(pe, hT_ready, i.g - 1)
                    for c in range(DC):
                        for t in range(GT):
                            last = nc.tensor.transpose(ps_x[:, c, t * P:(t + 1) * P],
                                                       xb[:, i.par, t, c * P:(c + 1) * P], ident[:])
                    last.then_inc(xT_done, 1)

                def adapter(i):
                    pe.wait_ge(xT_ready, i.g + 1)
                    wait(pe, logits_copied, i.g - 2)
                    for c in range(DC):
                        last = nc.tensor.matmul(ps_down, dw[:, c, :], xT[:, c, :], start=(c == 0), stop=(c == DC - 1))
                    last.then_inc(down_done, 1)
                    wait_apart(pe, wnow_ready, i.g + 1, dom_row)
                    pe.wait_ge(act_ready, i.g + 1)
                    wait(pe, dom_ready, i.g)
                    for b in range(GI):
                        last = nc.tensor.matmul(ps_dom[:, b * T:(b + 1) * T], wnow[:, b * A:(b + 1) * A],
                                                act[:, b * T:(b + 1) * T], start=True, stop=True)
                    last.then_inc(adapt_done, 1)
                    pe.wait_ge(dom_ready, i.g + 1)
                    wait(pe, s_ready, i.g)
                    for t in range(GT):
                        last = nc.tensor.matmul(ps_u[:, t, :], dom[:, t * P:(t + 1) * P], uw[:], start=True, stop=True)
                    last.then_inc(up_done, 1)

                def route_and_back(i):
                    pe.wait_ge(h_ready, i.g + 1)
                    pe.wait_ge(act_ready, upto(i.g, 3, GROUPS))
                    for t in range(GT):
                        for c in range(DC):
                            last = nc.tensor.matmul(ps_lg[:, t, :], hT[:, c, t * P:(t + 1) * P], rw[:, c, :],
                                                    start=(c == 0), stop=(c == DC - 1))
                    last.then_inc(logits_done, 1)
                    wait(pe, low_ready, i.g)
                    for t in range(GT):
                        for c in range(DC):
                            last = nc.tensor.transpose(ps_h[:, t, c * P:(c + 1) * P], hT[:, c, t * P:(t + 1) * P], ident[:])
                    last.then_inc(back_done, 1)

                def normed_into_features(i):
                    pe.wait_ge(n_ready, i.g + 1)
                    pe.wait_ge(xT_ready, upto(i.g, 2, GROUPS))
                    for c in range(DC):
                        for t in range(GT):
                            last = nc.tensor.transpose(ps_x[:, c, t * P:(t + 1) * P], nb[:, t, c * P:(c + 1) * P], ident[:])
                    last.then_inc(nT_done, 1)

                pe.wait_ge(pool_consts, 8)
                setup()
                pe.wait_ge(net_ready, 6)
                pe.wait_ge(select_copied, A // 8)
                pe.wait_ge(dom_row, 1)

                def body(i):
                    if (s1 := back(i, 0)) is not None:
                        into_features(s1)
                        adapter(s1)
                    if (s3 := back(i, 2)) is not None:
                        route_and_back(s3)
                    if (s2 := back(i, 1)) is not None:
                        normed_into_features(s2)

                iterations(pe, body)
                pe.wait_ge(mask_ready, 1)
                pe.wait_ge(route_consts, 4)
                mask = grid(0).rearrange("p j e -> p (j e)")
                nc.tensor.matmul(banks[:, 0, 0:W], earlier, mask, start=True, stop=True)
                nc.tensor.matmul(banks[:, 1, 0:W], ones, mask, start=True, stop=True).then_inc(rank_done, 1)

            @block.scalar
            def _(sc):
                sc.wait_ge(net_ready, 6)
                nc.scalar.activation(absz, style, ACT.Abs).then_inc(style_step, 1)
                sc.wait_ge(style_step, 1)
                nc.scalar.activation(expz, absz, ACT.Exp, scale=-1.0).then_inc(style_step, 1)
                sc.wait_ge(style_step, 2)
                nc.scalar.activation(lnz, expz, ACT.Ln, bias=1.0).then_inc(lnz_ready, 1)

                def cut_high(i):
                    for q, slot, turn in chunks(i):
                        sc.wait_ge(stage_loaded[slot], (turn + 1) * 16)
                        nc.scalar.activation(w_high[:, bass.ds(q * CHUNK, CHUNK)], stage[:, slot], ACT.Copy,
                                             scale=WSCALE).then_inc(w_high_ready, 1)

                def body(i):
                    s1, s2, s3 = back(i, 0), back(i, 1), back(i, 2)
                    if s1 is not None:
                        sc.wait_ge(xT_done, s1.g + 1)
                        wait(sc, down_done, s1.g)
                        nc.scalar.activation(xT[:], ps_x[:], ACT.Copy).then_inc(xT_ready, 1)
                        sc.wait_ge(down_done, s1.g + 1)
                        wait(sc, adapt_done, s1.g)
                        if isinstance(s1.g, int) and s1.g == 0:
                            sc.wait_ge(consts_loaded, 16 * N_CONSTS)
                        nc.scalar.activation(act[:], ps_down, ACT.Gelu, bias=ab[:, 0:1]).then_inc(act_ready, 1)
                    cut_high(i)
                    if s3 is not None:
                        sc.wait_ge(logits_done, s3.g + 1)
                        nc.scalar.activation(lg[:, bass.ds(s3.g * GT, GT), :], ps_lg, ACT.Copy).then_inc(logits_copied, 1)
                        sc.wait_ge(back_done, s3.g + 1)
                        if isinstance(s3.g, int) and s3.g == 6:
                            sc.wait_ge(slots_cleared, 16 * -(-TILES // ZROWS))
                        nc.scalar.activation(h_pair[:, bass.ds(s3.g * GT, GT), 0, :], ps_h, ACT.Copy).then_inc(high_ready, 1)
                    if s2 is not None:
                        sc.wait_ge(nT_done, s2.g + 1)
                        wait(sc, back_done, s2.g)
                        for c in range(DC):
                            last = nc.scalar.activation(hT[:, c, :], ps_x[:, c, :], ACT.Identity,
                                                        scale=feat[:, LN_G + c:LN_G + c + 1],
                                                        bias=feat[:, LN_B + c:LN_B + c + 1])
                        last.then_inc(hT_ready, 1)

                iterations(sc, body)
                sc.wait_ge(exp_in, 1)
                nc.scalar.activation(grid(1), grid(1), ACT.Exp).then_inc(exp_out, 1)

            @block.vector
            def _(dve):
                V = nc.vector
                step = [0]

                def link(ins):
                    step[0] += 1
                    ins.then_inc(route_step, 1)
                    dve.wait_ge(route_step, step[0])

                V.memset(dom[A:A + 1, :], 1.0).then_inc(dom_row, 1)
                dve.wait_ge(ids_loaded, 32)
                dve.wait_ge(pool_consts, 1)
                link(V.tensor_copy(idf, ids_i))
                link(V.tensor_copy(sidf, sids_i))
                link(V.tensor_scalar(idc, idf, 0.0, float(ADAPTERS - 1), ALU.max, ALU.min))
                link(V.tensor_scalar(hot_w, idf, part_no[0:NONE_ROW + 1, 0:1], None, ALU.is_equal))
                V.tensor_tensor(hot_w[NONE_ROW:NONE_ROW + 1], idf[NONE_ROW:NONE_ROW + 1],
                                idc[NONE_ROW:NONE_ROW + 1], ALU.not_equal).then_inc(hot_ready, 1)
                V.tensor_scalar(hot_e, idc[0:ADAPTERS], part_no[0:ADAPTERS, 0:1], None, ALU.is_equal).then_inc(hot_ready, 1)
                link(V.tensor_scalar(sidf, sidf, 0.0, float(SUBJECTS - 1), ALU.max, ALU.min))
                V.tensor_scalar(hot_s, sidf, part_no[0:SUBJECTS, 0:1], None, ALU.is_equal).then_inc(hot_ready, 1)
                dve.wait_ge(consts_loaded, 16 * N_CONSTS)
                dve.wait_ge(net_done, 1)
                V.tensor_copy(item_add[:], banks[0:A, 6, 0:ITEMS]).then_inc(net_ready, 1)
                V.tensor_copy(se_sb, banks[0:SE, 7, 0:ITEMS]).then_inc(net_ready, 1)
                for b in range(A // 8):
                    dve.wait_ge(select_done, b + 1)
                    V.tensor_copy(wsel_io[:, :, b * 8:(b + 1) * 8].rearrange("a i o -> a o i"),
                                  banks[0:A, b % 2, :].rearrange("a (o i) -> a o i", i=ITEMS)).then_inc(select_copied, 1)
                dve.wait_ge(net_done, 2)
                V.tensor_scalar(hy1, banks[0:SH, 6, 0:ITEMS], feat[:, HYP_B1:HYP_B1 + 1], 0.0, ALU.add, ALU.max).then_inc(net_ready, 1)
                dve.wait_ge(net_done, 3)
                V.tensor_scalar(hy2, banks[0:SH, 7, 0:ITEMS], feat[:, HYP_B2:HYP_B2 + 1], None, ALU.add).then_inc(net_ready, 1)
                dve.wait_ge(net_done, 4)
                V.tensor_scalar(st1, banks[0:SH // 2, 6, 0:ITEMS], ab[:, 1:2], 0.0, ALU.add, ALU.max).then_inc(net_ready, 1)
                dve.wait_ge(net_done, 5)
                for c in range(DC):
                    V.tensor_scalar(style[:, c * ITEMS:(c + 1) * ITEMS], banks[:, 7, c * ITEMS:(c + 1) * ITEMS],
                                    feat[:, STY_B2 + c:STY_B2 + c + 1], None, ALU.add)
                for c in range(DC):
                    last = V.tensor_scalar(item_beta[:, c, :], banks[:, 7, (DC + c) * ITEMS:(DC + c + 1) * ITEMS],
                                           feat[:, STY_B2 + DC + c:STY_B2 + DC + c + 1], None, ALU.add)
                last.then_inc(net_ready, 1)
                dve.wait_ge(lnz_ready, 1)
                gam = item_gamma[:].rearrange("p c i -> p (c i)")
                link(V.scalar_tensor_tensor(gam, style, 0.0, lnz, ALU.max, ALU.add))
                link(V.tensor_scalar(gam, gam, 1e-8, None, ALU.add))

                def bn(src, stats, st_sem, mv, mv_sem, g):
                    wait(dve, rs0_ready if mv is mv0 else rs1_ready, g)
                    for t in range(GT):
                        last = V.bn_stats(stats[:, t, :], src[:, t, :])
                    last.then_inc(st_sem, 1)
                    wait_apart(dve, st_sem, g + 1, pool_consts)
                    for t in range(GT):
                        last = V.bn_aggr(mv[:, t, :], stats[:, t, :])
                    last.then_inc(mv_sem, 1)

                def item_norm_moments(i):
                    dve.wait_ge(hT_ready, i.g + 1)
                    for c in range(DC):
                        for b in range(GI):
                            last = V.bn_stats(statsT[:, c * GI + b, :], hT[:, c, b * T:(b + 1) * T])
                    last.then_inc(stT_ready, 1)
                    dve.wait_ge(stT_ready, i.g + 1)
                    V.tensor_tensor(msum[:], statsT[:, :, 1], statsT[:, :, 4], ALU.add)
                    V.tensor_tensor(mdiff[:], statsT[:, :, 1], statsT[:, :, 4], ALU.subtract)
                    V.tensor_tensor(var4[:], statsT[:, :, 2], statsT[:, :, 5], ALU.add).then_inc(item_step, 1)
                    dve.wait_ge(item_step, i.g * 3 + 1)
                    V.tensor_tensor(mdiff[:], mdiff[:], mdiff[:], ALU.mult).then_inc(item_step, 1)
                    dve.wait_ge(item_step, i.g * 3 + 2)
                    V.scalar_tensor_tensor(var4[:], var4[:], 4.0 / T, mdiff[:], ALU.mult, ALU.add).then_inc(item_step, 1)
                    dve.wait_ge(item_step, i.g * 3 + 3)
                    V.tensor_scalar(var4[:], var4[:], 0.25, 1e-8, ALU.mult, ALU.add).then_inc(var4_ready, 1)

                def item_norm_apply(i):
                    dve.wait_ge(rsT_ready, i.g + 1)
                    items = bass.ds(i.g * GI, GI)
                    flat_a = aff_a[:].rearrange("p c b -> p (c b)")
                    flat_c = aff_c[:].rearrange("p c b -> p (c b)")
                    V.tensor_tensor(aff_a[:], rsT[:].rearrange("p (c b) -> p c b", b=GI), item_gamma[:, :, items],
                                    ALU.mult).then_inc(aff_a_ready, 1)
                    dve.wait_ge(aff_a_ready, i.g + 1)
                    V.scalar_tensor_tensor(flat_c, msum[:], 0.5, flat_a, ALU.mult, ALU.mult).then_inc(aff_c_ready, 1)
                    dve.wait_ge(aff_c_ready, i.g * 2 + 1)
                    V.tensor_tensor(aff_c[:], item_beta[:, :, items], aff_c[:], ALU.subtract).then_inc(aff_c_ready, 1)
                    for c in range(DC):
                        v = hT[:, c, :].rearrange("p (b t) -> p b t", t=T)
                        last = V.tensor_tensor(v, v, bcast(aff_a[:, c, :], 2, [P, GI, T]), ALU.mult)
                    last.then_inc(scaled_ready, 1)
                    dve.wait_ge(scaled_ready, i.g + 1)
                    dve.wait_ge(aff_c_ready, i.g * 2 + 2)
                    for c in range(DC):
                        v = hT[:, c, :].rearrange("p (b t) -> p b t", t=T)
                        last = V.tensor_tensor(v, v, bcast(aff_c[:, c, :], 2, [P, GI, T]), ALU.add)
                    last.then_inc(h_ready, 1)

                def body(i):
                    s1, s2, s3 = back(i, 0), back(i, 1), back(i, 2)
                    if s2 is not None:
                        dve.wait_ge(up_done, s2.g + 1)
                        V.tensor_tensor(xb[:, s2.par], ps_u, xb[:, s2.par], ALU.add).then_inc(s_ready, 1)
                        dve.wait_ge(s_ready, s2.g + 1)
                        bn(xb[:, s2.par], stats0, st0_ready, mv0, mv0_ready, s2.g)
                    if s3 is not None:
                        item_norm_moments(s3)
                    if s1 is not None:
                        dve.wait_ge(adapt_done, s1.g + 1)
                        wait(dve, up_done, s1.g)
                        V.tensor_tensor(dom[0:A, :].rearrange("a (b t) -> a b t", t=T),
                                        ps_dom.rearrange("a (b t) -> a b t", t=T),
                                        bcast(item_add[:, bass.ds(s1.g * GI, GI)], 2, [A, GI, T]),
                                        ALU.add).then_inc(dom_ready, 1)
                    if s2 is not None:
                        dve.wait_ge(rs0_ready, s2.g + 1)
                        for t in range(GT):
                            last = V.tensor_scalar(xb[:, s2.par, t, :], xb[:, s2.par, t, :], mv0[:, t, 0:1],
                                                   rs0[:, t:t + 1], ALU.subtract, ALU.mult)
                        last.then_inc(n0_ready, 1)
                        dve.wait_ge(n0_ready, s2.g + 1)
                        V.tensor_tensor(xb[:, s2.par], xb[:, s2.par], bcast(g0[:], 1, [P, GT, D]),
                                        ALU.mult).then_inc(n0g_ready, 1)
                    if s3 is not None:
                        item_norm_apply(s3)
                    if s2 is not None:
                        dve.wait_ge(x1_ready, s2.g + 1)
                        bn(xb[:, s2.par], stats1, st1_ready, mv1, mv1_ready, s2.g)
                    for q, slot, turn in chunks(i):
                        dve.wait_ge(w_high_ready, q + 1)
                        w = bass.ds(q * CHUNK, CHUNK)
                        V.scalar_tensor_tensor(w_low[:, w], stage[:, slot], WSCALE, w_high[:, w], ALU.mult,
                                               ALU.subtract).then_inc(w_low_ready, 1)
                    if s2 is not None:
                        dve.wait_ge(rs1_ready, s2.g + 1)
                        wait(dve, nT_done, s2.g)
                        for t in range(GT):
                            last = V.tensor_scalar(nb[:, t, :], xb[:, s2.par, t, :], mv1[:, t, 0:1],
                                                   rs1[:, t:t + 1], ALU.subtract, ALU.mult)
                        last.then_inc(n_ready, 1)
                    if s3 is not None:
                        dve.wait_ge(high_ready, s3.g + 1)
                        tiles = bass.ds(s3.g * GT, GT)
                        V.tensor_tensor(h_pair[:, tiles, 1, :], ps_h, h_pair[:, tiles, 0, :],
                                        ALU.subtract).then_inc(low_ready, 1)

                iterations(dve, body)

                G = [P, NT, EXPERTS]
                per_place = bcast(place_weight[:], 1, G)
                dve.wait_ge(logits_copied, GROUPS)
                dve.wait_ge(nT_done, GROUPS)
                dve.wait_ge(pool_consts, 8)
                dve.wait_ge(route_consts, 4)
                for par in range(2):
                    dve.wait_ge(res_stored[par], GROUPS // 2 * 16)
                link(V.tensor_reduce(line(0), lg[:], AX, ALU.max))
                V.tensor_tensor(grid(1), lg[:], bcast(line(0), 2, G), ALU.subtract).then_inc(exp_in, 1)
                dve.wait_ge(exp_out, 1)
                link(V.tensor_reduce(line(1), grid(1), AX, ALU.add))
                link(V.reciprocal(line(1), line(1)))
                link(V.tensor_tensor(grid(1), grid(1), bcast(line(1), 2, G), ALU.mult))

                def pick(best, mask):
                    link(V.tensor_reduce(best, grid(1), AX, ALU.max))
                    link(V.tensor_tensor(mask, grid(1), bcast(best, 2, G), ALU.is_equal))
                    link(V.tensor_tensor(mask, mask, per_place, ALU.mult))
                    link(V.tensor_reduce(line(2), mask, AX, ALU.max))
                    link(V.tensor_tensor(mask, per_place, bcast(line(2), 2, G), ALU.is_equal))

                pick(line(3), grid(2))
                link(V.scalar_tensor_tensor(grid(1), grid(2), -2.0, grid(1), ALU.mult, ALU.add))
                pick(line(4), grid(3))
                V.tensor_tensor(grid(0), grid(2), grid(3), ALU.add).then_inc(mask_ready, 1)
                link(V.tensor_tensor(line(5), line(3), line(4), ALU.add))
                link(V.reciprocal(line(5), line(5)))
                V.tensor_tensor(gate[:, 0, :], line(3), line(5), ALU.mult)
                V.tensor_tensor(gate[:, 1, :], line(4), line(5), ALU.mult)
                dve.wait_ge(rank_done, 1)
                by_expert = grid(4).rearrange("p j e -> p (j e)").rearrange("p (e j) -> p e j", j=NT)
                total = grid(5).rearrange("p j e -> p (j e)").rearrange("p (e j) -> p e j", j=NT)
                flat = lambda k: grid(k).rearrange("p j e -> p (j e)")
                link(V.tensor_copy(by_expert, banks[:, 1, 0:W].rearrange("p (j e) -> p e j", e=EXPERTS)))
                link(V.tensor_tensor_scan(flat(5), flat(4), zeros[:, 0:W], 0.0, ALU.add, ALU.add))
                before = grid(6).rearrange("p j e -> p (j e)").rearrange("p (e j) -> p e j", j=NT)
                link(V.tensor_tensor(before, total, by_expert, ALU.subtract))
                first = before[:, :, 0]
                count, ntiles, tile_end, tile_first, shift = (
                    stage[:, 1, 8 * k:8 * k + 8] for k in range(5))
                link(V.tensor_tensor(count, total[:, :, NT - 1], first, ALU.subtract))
                over = grid(7).rearrange("p j e -> p (j e)").rearrange("p (e j) -> p e j", j=NT)
                link(V.tensor_tensor(over, bcast(count, 2, [P, EXPERTS, NT]),
                                     bcast(tile_start[:], 1, [P, EXPERTS, NT]), ALU.is_gt))
                link(V.tensor_reduce(ntiles, over, AX, ALU.add))
                link(V.tensor_tensor_scan(tile_end, ntiles, zeros[:, 0:EXPERTS], 0.0, ALU.add, ALU.add))
                link(V.tensor_tensor(tile_first, tile_end, ntiles, ALU.subtract))
                link(V.scalar_tensor_tensor(shift, tile_first, float(P), first, ALU.mult, ALU.subtract))
                link(V.tensor_tensor(before, before, bcast(shift, 2, [P, EXPERTS, NT]), ALU.add))
                link(V.tensor_tensor(grid(8), banks[:, 0, 0:W].rearrange("p (j e) -> p j e", e=EXPERTS),
                                     before.rearrange("p e j -> p j e"), ALU.add))
                for k in range(2):
                    link(V.tensor_tensor(grid(2 + k), grid(2 + k), grid(8), ALU.mult))
                    link(V.tensor_reduce(line(6 + k), grid(2 + k), AX, ALU.add))
                    last = V.tensor_copy(slot_of[:, k, :], line(6 + k))
                last.then_inc(slots_known, 1)
                te = rt[0:1, 4 * W:4 * W + TILES * EXPERTS].rearrange("p (i e) -> p i e", e=EXPERTS)
                tf = stage[0:1, 2, 0:TILES]
                link(V.tensor_tensor(te, bcast(tile_no[:], 2, [1, TILES, EXPERTS]),
                                     bcast(tile_first[0:1], 1, [1, TILES, EXPERTS]), ALU.is_ge))
                link(V.tensor_reduce(tf, te, AX, ALU.add))
                link(V.tensor_scalar(tile_expert[:], tf, -1.0, None, ALU.add))


def experts(nc, sem, env):
    slots_in, slots_out, exp_b2 = env["slots_in"], env["slots_out"], env["exp_b2"]
    w_high, w_low, feat, ident16, tile_expert, banks = (
        env[n] for n in ("w_high", "w_low", "feat", "ident16", "tile_expert", "banks"))

    with ExitStack() as ctx:
        def sb(name, shape, dt=F32):
            return ctx.enter_context(nc.sbuf_tensor(name, shape, dt))

        b2 = sb("b2", [P, EXPERTS * D])
        rows = sb("rows", [P, 2, 2, D], F16)
        rT = sb("rT", [P, 2, 2, DC, P], F16)
        hid = sb("hid", [P, 2, FC, P])
        hid_high = sb("hid_high", [P, 2, FC, P], F16)
        hid_low = sb("hid_low", [P, 2, FC, P], F16)
        yb = sb("yb", [P, 2, D])

        b2_loaded = sem("b2_loaded")
        rows_loaded = [sem("rows_loaded0"), sem("rows_loaded1")]
        y_stored = [sem("y_stored0"), sem("y_stored1")]
        rT_done, rT_ready, in_done, hid_ready, split_high, split_low, out_done, y_ready = (
            sem(n) for n in ("rT_done", "rT_ready", "in_done", "hid_ready", "split_high", "split_low",
                             "out_done", "y_ready"))

        HB = FC // 2

        def ps_in(par, c):
            return banks[:, 2 * par + c // HB, (c % HB) * P:(c % HB + 1) * P]

        def ps_rT(par):
            return banks[:, 4 + par, 0:2 * DC * P // 2].bitcast(F16)

        def ps_out(par):
            return banks[:, 6 + par, 0:D]

        def rows_of(dram, i):
            if isinstance(i.g, int):
                return dram[i.g * P:(i.g + 1) * P, :]
            return dram[bass.ds(i.g * P, P), :]

        def expert_of(eng, i):
            return eng.value_load(tile_expert[0:1, bass.ds(i.g, 1)], min_val=0, max_val=EXPERTS - 1)

        with nc.Block() as block:

            @block.sync
            def _(sp):
                sp.dma_start(b2[:], exp_b2.partition_broadcast(P).rearrange("q o n -> q (o n)")).then_inc(b2_loaded, 16)

                def load(i):
                    wait(sp, rT_done, i.g - 1)
                    sp.dma_start(rows[:, i.par].rearrange("p k d -> p (k d)"),
                                 rows_of(slots_in, i)).then_inc(rows_loaded[i.par], 16)

                def store(i):
                    sp.wait_ge(y_ready, i.g + 1)
                    sp.dma_start(rows_of(slots_out, i), yb[:, i.par]).then_inc(y_stored[i.par], 16)

                load(At(0, 0))
                load(At(0, 1))
                load(At(1, 0))
                store(At(0, 0))
                with sp.Fori(1, TILES // 2) as h:
                    load(At(h, 1))
                    store(At(h, -1))
                    load(At(h, 2))
                    store(At(h, 0))
                store(At(TILES // 2, -1))
                store(At(TILES // 2, 0))
                sp.wait_ge(y_stored[0], (TILES + 1) // 2 * 16)
                sp.wait_ge(y_stored[1], TILES // 2 * 16)

            @block.tensor
            def _(pe):
                def transpose_rows(i):
                    pe.wait_ge(rows_loaded[i.par], (i.half + 1) * 16)
                    wait(pe, rT_ready, i.g - 1)
                    for k in range(2):
                        for c in range(DC):
                            n = k * DC + c
                            last = nc.tensor.transpose(ps_rT(i.par)[:, n * P:(n + 1) * P],
                                                       rows[:, i.par, k, c * P:(c + 1) * P], ident16[:])
                    last.then_inc(rT_done, 1)

                def layer_in(i):
                    e = expert_of(pe, i)
                    pe.wait_ge(rT_ready, i.g + 1)
                    for c in range(FC):
                        if c % HB == 0:
                            wait(pe, hid_ready, (i.g - 2) * 2 + c // HB + 1)
                        n = 0
                        for k in range(DC):
                            at = bass.ds(e * (DC * FF) + (k * FF + c * P), P)
                            for w, v in ((w_high, 0), (w_high, 1), (w_low, 0)):
                                last = nc.tensor.matmul(ps_in(i.par, c), w[:, at], rT[:, i.par, v, k, :],
                                                        start=(n == 0), stop=(n == 3 * DC - 1))
                                n += 1
                        if c % HB == HB - 1:
                            last.then_inc(in_done, 1)

                def layer_out(i):
                    e = expert_of(pe, i)
                    wait(pe, y_ready, i.g - 1)
                    n = 0
                    for c in range(FC):
                        if c % HB == 0:
                            pe.wait_ge(split_low, i.g * 2 + c // HB + 1)
                        at = bass.ds(e * (FC * D) + (W2_AT + c * D), D)
                        for w, v in ((w_high, hid_high), (w_high, hid_low), (w_low, hid_high)):
                            last = nc.tensor.matmul(ps_out(i.par), v[:, i.par, c, :], w[:, at],
                                                    start=(n == 0), stop=(n == 3 * FC - 1))
                            n += 1
                    last.then_inc(out_done, 1)

                transpose_rows(At(0, 0))
                layer_in(At(0, 0))
                transpose_rows(At(0, 1))
                layer_in(At(0, 1))
                transpose_rows(At(1, 0))
                layer_out(At(0, 0))
                with pe.Fori(1, TILES // 2) as h:
                    for c in (0, 1):
                        layer_in(At(h, c))
                        transpose_rows(At(h, c + 1))
                        layer_out(At(h, c - 1))
                layer_in(At(TILES // 2, 0))
                layer_out(At(TILES // 2, -1))
                layer_out(At(TILES // 2, 0))

            @block.scalar
            def _(sc):
                def bias_relu(i):
                    e = expert_of(sc, i)
                    for c in range(FC):
                        if c % HB == 0:
                            sc.wait_ge(in_done, i.g * 2 + c // HB + 1)
                            wait(sc, split_low, (i.g - 2) * 2 + c // HB + 1)
                        last = nc.scalar.activation(hid[:, i.par, c, :], ps_in(i.par, c), ACT.Relu,
                                                    scale=1.0 / WSCALE, bias=feat[:, bass.ds(e * FC + (B1 + c), 1)])
                        if c % HB == HB - 1:
                            last.then_inc(hid_ready, 1)

                bias_relu(At(0, 0))
                bias_relu(At(0, 1))
                with sc.Fori(1, TILES // 2) as h:
                    bias_relu(At(h, 0))
                    bias_relu(At(h, 1))
                bias_relu(At(TILES // 2, 0))

            @block.vector
            def _(dve):
                V = nc.vector

                def rows_out(i):
                    dve.wait_ge(rT_done, i.g + 1)
                    wait(dve, in_done, (i.g - 1) * 2)
                    V.tensor_copy(rT[:, i.par].rearrange("p k c s -> p (k c s)"), ps_rT(i.par)).then_inc(rT_ready, 1)

                def split(i, half):
                    dve.wait_ge(hid_ready, i.g * 2 + half + 1)
                    wait(dve, out_done, i.g - 1)
                    s = slice(half * HB, (half + 1) * HB)
                    V.tensor_copy(hid_high[:, i.par, s, :], hid[:, i.par, s, :]).then_inc(split_high, 1)
                    dve.wait_ge(split_high, i.g * 2 + half + 1)
                    V.tensor_tensor(hid_low[:, i.par, s, :], hid[:, i.par, s, :], hid_high[:, i.par, s, :],
                                    ALU.subtract).then_inc(split_low, 1)

                def add_bias(i):
                    e = expert_of(dve, i)
                    dve.wait_ge(out_done, i.g + 1)
                    wait(dve, y_stored[i.par], i.half * 16)
                    V.scalar_tensor_tensor(yb[:, i.par], ps_out(i.par), 1.0 / WSCALE, b2[:, bass.ds(e * D, D)],
                                           ALU.mult, ALU.add).then_inc(y_ready, 1)

                dve.wait_ge(b2_loaded, 16)
                rows_out(At(0, 0))
                split(At(0, 0), 0)
                rows_out(At(0, 1))
                split(At(0, 0), 1)
                split(At(0, 1), 0)
                rows_out(At(1, 0))
                split(At(0, 1), 1)
                add_bias(At(0, 0))
                with dve.Fori(1, TILES // 2) as h:
                    for c in (0, 1):
                        split(At(h, c), 0)
                        rows_out(At(h, c + 1))
                        split(At(h, c), 1)
                        add_bias(At(h, c - 1))
                split(At(TILES // 2, 0), 0)
                split(At(TILES // 2, 0), 1)
                add_bias(At(TILES // 2, -1))
                add_bias(At(TILES // 2, 0))


def combine(nc, sem, env):
    slots_out, residual_rows, out_rows, slot_of, gate = (
        env[n] for n in ("slots_out", "residual_rows", "out_rows", "slot_of", "gate"))

    with ExitStack() as ctx:
        def sb(name, shape, dt=F32):
            return ctx.enter_context(nc.sbuf_tensor(name, shape, dt))

        got = sb("got", [P, RING, 2, D])
        res = sb("res", [P, 2, GT, D])
        got_loaded = [sem(f"got_loaded{s}") for s in range(RING)]
        res_loaded = [sem("res_loaded0"), sem("res_loaded1")]
        out_stored = [sem("out_stored0"), sem("out_stored1")]
        first_added, second_added = sem("first_added"), sem("second_added")

        def of(rows, i):
            return rows[i.g] if isinstance(i.g, int) else rows[bass.ds(i.g, 1)].rearrange("o p t d -> (o p) t d")

        with nc.Block() as block:

            @block.gpsimd
            def _(pool):
                for j in range(NT):
                    wait(pool, second_added, j - RING + 1)
                    for k in range(2):
                        nc.gpsimd.indirect_dma_start(
                            out=got[:, j % RING, k, :], out_offset=None, in_=slots_out,
                            in_offset=bass.IndirectOffsetOnAxis(ap=slot_of[:, k, j:j + 1], axis=0),
                        ).then_inc(got_loaded[j % RING], 16)

            @block.sync
            def _(sp):
                def load(i):
                    wait(sp, out_stored[i.par], i.half * 16)
                    sp.dma_start(res[:, i.par], of(residual_rows, i)).then_inc(res_loaded[i.par], 16)

                def store(i):
                    sp.wait_ge(second_added, (i.g + 1) * GT)
                    sp.dma_start(of(out_rows, i), res[:, i.par]).then_inc(out_stored[i.par], 16)

                load(At(0, 0))
                load(At(0, 1))
                with sp.Fori(0, GROUPS // 2 - 1) as h:
                    for c in (0, 1):
                        store(At(h, c))
                        load(At(h, c + 2))
                store(At(GROUPS // 2 - 1, 0))
                store(At(GROUPS // 2 - 1, 1))
                for par in range(2):
                    sp.wait_ge(out_stored[par], GROUPS // 2 * 16)

            @block.vector
            def _(dve):
                def add(i):
                    dve.wait_ge(res_loaded[i.par], (i.half + 1) * 16)
                    for t in range(GT):
                        place = (i.par * GT + t) % RING
                        dve.wait_ge(got_loaded[place], (i.half + 1) * 32)
                        acc = res[:, i.par, t, :]
                        for k, done in ((0, first_added), (1, second_added)):
                            if k:
                                dve.wait_ge(first_added, i.g * GT + (t + 1))
                            nc.vector.scalar_tensor_tensor(acc, got[:, place, k, :],
                                                           gate[:, k, bass.ds(i.g * GT + t, 1)], acc,
                                                           ALU.mult, ALU.add).then_inc(done, 1)

                with dve.Fori(0, GROUPS // 2) as h:
                    add(At(h, 0))
                    add(At(h, 1))


def kernel(**inputs):
    import numpy as np
    import concourse.bacc as bacc
    from concourse.bass_utils import run_bass_kernel_spmd

    v = {name: np.asarray(a) for name, a in inputs.items()}
    adapter = {name[len("L0_cond_"):]: a for name, a in v.items() if name.startswith("L0_cond_")}
    moe = {name[len("L1_cond_"):]: a for name, a in v.items() if name.startswith("L1_cond_")}

    def columns(a):
        return a.reshape(-1, P).T

    w1 = moe["exp_w1"].reshape(EXPERTS, DC, P, FF).reshape(EXPERTS * DC, P, FF)
    w2 = moe["exp_w2"].reshape(EXPERTS, FC, P, D).transpose(0, 2, 1, 3).reshape(EXPERTS, P, DC, CHUNK)
    w2 = w2.transpose(0, 2, 1, 3).reshape(EXPERTS * DC, P, CHUNK)
    arrays = {
        "x": v["x"].reshape(TOKENS, D),
        "ids": v["itok_B_0_15"].reshape(1, ITEMS),
        "subject_ids": v["itok_B_6_14"].reshape(1, ITEMS),
        "down_w": adapter["down_W"].T.reshape(DC, P, A).transpose(1, 0, 2),
        "down_b": adapter["down_b"].reshape(A, 1),
        "up_w": adapter["up_W"].T,
        "up_b": adapter["up_b"].reshape(1, D),
        "adapter_w": adapter["expert_W"].reshape(ADAPTERS, A * A),
        "adapter_b": adapter["expert_b"],
        "domain_emb": adapter["domain_emb"],
        "gamma0": adapter["ln_gamma"].reshape(1, D),
        "beta0": adapter["ln_beta"].reshape(1, D),
        "subj_emb": moe["subj_emb"],
        "hyp_w1": moe["hyp_w1"],
        "hyp_w2": moe["hyp_w2"],
        "sty_w1": moe["sty_w1"],
        "sty_b1": moe["sty_b1"].reshape(SH // 2, 1),
        "sty_w2": moe["sty_w2"],
        "feature": np.concatenate([columns(moe[n]) for n in
                                   ("ln_g", "ln_b", "hyp_b1", "hyp_b2", "sty_b2", "exp_b1")], axis=1),
        "router_w": moe["router_w"].reshape(DC, P, EXPERTS).transpose(1, 0, 2),
        "expert_w": np.concatenate([w1, w2], axis=0),
        "exp_b2": moe["exp_b2"].reshape(1, EXPERTS * D),
    }
    arrays = {name: np.ascontiguousarray(a) for name, a in arrays.items()}

    nc = bacc.Bacc("TRN2", target_bir_lowering=False, num_devices=1)
    args = {name: nc.dram_tensor(name, a.shape, mybir.dt.from_np(a.dtype), kind="ExternalInput").ap()
            for name, a in arrays.items()}
    out = nc.dram_tensor("out", (TOKENS, D), F32, kind="ExternalOutput").ap()
    build(nc, **args, out=out)
    result = run_bass_kernel_spmd(nc, [arrays], core_ids=[0])
    return result.results[0]["out"].reshape(ITEMS, T, D)
```

```python
from contextlib import ExitStack

import concourse.bass as bass
from concourse import mybir

F32 = mybir.dt.float32
F16 = mybir.dt.float16
I32 = mybir.dt.int32
U32 = mybir.dt.uint32
ALU = mybir.AluOpType
ACT = mybir.ActivationFunctionType
AX = mybir.AxisListType.X

P = 128
ITEMS, T, D = 64, 64, 256
A, ADAPTERS = 64, 16
SUBJECTS, SE, SH = 32, 64, 128
EXPERTS, FF = 8, 1024
TOKENS = ITEMS * T
DC = D // P
FC = FF // P
GROUP = 512
GROUPS = TOKENS // GROUP
GT = GROUP // P
GI = GROUP // T
SUB = 2
SLOTS = SUB * P
TILES = (2 * TOKENS + EXPERTS * (SLOTS - 1)) // SLOTS
QUEUE = TOKENS + SLOTS
IDLE = EXPERTS * QUEUE
NONE_ROW = 32
CHUNK = 1024
CHUNKS = 2 * EXPERTS * DC * FF // CHUNK
CUTS = CHUNKS // GROUPS
W2_AT = EXPERTS * DC * FF
LOOP_FROM = 2
STAGES = 4
WSCALE = 256.0

ROW_TOKEN, ROW_DIFF, ROW_FIRST, ROW = 2 * D, 2 * D + 2, 2 * D + 4, 2 * D + 8

LN_G, LN_B, HYP_B1, HYP_B2, STY_B2, B1 = 0, DC, 2 * DC, 2 * DC + 1, 2 * DC + 2, 4 * DC + 2
FEATURE_COLS = B1 + EXPERTS * FC


class At:

    def __init__(self, h, c=0):
        self.g = h * 2 + c
        self.par = c % 2
        self.half = h + c // 2


def wait(eng, sem, value):
    if not isinstance(value, int) or value > 0:
        eng.wait_ge(sem, value)


def wait_apart(eng, held, *waits):
    waits = [(sem, value if isinstance(value, int) else eng.to_reg(value)) for sem, value in waits]
    if not isinstance(waits[0][1], int):
        eng.wait_ge(held, 1)
    for sem, value in waits:
        wait(eng, sem, value)


def upto(g, n, most):
    return min(g + n, most) if isinstance(g, int) else g + n


def bcast(ap, axis, shape):
    return ap.unsqueeze(axis).broadcast_to(shape)


def spread(ap, partitions):
    return ap.partition_broadcast(partitions).rearrange("q o n -> q (o n)")


def build(nc, x, ids, subject_ids, down_w, down_b, up_w, up_b, adapter_w, adapter_b, domain_emb,
          gamma0, beta0, subj_emb, hyp_w1, hyp_w2, sty_w1, sty_b1, sty_w2, feature, router_w,
          expert_w, exp_b2, out):
    x_rows = x.rearrange("(g t p) d -> g p t d", t=GT, p=P)
    out_rows = out[0:TOKENS].rearrange("(g t p) d -> g p t d", t=GT, p=P)
    spare_rows = out[TOKENS:TOKENS + P]

    queues = nc.dram_tensor("queues", (IDLE + SLOTS, ROW // 2), U32, kind="Internal").ap()

    with ExitStack() as whole:
        def sem(name):
            return whole.enter_context(nc.semaphore(name))

        def keep(name, shape, dt):
            return whole.enter_context(nc.sbuf_tensor(name, shape, dt))

        w_high = keep("w_high", [P, CHUNKS * CHUNK], F16)
        w_low = keep("w_low", [P, CHUNKS * CHUNK], F16)
        feat = keep("feat", [P, FEATURE_COLS], F32)
        ident16 = keep("ident16", [P, P], F16)
        tile_expert = keep("tile_expert", [1, TILES], I32)
        tile_row = keep("tile_row", [1, TILES], I32)
        tile_expert_f = keep("tile_expert_f", [P, TILES], F32)
        banks = whole.enter_context(nc.psum_tensor("banks", [P, 8, 512], F32))

        dense(nc, sem, locals())
        experts(nc, sem, locals())


def dense(nc, sem, env):
    (x_rows, ids, subject_ids, down_w, down_b, up_w, up_b, adapter_w, adapter_b, domain_emb, gamma0,
     beta0, subj_emb, hyp_w1, hyp_w2, sty_w1, sty_b1, sty_w2, feature, router_w, expert_w, out_rows,
     spare_rows, queues) = (env[n] for n in (
         "x_rows", "ids", "subject_ids", "down_w", "down_b", "up_w", "up_b", "adapter_w",
         "adapter_b", "domain_emb", "gamma0", "beta0", "subj_emb", "hyp_w1", "hyp_w2", "sty_w1",
         "sty_b1", "sty_w2", "feature", "router_w", "expert_w", "out_rows", "spare_rows", "queues"))
    w_high, w_low, feat, ident16, tile_expert, tile_row, tile_expert_f, banks = (
        env[n] for n in ("w_high", "w_low", "feat", "ident16", "tile_expert", "tile_row",
                         "tile_expert_f", "banks"))

    with ExitStack() as ctx:
        def sb(name, shape, dt=F32):
            return ctx.enter_context(nc.sbuf_tensor(name, shape, dt))

        ident = sb("ident", [P, P])
        minus_half = sb("minus_half", [P, GI * DC])
        part_no = sb("part_no", [P, 1])
        expert_no = sb("expert_no", [P, EXPERTS])
        queue_start = sb("queue_start", [P, EXPERTS])
        earlier16 = sb("earlier16", [P, P], F16)
        ones16 = sb("ones16", [P, P], F16)
        dw = sb("dw", [P, DC, A])
        ab = sb("ab", [A, 2])
        uw = sb("uw", [A + 1, D])
        g0 = sb("g0", [P, D])
        b0 = sb("b0", [P, D])
        rw = sb("rw", [P, DC, EXPERTS])
        item_gamma = sb("item_gamma", [P, DC, ITEMS])
        item_beta = sb("item_beta", [P, DC, ITEMS])
        item_add = sb("item_add", [P, A])

        h_rows = sb("h_rows", [P, 2, GT, ROW], F16)
        stage = sb("stage", [P, STAGES, CHUNK])
        xb = sb("xb", [P, 2, GT, D])
        rb = sb("rb", [P, 2, GT, D])
        nb = sb("nb", [P, GT, D])
        xT = sb("xT", [P, DC, GROUP])
        hT = sb("hT", [P, DC, GROUP])
        act = sb("act", [A, GROUP])
        dom = sb("dom", [A + 1, GROUP])
        wnow = sb("wnow", [A, 2, GI * A])
        stats0 = sb("stats0", [P, GT, 6])
        mv0 = sb("mv0", [P, GT, 2])
        rs0 = sb("rs0", [P, GT])
        stats1 = sb("stats1", [P, GT, 6])
        mv1 = sb("mv1", [P, GT, 2])
        rs1 = sb("rs1", [P, GT])
        shift1 = sb("shift1", [P, GT])
        statsT = sb("statsT", [P, DC * GI, 6])
        msum = sb("msum", [P, DC * GI])
        mdiff = sb("mdiff", [P, DC * GI])
        var4 = sb("var4", [P, DC * GI])
        rsT = sb("rsT", [P, DC * GI])
        aff_a = sb("aff_a", [P, DC, GI])
        aff_c = sb("aff_c", [P, DC, GI])

        pad_row = sb("pad_row", [P, ROW], F16)
        tile_no = sb("tile_no", [P, TILES])
        tile_start = sb("tile_start", [P, TOKENS // SLOTS])
        zeros = sb("zeros", [P, EXPERTS])
        counts = sb("counts", [1, EXPERTS], I32)
        lg = sb("lg", [P, GT, EXPERTS])
        top = sb("top", [P, GT, 8])
        top_at = sb("top_at", [P, GT, 8], U32)
        choice = sb("choice", [P, GT, 2])
        mask = sb("mask", [P, GT, 2, EXPERTS])
        chosen = sb("chosen", [P, GT, EXPERTS], F16)
        chosen_sum = sb("chosen_sum", [P, GT, EXPERTS], F16)
        place = sb("place", [P, GT, EXPERTS])
        slot_f = sb("slot_f", [P, GT, 2])
        slot = sb("slot", [P, 2, GT, 2], U32)

        table = w_low[0:NONE_ROW + 1, 16 * CHUNK:24 * CHUNK].bitcast(F32)
        wsel = w_low[0:A, 24 * CHUNK:32 * CHUNK].bitcast(F32)
        wsel_io = wsel.rearrange("a (i o) -> a i o", o=A)
        scratch = w_high[:, 24 * CHUNK:32 * CHUNK].bitcast(F32)
        at = [0]

        def scr(rows, cols):
            at[0] += cols
            return scratch[0:rows, at[0] - cols:at[0]]

        idf = scr(NONE_ROW + 1, ITEMS)
        sidf = scr(SUBJECTS, ITEMS)
        idc = scr(NONE_ROW + 1, ITEMS)
        hot_w = scr(NONE_ROW + 1, ITEMS)
        hot_e = scr(ADAPTERS, ITEMS)
        hot_s = scr(SUBJECTS, ITEMS)
        t_ab = scr(ADAPTERS, A)
        t_de = scr(ADAPTERS, A)
        t_se = scr(SUBJECTS, SE)
        hw1 = scr(SE, SH)
        hw2 = scr(SH, SH)
        sw1 = scr(SH, SH // 2)
        sw2 = scr(SH // 2, 2 * D)
        se_sb = scr(SE, ITEMS)
        hy1 = scr(SH, ITEMS)
        hy2 = scr(SH, ITEMS)
        st1 = scr(SH // 2, ITEMS)
        style = scr(P, DC * ITEMS)
        absz = scr(P, DC * ITEMS)
        expz = scr(P, DC * ITEMS)
        lnz = scr(P, DC * ITEMS)
        ids_i = scr(NONE_ROW + 1, ITEMS).bitcast(I32)
        sids_i = scr(SUBJECTS, ITEMS).bitcast(I32)

        zero_out = hT[:, 0, 0:D]
        earlier = hT[:, 1, 0:P]
        first_tokens = hT[:, 1, P:P + 2 * GT].rearrange("p (a t) -> p a t", t=GT)
        spare_no = hT[:, 1, P + 2 * GT:P + 2 * GT + 1]

        G = TILES * EXPERTS
        assert 3 * G + 2 * TILES + 8 * 16 + TOKENS // SLOTS * EXPERTS <= 2 * GT * D
        tabs = rb[:, :, :, :].rearrange("p a t d -> p (a t d)")

        def grid(k):
            return tabs[:, k * G:(k + 1) * G].rearrange("p (i e) -> p i e", e=EXPERTS)

        def line(k):
            return tabs[:, 3 * G + k * TILES:3 * G + (k + 1) * TILES]

        def per_expert(k):
            at = 3 * G + 2 * TILES + k * EXPERTS
            return tabs[:, at:at + EXPERTS]

        over = tabs[:, 3 * G + 2 * TILES + 8 * 16:3 * G + 2 * TILES + 8 * 16 + TOKENS // SLOTS * EXPERTS]
        def float_field(rows, at):
            return rows[:, :, at:at + 2].bitcast(F32).rearrange("p t o -> p (t o)")

        def token_field(rows, flat):
            field = rows[:, :, ROW_TOKEN:ROW_TOKEN + 2] if len(rows.shape) == 3 else rows[:, :, :, ROW_TOKEN:ROW_TOKEN + 2]
            return field.bitcast(I32).rearrange(flat)

        ps_x = banks[:, 0:2, :]
        ps_u = banks[:, 2:4, :].rearrange("p a b -> p (a b)").rearrange("p (t d) -> p t d", d=D)
        ps_h = banks[:, 4:6, :].rearrange("p a b -> p (a b)").rearrange("p (t d) -> p t d", d=D)
        ps_down = banks[0:A, 6, :]
        ps_lg = banks[:, 6, 0:GT * EXPERTS].rearrange("p (t e) -> p t e", e=EXPERTS)
        ps_dom = banks[0:A, 7, :]
        ps_rank = banks[:, 7, 0:GT * EXPERTS].rearrange("p (t e) -> p t e", e=EXPERTS)

        ids_loaded, table_loaded, consts_loaded = sem("ids_loaded"), sem("table_loaded"), sem("consts_loaded")
        table_cleared, pool_consts, cleared_zero = sem("table_cleared"), sem("pool_consts"), sem("cleared_zero")
        rows_cleared, rows_numbered, filled = sem("rows_cleared"), sem("rows_numbered"), sem("filled")
        ids_float, hot_ready, select_done, select_copied = (
            sem("ids_float"), sem("hot_ready"), sem("select_done"), sem("select_copied"))
        net_done, net_ready, style_step, lnz_ready = (
            sem("net_done"), sem("net_ready"), sem("style_step"), sem("lnz_ready"))
        dom_row, spare_stored = sem("dom_row"), sem("spare_stored")
        x_loaded = [sem("x_loaded0"), sem("x_loaded1")]
        wnow_loaded = [sem("wnow_loaded0"), sem("wnow_loaded1")]
        x1_stored = [sem("x1_stored0"), sem("x1_stored1")]
        stage_loaded = [sem(f"stage_loaded{s}") for s in range(STAGES)]
        (xT_done, xT_ready, down_done, act_ready, adapt_done, dom_ready, up_done, st0_ready,
         mv0_ready, ve0_ready, rs0_ready, centred_ready, x1_ready, st1_ready, mv1_ready, ve1_ready,
         rs1_ready, shift1_ready, n_ready, nT_done, hT_ready) = (sem(n) for n in (
             "xT_done", "xT_ready", "down_done", "act_ready", "adapt_done", "dom_ready", "up_done",
             "st0_ready", "mv0_ready", "ve0_ready", "rs0_ready", "centred_ready",
             "x1_ready", "st1_ready", "mv1_ready", "ve1_ready", "rs1_ready", "shift1_ready",
             "n_ready", "nT_done", "hT_ready"))
        (stT_ready, item_step, var4_ready, rsT_ready, scaled_ready, aff_c_ready, h_ready, h_rest_ready, logits_done,
         logits_copied, back_done, high_ready, low_ready) = (sem(n) for n in (
             "stT_ready", "item_step", "var4_ready", "rsT_ready", "scaled_ready", "aff_c_ready",
             "h_ready", "h_rest_ready", "logits_done", "logits_copied", "back_done", "high_ready", "low_ready"))
        w_high_ready, w_low_ready = sem("w_high_ready"), sem("w_low_ready")
        (top_ready, top_at_ready, choice_ready, mask_ready, chosen_ready, rank_done, sum_ready,
         place_ready, picked_ready, slot_f_ready, slots_known) = (sem(n) for n in (
             "top_ready", "top_at_ready", "choice_ready", "mask_ready", "chosen_ready", "rank_done",
             "sum_ready", "place_ready", "picked_ready", "slot_f_ready", "slots_known"))
        scattered = [sem("scattered0"), sem("scattered1")]
        counted, counts_known, table_step = sem("counted"), sem("counts_known"), sem("table_step")
        N_CONSTS = 16
        N_POOL = 13

        def iterations(eng, body, first=LOOP_FROM, until=GROUPS // 2):
            for i in range(2 * first):
                body(At(i // 2, i % 2))
            with eng.Fori(first, until) as h:
                body(At(h, 0))
                body(At(h, 1))
            for i in range(2 * until, GROUPS + 2):
                body(At(i // 2, i % 2))

        def back(i, n):
            if isinstance(i.g, int):
                g = i.g - n
                return At(g // 2, g % 2) if 0 <= g < GROUPS else None
            return At(i.half, i.par - n)

        def chunks(i):
            if isinstance(i.g, int) and i.g >= GROUPS:
                return []
            return [(i.g * CUTS + s, s) for s in range(CUTS)]

        with nc.Block() as block:

            @block.sync
            def _(sp):
                def of(rows, g):
                    return rows[g] if isinstance(g, int) else rows[bass.ds(g, 1)].rearrange("o p t d -> (o p) t d")

                def load_x(i):
                    sp.dma_start(xb[:, i.par], of(x_rows, i.g)).then_inc(x_loaded[i.par], 16)

                def load_adapters(i):
                    wait(sp, adapt_done, i.g - 1)
                    sp.dma_start(wnow[:, i.par], wsel[:, bass.ds(i.g * GI * A, GI * A)]).then_inc(wnow_loaded[i.par], 16)

                def load_weights(i):
                    for q, slot in chunks(i):
                        wait(sp, w_low_ready, q - STAGES + 1)
                        src = expert_w[q] if isinstance(q, int) else expert_w[bass.ds(q, 1)].rearrange("o p c -> (o p) c")
                        sp.dma_start(stage[:, slot], src).then_inc(stage_loaded[slot], 16)

                sp.dma_start(ids_i, spread(ids, NONE_ROW + 1)).then_inc(ids_loaded, 16)
                sp.dma_start(sids_i, spread(subject_ids, SUBJECTS)).then_inc(ids_loaded, 16)
                load_x(At(0, 0))
                for dst, src in ((dw[:], down_w), (ab[:, 0:1], down_b), (ab[:, 1:2], sty_b1),
                                 (t_ab, adapter_b), (t_de, domain_emb), (t_se, subj_emb)):
                    sp.dma_start(dst, src).then_inc(consts_loaded, 16)
                sp.wait_ge(table_cleared, 2)
                sp.dma_start(table[0:ADAPTERS], adapter_w).then_inc(table_loaded, 16)
                for dst, src in ((uw[0:A], up_w), (uw[A:A + 1], up_b), (feat[:], feature),
                                 (hw1, hyp_w1), (hw2, hyp_w2), (sw1, sty_w1), (sw2, sty_w2),
                                 (rw[:], router_w), (g0[:], spread(gamma0, P)), (b0[:], spread(beta0, P))):
                    sp.dma_start(dst, src).then_inc(consts_loaded, 16)
                load_x(At(0, 1))
                sp.wait_ge(cleared_zero, 1)
                sp.dma_start(spare_rows, zero_out).then_inc(spare_stored, 16)
                sp.wait_ge(rows_numbered, 2)
                sp.dma_start(queues[IDLE:IDLE + SLOTS].rearrange("(s p) d -> p s d", p=P),
                             bcast(pad_row[:].bitcast(U32), 1, [P, SUB, ROW // 2])).then_inc(filled, 16)
                sp.wait_ge(select_copied, A // 8)

                def body(i):
                    if (s1 := back(i, 0)) is not None:
                        load_adapters(s1)
                    load_weights(i)
                    if (s2 := back(i, 1)) is not None:
                        if not isinstance(i.g, int) or i.g + 1 < GROUPS:
                            wait_apart(sp, ids_loaded, (up_done, s2.g + 1))
                            load_x(At(s2.half + 1, s2.par))
                        sp.wait_ge(x1_ready, s2.g + 1)
                        sp.dma_start(of(out_rows, s2.g), rb[:, s2.par]).then_inc(x1_stored[s2.par], 16)

                iterations(sp, body, until=GROUPS // 2 - 1)
                sp.wait_ge(counts_known, 1)
                with sp.Fori(0, EXPERTS) as e:
                    count = sp.value_load(counts[0:1, bass.ds(e, 1)], min_val=0, max_val=TOKENS)
                    sp.dma_start(queues[bass.ds(e * QUEUE + count, SLOTS)].rearrange("(s p) d -> p s d", p=P),
                                 bcast(pad_row[:].bitcast(U32), 1, [P, SUB, ROW // 2])).then_inc(filled, 16)
                for par in range(2):
                    sp.wait_ge(x1_stored[par], GROUPS // 2 * 16)
                sp.wait_ge(spare_stored, 16)
                sp.wait_ge(filled, (EXPERTS + 1) * 16)

            @block.gpsimd
            def _(pool):
                def iota(dst, pattern, base=0, channel=0):
                    return nc.gpsimd.iota(dst, pattern, base=base, channel_multiplier=channel,
                                          allow_small_or_imprecise_dtypes=True)

                nc.gpsimd.memset(table[:], 0.0).then_inc(table_cleared, 1)
                pool.wait_ge(table_cleared, 1)
                row = table[NONE_ROW:NONE_ROW + 1].rearrange("r (o a) -> r o a", a=A)
                nc.gpsimd.affine_select(out=row, in_=row, compare_op=ALU.not_equal, fill=1.0, base=0,
                                        pattern=[[1, A], [-1, A]], channel_multiplier=0).then_inc(table_cleared, 1)
                pool.wait_ge(table_cleared, 2)
                iota(part_no[:], [[0, 1]], channel=1).then_inc(pool_consts, 1)
                nc.gpsimd.memset(ident[:], 0.0).then_inc(pool_consts, 1)
                pool.wait_ge(pool_consts, 2)
                nc.gpsimd.affine_select(out=ident[:], in_=ident[:], compare_op=ALU.not_equal, fill=1.0, base=0,
                                        pattern=[[-1, P]], channel_multiplier=1).then_inc(pool_consts, 1)
                nc.gpsimd.memset(minus_half[:], -0.5).then_inc(pool_consts, 1)
                nc.gpsimd.memset(item_add[:], 0.0).then_inc(pool_consts, 1)
                nc.gpsimd.memset(zero_out, 0.0).then_inc(cleared_zero, 1)
                nc.gpsimd.memset(earlier, 0.0).then_inc(pool_consts, 1)
                pool.wait_ge(pool_consts, 6)
                nc.gpsimd.affine_select(out=earlier, in_=earlier, compare_op=ALU.is_ge, fill=1.0, base=0,
                                        pattern=[[-1, P]], channel_multiplier=1).then_inc(pool_consts, 1)
                nc.gpsimd.tensor_copy(ident16[:], ident[:]).then_inc(pool_consts, 1)
                nc.gpsimd.memset(ones16[:], 1.0).then_inc(pool_consts, 1)
                pool.wait_ge(pool_consts, 7)
                nc.gpsimd.tensor_copy(earlier16[:], earlier).then_inc(pool_consts, 1)
                iota(expert_no[:], [[1, EXPERTS]]).then_inc(pool_consts, 1)
                iota(queue_start[:], [[QUEUE, EXPERTS]]).then_inc(pool_consts, 1)
                nc.gpsimd.memset(chosen_sum[:], 0.0).then_inc(pool_consts, 1)
                nc.gpsimd.memset(h_rows[:], 0.0).then_inc(rows_cleared, 1)
                nc.gpsimd.memset(pad_row[:], 0.0).then_inc(rows_cleared, 1)
                iota(first_tokens, [[GROUP, 2], [P, GT]], base=-2 * GROUP, channel=1).then_inc(rows_cleared, 1)
                iota(spare_no, [[0, 1]], base=TOKENS, channel=1).then_inc(rows_cleared, 1)
                iota(tile_no[:], [[1, TILES]]).then_inc(rows_cleared, 1)
                iota(tile_start[:], [[SLOTS, TOKENS // SLOTS]]).then_inc(rows_cleared, 1)
                nc.gpsimd.memset(zeros[:], 0.0).then_inc(rows_cleared, 1)

                def rstd(g, mv, mv_sem, rs, used_sem, ve_sem, rs_sem):
                    wait_apart(pool, select_copied, (mv_sem, g + 1), (used_sem, g))
                    nc.gpsimd.tensor_scalar(rs[:], mv[:, :, 1], 1e-5, None, ALU.add).then_inc(ve_sem, 1)
                    pool.wait_ge(ve_sem, g + 1)
                    nc.gpsimd.tensor_tensor(rs[:], rs[:], minus_half[:, 0:GT], ALU.pow).then_inc(rs_sem, 1)

                def scatter(i, tiles):
                    wait_apart(pool, select_copied, (slots_known, i.g + 1))
                    for t in tiles:
                        for k in range(2):
                            nc.gpsimd.indirect_dma_start(
                                out=queues, out_offset=bass.IndirectOffsetOnAxis(ap=slot[:, i.par, t, k:k + 1], axis=0),
                                in_=h_rows[:, i.par, t, :].bitcast(U32), in_offset=None).then_inc(scattered[i.par], 16)

                def body(i):
                    s2, s3, s4 = back(i, 1), back(i, 2), back(i, 3)
                    if s2 is not None:
                        rstd(s2.g, mv0, mv0_ready, rs0, x1_ready, ve0_ready, rs0_ready)
                    if s3 is not None:
                        pool.wait_ge(var4_ready, s3.g + 1)
                        nc.gpsimd.tensor_tensor(rsT[:], var4[:], minus_half[:], ALU.pow).then_inc(rsT_ready, 1)
                    if s4 is not None:
                        scatter(s4, range(0, GT // 2))
                    if s2 is not None:
                        rstd(s2.g, mv1, mv1_ready, rs1, n_ready, ve1_ready, rs1_ready)
                    if s4 is not None:
                        scatter(s4, range(GT // 2, GT))

                pool.wait_ge(select_copied, A // 8)
                iterations(pool, body)
                scatter(At(GROUPS // 2, -1), range(GT))
                for par in range(2):
                    pool.wait_ge(scattered[par], GROUPS // 2 * GT * 2 * 16)

            @block.tensor
            def _(pe):
                def setup():
                    pe.wait_ge(consts_loaded, 16 * N_CONSTS)
                    pe.wait_ge(hot_ready, 3)
                    nc.tensor.matmul(banks[0:ITEMS, 6, 0:A], hot_w[0:ADAPTERS], t_ab, start=True, stop=False)
                    nc.tensor.matmul(banks[0:ITEMS, 6, 0:A], hot_e, t_de, start=False, stop=True)
                    nc.tensor.matmul(banks[0:SE, 7, 0:ITEMS], t_se, hot_s, start=True, stop=True).then_inc(net_done, 1)
                    pe.wait_ge(table_loaded, 16)
                    for b in range(A // 8):
                        wait(pe, select_copied, b - 1)
                        for k in range(8):
                            o = b * 8 + k
                            last = nc.tensor.matmul(banks[0:A, b % 2, k * ITEMS:(k + 1) * ITEMS],
                                                    table[:, o * A:(o + 1) * A], hot_w, start=True, stop=True)
                        last.then_inc(select_done, 1)
                    for w, src, bank, n, k in ((hw1, se_sb, 6, SH, 1), (hw2, hy1, 7, SH, 2), (sw1, hy2, 6, SH // 2, 3)):
                        pe.wait_ge(net_ready, k + 1)
                        nc.tensor.matmul(banks[0:n, bank, 0:ITEMS], w, src, start=True, stop=True).then_inc(net_done, 1)
                    pe.wait_ge(net_ready, 5)
                    for c in range(2 * DC):
                        last = nc.tensor.matmul(banks[:, 7, c * ITEMS:(c + 1) * ITEMS], sw2[:, c * P:(c + 1) * P],
                                                st1, start=True, stop=True)
                    last.then_inc(net_done, 1)

                def into_features(i):
                    pe.wait_ge(x_loaded[i.par], (i.half + 1) * 16)
                    wait(pe, hT_ready, i.g - 1)
                    for c in range(DC):
                        for t in range(GT):
                            last = nc.tensor.transpose(ps_x[:, c, t * P:(t + 1) * P],
                                                       xb[:, i.par, t, c * P:(c + 1) * P], ident[:])
                    last.then_inc(xT_done, 1)

                def adapter(i):
                    wait_apart(pe, dom_row, (dom_ready, i.g))
                    wait(pe, place_ready, i.g - 2)
                    nc.tensor.matmul(ps_dom, item_add[:], bcast(ident[:, bass.ds(i.g * GI, GI)], 2, [P, GI, T]),
                                     start=True, stop=False)
                    pe.wait_ge(xT_ready, i.g + 1)
                    wait(pe, logits_copied, i.g - 2)
                    for c in range(DC):
                        last = nc.tensor.matmul(ps_down, dw[:, c, :], xT[:, c, :], start=(c == 0), stop=(c == DC - 1))
                    last.then_inc(down_done, 1)
                    wait_apart(pe, dom_row, (wnow_loaded[i.par], (i.half + 1) * 16))
                    pe.wait_ge(act_ready, i.g + 1)
                    for b in range(GI):
                        last = nc.tensor.matmul(ps_dom[:, b * T:(b + 1) * T], wnow[:, i.par, b * A:(b + 1) * A],
                                                act[:, b * T:(b + 1) * T], start=False, stop=(b == GI - 1))
                    last.then_inc(adapt_done, 1)
                    pe.wait_ge(dom_ready, i.g + 1)
                    wait(pe, centred_ready, i.g)
                    for t in range(GT):
                        nc.tensor.matmul(ps_u[:, t, :], dom[:, t * P:(t + 1) * P], uw[:], start=True, stop=False)
                        last = nc.tensor.matmul(ps_u[:, t, :], ident[:], xb[:, i.par, t, :], start=False, stop=True)
                    last.then_inc(up_done, 1)

                def route_and_back(i):
                    pe.wait_ge(h_ready, i.g + 1)
                    pe.wait_ge(h_rest_ready, i.g + 1)
                    pe.wait_ge(act_ready, upto(i.g, 3, GROUPS))
                    for t in range(GT):
                        for c in range(DC):
                            last = nc.tensor.matmul(ps_lg[:, t, :], hT[:, c, t * P:(t + 1) * P], rw[:, c, :],
                                                    start=(c == 0), stop=(c == DC - 1))
                    last.then_inc(logits_done, 1)
                    wait(pe, low_ready, i.g)
                    for t in range(GT):
                        for c in range(DC):
                            last = nc.tensor.transpose(ps_h[:, t, c * P:(c + 1) * P], hT[:, c, t * P:(t + 1) * P], ident[:])
                    last.then_inc(back_done, 1)

                def normed_into_features(i):
                    pe.wait_ge(n_ready, i.g + 1)
                    pe.wait_ge(xT_ready, upto(i.g, 2, GROUPS))
                    for c in range(DC):
                        for t in range(GT):
                            last = nc.tensor.transpose(ps_x[:, c, t * P:(t + 1) * P], nb[:, t, c * P:(c + 1) * P], ident[:])
                    last.then_inc(nT_done, 1)

                def rank(i):
                    pe.wait_ge(chosen_ready, i.g + 1)
                    pe.wait_ge(dom_ready, upto(i.g, 3, GROUPS))
                    wait(pe, sum_ready, i.g)
                    nc.tensor.matmul(ps_rank, earlier16[:], chosen[:], start=True, stop=False)
                    for n in range(1, GT):
                        nc.tensor.matmul(ps_rank[:, n:GT, :], ones16[:], chosen[:, 0:GT - n, :], start=False, stop=False)
                    for t in range(GT):
                        last = nc.tensor.matmul(ps_rank, ones16[:], bcast(chosen_sum[:, t, :], 1, [P, GT, EXPERTS]),
                                                start=False, stop=(t == GT - 1))
                    last.then_inc(rank_done, 1)

                pe.wait_ge(pool_consts, N_POOL)
                setup()
                pe.wait_ge(net_ready, 6)
                pe.wait_ge(select_copied, A // 8)
                pe.wait_ge(dom_row, 2)

                def body(i):
                    s1, s2, s3 = back(i, 0), back(i, 1), back(i, 2)
                    if s1 is not None:
                        into_features(s1)
                        adapter(s1)
                    if s3 is not None:
                        route_and_back(s3)
                    if s2 is not None:
                        normed_into_features(s2)
                    if s3 is not None:
                        rank(s3)

                iterations(pe, body)
                pe.wait_ge(sum_ready, GROUPS)
                for t in range(GT):
                    last = nc.tensor.matmul(banks[:, 6, 0:EXPERTS], ones16[:], chosen_sum[:, t, :],
                                            start=(t == 0), stop=(t == GT - 1))
                last.then_inc(counted, 1)

            @block.scalar
            def _(sc):
                sc.wait_ge(net_ready, 6)
                nc.scalar.activation(absz, style, ACT.Abs).then_inc(style_step, 1)
                sc.wait_ge(style_step, 1)
                nc.scalar.activation(expz, absz, ACT.Exp, scale=-1.0).then_inc(style_step, 1)
                sc.wait_ge(style_step, 2)
                nc.scalar.activation(lnz, expz, ACT.Ln, bias=1.0).then_inc(lnz_ready, 1)

                def cut_high(i, some):
                    for q, slot in chunks(i)[some]:
                        sc.wait_ge(stage_loaded[slot], (i.g + 1) * 16)
                        nc.scalar.activation(w_high[:, bass.ds(q * CHUNK, CHUNK)], stage[:, slot], ACT.Copy,
                                             scale=WSCALE).then_inc(w_high_ready, 1)

                def activate(i):
                    sc.wait_ge(xT_done, i.g + 1)
                    wait(sc, down_done, i.g)
                    nc.scalar.activation(xT[:], ps_x[:], ACT.Copy).then_inc(xT_ready, 1)
                    sc.wait_ge(down_done, i.g + 1)
                    wait(sc, adapt_done, i.g)
                    if isinstance(i.g, int) and i.g == 0:
                        sc.wait_ge(consts_loaded, 16 * N_CONSTS)
                    nc.scalar.activation(act[:], ps_down, ACT.Gelu, bias=ab[:, 0:1]).then_inc(act_ready, 1)

                def adapted(i):
                    sc.wait_ge(adapt_done, i.g + 1)
                    wait(sc, up_done, i.g)
                    nc.scalar.activation(dom[0:A], ps_dom, ACT.Copy).then_inc(dom_ready, 1)

                def item_norm(i):
                    sc.wait_ge(aff_c_ready, (i.g + 1) * 3)
                    for b in range(GI):
                        v = hT[:, 0, b * T:(b + 1) * T]
                        last = nc.scalar.activation(v, v, ACT.Identity, scale=aff_a[:, 0, b:b + 1],
                                                    bias=aff_c[:, 0, b:b + 1])
                    last.then_inc(h_ready, 1)

                def logits(i):
                    sc.wait_ge(logits_done, i.g + 1)
                    wait(sc, top_at_ready, i.g)
                    nc.scalar.activation(lg[:], ps_lg, ACT.Copy).then_inc(logits_copied, 1)

                def high(i):
                    sc.wait_ge(back_done, i.g + 1)
                    if isinstance(i.g, int) and i.g == 0:
                        sc.wait_ge(rows_numbered, 2)
                    wait(sc, scattered[i.par], i.half * GT * 2 * 16)
                    nc.scalar.activation(h_rows[:, i.par, :, 0:D], ps_h, ACT.Copy).then_inc(high_ready, 1)

                def layer_norm(i):
                    sc.wait_ge(shift1_ready, i.g + 1)
                    wait(sc, nT_done, i.g)
                    for t in range(GT):
                        last = nc.scalar.activation(nb[:, t, :], rb[:, i.par, t, :], ACT.Identity,
                                                    scale=rs1[:, t:t + 1], bias=shift1[:, t:t + 1])
                    last.then_inc(n_ready, 1)
                    if isinstance(i.g, int) and i.g == 0:
                        sc.wait_ge(spare_stored, 16)

                def scale_features(i):
                    sc.wait_ge(nT_done, i.g + 1)
                    wait(sc, back_done, i.g)
                    for c in range(DC):
                        last = nc.scalar.activation(hT[:, c, :], ps_x[:, c, :], ACT.Identity,
                                                    scale=feat[:, LN_G + c:LN_G + c + 1],
                                                    bias=feat[:, LN_B + c:LN_B + c + 1])
                    last.then_inc(hT_ready, 1)

                def body(i):
                    s1, s2, s3 = back(i, 0), back(i, 1), back(i, 2)
                    if s1 is not None:
                        activate(s1)
                        cut_high(i, slice(0, 1))
                        adapted(s1)
                    cut_high(i, slice(1, 2))
                    if s3 is not None:
                        item_norm(s3)
                    cut_high(i, slice(2, 3))
                    if s3 is not None:
                        logits(s3)
                    cut_high(i, slice(3, 4))
                    if s2 is not None:
                        layer_norm(s2)
                    if s3 is not None:
                        high(s3)
                    if s2 is not None:
                        scale_features(s2)

                iterations(sc, body)

            @block.vector
            def _(dve):
                V = nc.vector
                step = [0]

                def link(ins):
                    step[0] += 1
                    ins.then_inc(table_step, 1)
                    dve.wait_ge(table_step, step[0])

                V.memset(dom[A:A + 1, :], 1.0).then_inc(dom_row, 1)
                dve.wait_ge(ids_loaded, 32)
                dve.wait_ge(pool_consts, 1)
                link(V.tensor_copy(idf, ids_i))
                link(V.tensor_copy(sidf, sids_i))
                link(V.tensor_scalar(idc, idf, 0.0, float(ADAPTERS - 1), ALU.max, ALU.min))
                link(V.tensor_scalar(hot_w, idf, part_no[0:NONE_ROW + 1, 0:1], None, ALU.is_equal))
                V.tensor_tensor(hot_w[NONE_ROW:NONE_ROW + 1], idf[NONE_ROW:NONE_ROW + 1],
                                idc[NONE_ROW:NONE_ROW + 1], ALU.not_equal).then_inc(hot_ready, 1)
                V.tensor_scalar(hot_e, idc[0:ADAPTERS], part_no[0:ADAPTERS, 0:1], None, ALU.is_equal).then_inc(hot_ready, 1)
                link(V.tensor_scalar(sidf, sidf, 0.0, float(SUBJECTS - 1), ALU.max, ALU.min))
                V.tensor_scalar(hot_s, sidf, part_no[0:SUBJECTS, 0:1], None, ALU.is_equal).then_inc(hot_ready, 1)
                dve.wait_ge(consts_loaded, 16 * N_CONSTS)
                dve.wait_ge(net_done, 1)
                dve.wait_ge(pool_consts, N_POOL)
                V.tensor_copy(item_add[0:ITEMS], banks[0:ITEMS, 6, 0:A]).then_inc(dom_row, 1)
                V.tensor_copy(se_sb, banks[0:SE, 7, 0:ITEMS]).then_inc(net_ready, 2)
                for b in range(A // 8):
                    dve.wait_ge(select_done, b + 1)
                    V.tensor_copy(wsel_io[:, :, b * 8:(b + 1) * 8].rearrange("a i o -> a o i"),
                                  banks[0:A, b % 2, :].rearrange("a (o i) -> a o i", i=ITEMS)).then_inc(select_copied, 1)
                dve.wait_ge(net_done, 2)
                V.tensor_scalar(hy1, banks[0:SH, 6, 0:ITEMS], feat[:, HYP_B1:HYP_B1 + 1], 0.0, ALU.add, ALU.max).then_inc(net_ready, 1)
                dve.wait_ge(net_done, 3)
                V.tensor_scalar(hy2, banks[0:SH, 7, 0:ITEMS], feat[:, HYP_B2:HYP_B2 + 1], None, ALU.add).then_inc(net_ready, 1)
                dve.wait_ge(net_done, 4)
                V.tensor_scalar(st1, banks[0:SH // 2, 6, 0:ITEMS], ab[:, 1:2], 0.0, ALU.add, ALU.max).then_inc(net_ready, 1)
                dve.wait_ge(net_done, 5)
                for c in range(DC):
                    V.tensor_scalar(style[:, c * ITEMS:(c + 1) * ITEMS], banks[:, 7, c * ITEMS:(c + 1) * ITEMS],
                                    feat[:, STY_B2 + c:STY_B2 + c + 1], None, ALU.add)
                for c in range(DC):
                    last = V.tensor_scalar(item_beta[:, c, :], banks[:, 7, (DC + c) * ITEMS:(DC + c + 1) * ITEMS],
                                           feat[:, STY_B2 + DC + c:STY_B2 + DC + c + 1], None, ALU.add)
                last.then_inc(net_ready, 1)
                dve.wait_ge(rows_cleared, 7)
                V.tensor_copy(token_field(h_rows[:], "p a t o -> p a (t o)"), first_tokens).then_inc(rows_numbered, 1)
                V.tensor_copy(pad_row[:, ROW_TOKEN:ROW_TOKEN + 2].bitcast(I32), spare_no).then_inc(rows_numbered, 1)
                dve.wait_ge(lnz_ready, 1)
                gam = item_gamma[:].rearrange("p c i -> p (c i)")
                link(V.scalar_tensor_tensor(gam, style, 0.0, lnz, ALU.max, ALU.add))
                link(V.tensor_scalar(gam, gam, 1e-8, None, ALU.add))

                def bn(src, stats, st_sem, mv, mv_sem, used, g):
                    wait(dve, used, g)
                    for t in range(GT):
                        last = V.bn_stats(stats[:, t, :], src[:, t, :])
                    last.then_inc(st_sem, 1)
                    wait_apart(dve, pool_consts, (st_sem, g + 1))
                    for t in range(GT):
                        last = V.bn_aggr(mv[:, t, :], stats[:, t, :])
                    last.then_inc(mv_sem, 1)

                def sum_moments(i):
                    dve.wait_ge(up_done, i.g + 1)
                    bn(ps_u, stats0, st0_ready, mv0, mv0_ready, rs0_ready, i.g)

                def adapter_norm(i):
                    dve.wait_ge(mv0_ready, i.g + 1)
                    wait(dve, x1_stored[i.par], i.half * 16)
                    wait(dve, n_ready, i.g - 1)
                    for t in range(GT):
                        last = V.scalar_tensor_tensor(rb[:, i.par, t, :], ps_u[:, t, :], mv0[:, t, 0:1], g0[:], ALU.subtract, ALU.mult)
                    last.then_inc(centred_ready, 1)
                    dve.wait_ge(centred_ready, i.g + 1)
                    dve.wait_ge(rs0_ready, i.g + 1)
                    for t in range(GT):
                        v = rb[:, i.par, t, :]
                        last = V.scalar_tensor_tensor(v, v, rs0[:, t:t + 1], b0[:], ALU.mult, ALU.add)
                    last.then_inc(x1_ready, 1)

                def x1_moments(i):
                    dve.wait_ge(x1_ready, i.g + 1)
                    bn(rb[:, i.par], stats1, st1_ready, mv1, mv1_ready, rs1_ready, i.g)

                def norm_shift(i):
                    dve.wait_ge(rs1_ready, i.g + 1)
                    wait(dve, n_ready, i.g)
                    V.scalar_tensor_tensor(shift1[:], mv1[:, :, 0], -1.0, rs1[:], ALU.mult, ALU.mult).then_inc(shift1_ready, 1)

                def item_norm_moments(i):
                    dve.wait_ge(hT_ready, i.g + 1)
                    for c in range(DC):
                        for b in range(GI):
                            last = V.bn_stats(statsT[:, c * GI + b, :], hT[:, c, b * T:(b + 1) * T])
                    last.then_inc(stT_ready, 1)
                    dve.wait_ge(stT_ready, i.g + 1)
                    V.tensor_tensor(msum[:], statsT[:, :, 1], statsT[:, :, 4], ALU.add)
                    V.tensor_tensor(mdiff[:], statsT[:, :, 1], statsT[:, :, 4], ALU.subtract)
                    V.tensor_tensor(var4[:], statsT[:, :, 2], statsT[:, :, 5], ALU.add).then_inc(item_step, 1)
                    dve.wait_ge(item_step, i.g * 3 + 1)
                    V.tensor_tensor(mdiff[:], mdiff[:], mdiff[:], ALU.mult).then_inc(item_step, 1)
                    dve.wait_ge(item_step, i.g * 3 + 2)
                    V.scalar_tensor_tensor(var4[:], var4[:], 4.0 / T, mdiff[:], ALU.mult, ALU.add).then_inc(item_step, 1)
                    dve.wait_ge(item_step, i.g * 3 + 3)
                    V.tensor_scalar(var4[:], var4[:], 0.25, 1e-8, ALU.mult, ALU.add).then_inc(var4_ready, 1)

                def item_norm_scale(i):
                    dve.wait_ge(rsT_ready, i.g + 1)
                    wait(dve, h_ready, i.g)
                    items = bass.ds(i.g * GI, GI)
                    flat_a = aff_a[:].rearrange("p c b -> p (c b)")
                    flat_c = aff_c[:].rearrange("p c b -> p (c b)")
                    V.tensor_tensor(aff_a[:], rsT[:].rearrange("p (c b) -> p c b", b=GI), item_gamma[:, :, items],
                                    ALU.mult).then_inc(aff_c_ready, 1)
                    dve.wait_ge(aff_c_ready, i.g * 3 + 1)
                    V.scalar_tensor_tensor(flat_c, msum[:], 0.5, flat_a, ALU.mult, ALU.mult).then_inc(aff_c_ready, 1)
                    dve.wait_ge(aff_c_ready, i.g * 3 + 2)
                    V.tensor_tensor(aff_c[:], item_beta[:, :, items], aff_c[:], ALU.subtract).then_inc(aff_c_ready, 1)
                    for c in range(1, DC):
                        v = hT[:, c, :].rearrange("p (b t) -> p b t", t=T)
                        V.tensor_tensor(v, v, bcast(aff_a[:, c, :], 2, [P, GI, T]), ALU.mult).then_inc(scaled_ready, 1)
                        dve.wait_ge(scaled_ready, i.g * (DC - 1) + c)
                        if c == 1:
                            dve.wait_ge(aff_c_ready, (i.g + 1) * 3)
                        last = V.tensor_tensor(v, v, bcast(aff_c[:, c, :], 2, [P, GI, T]), ALU.add)
                    last.then_inc(h_rest_ready, 1)

                def cut_low(i, some):
                    for q, slot in chunks(i)[some]:
                        dve.wait_ge(w_high_ready, q + 1)
                        w = bass.ds(q * CHUNK, CHUNK)
                        V.scalar_tensor_tensor(w_low[:, w], stage[:, slot], WSCALE, w_high[:, w], ALU.mult,
                                               ALU.subtract).then_inc(w_low_ready, 1)

                def choose(i):
                    wait_apart(dve, pool_consts, (logits_copied, i.g + 1))
                    for t in range(GT):
                        last = V.max(top[:, t, :], lg[:, t, :])
                    last.then_inc(top_ready, 1)
                    wait_apart(dve, pool_consts, (top_ready, i.g + 1))
                    for t in range(GT):
                        last = V.max_index(top_at[:, t, :], top[:, t, :], lg[:, t, :])
                    last.then_inc(top_at_ready, 1)
                    dve.wait_ge(top_at_ready, i.g + 1)
                    V.tensor_copy(choice[:], top_at[:, :, 0:2]).then_inc(choice_ready, 1)
                    dve.wait_ge(choice_ready, i.g + 1)
                    V.tensor_tensor(mask[:], bcast(expert_no[:].unsqueeze(1), 1, [P, GT, 2, EXPERTS]),
                                    bcast(choice[:], 3, [P, GT, 2, EXPERTS]), ALU.is_equal).then_inc(mask_ready, 1)
                    dve.wait_ge(mask_ready, i.g + 1)
                    V.tensor_tensor(chosen[:], mask[:, :, 0, :], mask[:, :, 1, :], ALU.add).then_inc(chosen_ready, 1)

                def low(i):
                    dve.wait_ge(high_ready, i.g + 1)
                    V.tensor_tensor(h_rows[:, i.par, :, D:2 * D], ps_h, h_rows[:, i.par, :, 0:D],
                                    ALU.subtract).then_inc(low_ready, 1)
                    field = h_rows[:, i.par]
                    V.tensor_tensor(float_field(field, ROW_DIFF), top[:, :, 1], top[:, :, 0], ALU.subtract)
                    V.tensor_copy(float_field(field, ROW_FIRST), choice[:, :, 0])
                    tok = token_field(field, "p t o -> p (t o)")
                    V.tensor_scalar(tok, tok, float(2 * GROUP), None, ALU.add)

                def place_rows(i):
                    dve.wait_ge(rank_done, i.g + 1)
                    V.tensor_tensor(place[:], ps_rank, bcast(queue_start[:], 1, [P, GT, EXPERTS]),
                                    ALU.add).then_inc(place_ready, 1)
                    V.tensor_tensor(chosen_sum[:], chosen_sum[:], chosen[:], ALU.add).then_inc(sum_ready, 1)
                    dve.wait_ge(place_ready, i.g + 1)
                    V.tensor_tensor(mask[:], mask[:], bcast(place[:], 2, [P, GT, 2, EXPERTS]),
                                    ALU.mult).then_inc(picked_ready, 1)
                    dve.wait_ge(picked_ready, i.g + 1)
                    V.tensor_reduce(slot_f[:], mask[:], AX, ALU.add).then_inc(slot_f_ready, 1)
                    dve.wait_ge(slot_f_ready, i.g + 1)
                    V.tensor_copy(slot[:, i.par], slot_f[:]).then_inc(slots_known, 1)

                def body(i):
                    s1, s2, s3 = back(i, 0), back(i, 1), back(i, 2)
                    if s2 is not None:
                        sum_moments(s2)
                    if s3 is not None:
                        item_norm_moments(s3)
                    if s2 is not None:
                        adapter_norm(s2)
                    if s3 is not None:
                        item_norm_scale(s3)
                    if s2 is not None:
                        x1_moments(s2)
                    if s1 is not None:
                        wait_apart(dve, pool_consts, (wnow_loaded[s1.par], (s1.half + 1) * 16))
                    cut_low(i, slice(0, 1))
                    if s2 is not None:
                        norm_shift(s2)
                    cut_low(i, slice(1, 2))
                    if s3 is not None:
                        choose(s3)
                    cut_low(i, slice(2, 3))
                    if s3 is not None:
                        low(s3)
                    cut_low(i, slice(3, 4))
                    if s3 is not None:
                        place_rows(s3)

                iterations(dve, body)

                GRID = [P, TILES, EXPERTS]
                count, ntiles, tile_end, tile_first, offset = (per_expert(k) for k in range(5))
                dve.wait_ge(counted, 1)
                for par in range(2):
                    dve.wait_ge(x1_stored[par], GROUPS // 2 * 16)
                dve.wait_ge(nT_done, GROUPS)
                V.tensor_copy(counts[:], banks[0:1, 6, 0:EXPERTS]).then_inc(counts_known, 1)
                link(V.tensor_copy(count, banks[:, 6, 0:EXPERTS]))
                over_e = over.rearrange("p (e k) -> p e k", e=EXPERTS)
                OVER = [P, EXPERTS, TOKENS // SLOTS]
                link(V.tensor_tensor(over_e, bcast(count, 2, OVER), bcast(tile_start[:], 1, OVER), ALU.is_gt))
                link(V.tensor_reduce(ntiles, over_e, AX, ALU.add))
                link(V.tensor_tensor_scan(tile_end, ntiles, zeros[:], 0.0, ALU.add, ALU.add))
                link(V.tensor_tensor(tile_first, tile_end, ntiles, ALU.subtract))
                link(V.tensor_tensor(grid(0), bcast(tile_no[:], 2, GRID), bcast(tile_first, 1, GRID), ALU.is_ge))
                link(V.tensor_reduce(line(0), grid(0), AX, ALU.add))
                link(V.tensor_scalar(tile_expert_f[:], line(0), -1.0, None, ALU.add))
                V.tensor_copy(tile_expert[:], tile_expert_f[0:1])
                link(V.scalar_tensor_tensor(offset, tile_first, -float(SLOTS), queue_start[:], ALU.mult, ALU.add))
                link(V.tensor_tensor(grid(1), bcast(tile_expert_f[:], 2, GRID), bcast(expert_no[:], 1, GRID), ALU.is_equal))
                link(V.tensor_tensor(grid(1), grid(1), bcast(offset, 1, GRID), ALU.mult))
                link(V.tensor_reduce(line(0), grid(1), AX, ALU.add))
                link(V.scalar_tensor_tensor(line(0), tile_no[:], float(SLOTS), line(0), ALU.mult, ALU.add))
                link(V.tensor_scalar(line(1), tile_no[:], tile_end[:, EXPERTS - 1:EXPERTS], None, ALU.is_lt))
                link(V.scalar_tensor_tensor(line(0), line(0), -float(IDLE), line(1), ALU.add, ALU.mult))
                V.tensor_scalar(tile_row[:], line(0)[0:1], float(IDLE), None, ALU.add)


def experts(nc, sem, env):
    queues, out, exp_b2 = env["queues"], env["out"], env["exp_b2"]
    w_high, w_low, feat, ident16, tile_expert, tile_row, tile_expert_f, banks = (
        env[n] for n in ("w_high", "w_low", "feat", "ident16", "tile_expert", "tile_row",
                         "tile_expert_f", "banks"))

    with ExitStack() as ctx:
        def sb(name, shape, dt=F32):
            return ctx.enter_context(nc.sbuf_tensor(name, shape, dt))

        b2 = sb("b2", [P, EXPERTS * D])
        rows = sb("rows", [P, 2, SUB, ROW], F16)
        rT = sb("rT", [P, 2, 2, DC, SLOTS], F16)
        hid = sb("hid", [P, FC, SLOTS])
        hid_high = sb("hid_high", [P, 2, FC, SLOTS], F16)
        hid_low = sb("hid_low", [P, 2, FC, SLOTS], F16)
        yb = sb("yb", [P, SUB, D])
        yg = sb("yg", [P, 2, SUB, D])
        token = sb("token", [P, 2, SUB], U32)
        gate = sb("gate", [P, 2, SUB])
        ratio = sb("ratio", [P, SUB])
        norm = sb("norm", [P, SUB])
        second = sb("second", [P, SUB])
        is_first = sb("is_first", [P, SUB])

        b2_loaded = sem("b2_loaded")
        rows_loaded = [sem("rows_loaded0"), sem("rows_loaded1")]
        rT_done, rT_ready, in_done, hid_ready, split_high, split_low, out_done, y_ready = (
            sem(n) for n in ("rT_done", "rT_ready", "in_done", "hid_ready", "split_high", "split_low",
                             "out_done", "y_ready"))
        ratio_ready, meta_taken, gate_step, norm_ready, gate_ready, gated, added = (
            sem(n) for n in ("ratio_ready", "meta_taken", "gate_step", "norm_ready", "gate_ready",
                             "gated", "added"))

        PAIRS = FC // 2

        def ps_in(c):
            return banks[:, c // 2, (c % 2) * SLOTS:(c % 2 + 1) * SLOTS]

        def ps_rT(par):
            return banks[:, 4 + par, :].bitcast(F16)

        def ps_out(par):
            return banks[:, 6 + par, :].rearrange("p (s d) -> p s d", d=D)

        def part_of(par, s, k, c):
            return rows[:, par, s, k * D + c * P:k * D + (c + 1) * P]

        def field(par, place, dt):
            return rows[:, par, :, place:place + 2].bitcast(dt).rearrange("p s o -> p (s o)")

        def expert_of(eng, i):
            return eng.value_load(tile_expert[0:1, bass.ds(i.g, 1)], min_val=0, max_val=EXPERTS - 1)

        with nc.Block() as block:

            @block.sync
            def _(sp):
                sp.dma_start(b2[:], spread(exp_b2, P)).then_inc(b2_loaded, 16)

                def load(i):
                    row = sp.value_load(tile_row[0:1, bass.ds(i.g, 1)], min_val=0, max_val=IDLE)
                    wait(sp, rT_done, i.g - 1)
                    wait(sp, meta_taken, i.g - 1)
                    sp.dma_start(rows[:, i.par].bitcast(U32), queues[bass.ds(row, SLOTS)].rearrange("(s p) d -> p s d", p=P)
                                 ).then_inc(rows_loaded[i.par], 16)

                load(At(0, 0))
                load(At(0, 1))
                with sp.Fori(1, TILES // 2) as h:
                    load(At(h, 0))
                    load(At(h, 1))
                load(At(TILES // 2, 0))

            @block.gpsimd
            def _(pool):
                def add_rows(i):
                    for s in range(SUB):
                        wait_apart(pool, b2_loaded, (gated, i.g * SUB + s + 1), (added, (i.g * SUB + s) * 16))
                        nc.gpsimd.indirect_dma_start(
                            out=out, out_offset=bass.IndirectOffsetOnAxis(ap=token[:, i.par, s:s + 1], axis=0),
                            in_=yg[:, i.par, s, :], in_offset=None, compute_op=ALU.add).then_inc(added, 16)

                add_rows(At(0, 0))
                add_rows(At(0, 1))
                with pool.Fori(1, TILES // 2) as h:
                    add_rows(At(h, 0))
                    add_rows(At(h, 1))
                add_rows(At(TILES // 2, 0))
                pool.wait_ge(added, TILES * SUB * 16)

            @block.tensor
            def _(pe):
                def transpose_rows(i):
                    pe.wait_ge(rows_loaded[i.par], (i.half + 1) * 16)
                    wait(pe, rT_ready, i.g - 1)
                    for k in range(2):
                        for c in range(DC):
                            for s in range(SUB):
                                at = (k * DC + c) * SLOTS + s * P
                                last = nc.tensor.transpose(ps_rT(i.par)[:, at:at + P],
                                                           part_of(i.par, s, k, c), ident16[:])
                    last.then_inc(rT_done, 1)

                def layer_in(i):
                    e = expert_of(pe, i)
                    pe.wait_ge(rT_ready, i.g + 1)
                    for c in range(FC):
                        if c % 2 == 0:
                            wait(pe, hid_ready, (i.g - 1) * PAIRS + c // 2 + 1)
                        n = 0
                        for k in range(DC):
                            at = bass.ds(e * (DC * FF) + (k * FF + c * P), P)
                            for w, v in ((w_high, 0), (w_high, 1), (w_low, 0)):
                                last = nc.tensor.matmul(ps_in(c), w[:, at], rT[:, i.par, v, k, :],
                                                        start=(n == 0), stop=(n == 3 * DC - 1))
                                n += 1
                        if c % 2 == 1:
                            last.then_inc(in_done, 1)

                def layer_out(i):
                    e = expert_of(pe, i)
                    wait(pe, y_ready, i.g - 1)
                    for s in range(SUB):
                        n = 0
                        for c in range(FC):
                            if s == 0 and c % 2 == 0:
                                pe.wait_ge(split_low, i.g * PAIRS + c // 2 + 1)
                            at = bass.ds(e * (FC * D) + (W2_AT + c * D), D)
                            for w, v in ((w_high, hid_high), (w_high, hid_low), (w_low, hid_high)):
                                last = nc.tensor.matmul(ps_out(i.par)[:, s, :], v[:, i.par, c, s * P:(s + 1) * P],
                                                        w[:, at], start=(n == 0), stop=(n == 3 * FC - 1))
                                n += 1
                    last.then_inc(out_done, 1)

                transpose_rows(At(0, 0))
                layer_in(At(0, 0))
                transpose_rows(At(0, 1))
                layer_in(At(0, 1))
                transpose_rows(At(1, 0))
                layer_out(At(0, 0))
                with pe.Fori(1, TILES // 2) as h:
                    for c in (0, 1):
                        layer_in(At(h, c))
                        transpose_rows(At(h, c + 1))
                        layer_out(At(h, c - 1))
                layer_in(At(TILES // 2, 0))
                layer_out(At(TILES // 2, -1))
                layer_out(At(TILES // 2, 0))

            @block.scalar
            def _(sc):
                def bias_relu(i):
                    e = expert_of(sc, i)
                    for c in range(FC):
                        if c % 2 == 0:
                            sc.wait_ge(in_done, i.g * PAIRS + c // 2 + 1)
                            wait(sc, split_low, (i.g - 1) * PAIRS + c // 2 + 1)
                        last = nc.scalar.activation(hid[:, c, :], ps_in(c), ACT.Relu,
                                                    scale=1.0 / WSCALE, bias=feat[:, bass.ds(e * FC + (B1 + c), 1)])
                        if c % 2 == 1:
                            last.then_inc(hid_ready, 1)

                def choice_ratio(i):
                    sc.wait_ge(rows_loaded[i.par], (i.half + 1) * 16)
                    wait(sc, gate_ready, i.g)
                    nc.scalar.activation(ratio[:], field(i.par, ROW_DIFF, F32), ACT.Exp).then_inc(ratio_ready, 1)

                def times_gate(i):
                    sc.wait_ge(y_ready, i.g + 1)
                    sc.wait_ge(gate_ready, i.g + 1)
                    wait(sc, added, (i.g - 1) * SUB * 16)
                    for s in range(SUB):
                        nc.scalar.activation(yg[:, i.par, s, :], yb[:, s, :], ACT.Copy,
                                             scale=gate[:, i.par, s:s + 1]).then_inc(gated, 1)

                bias_relu(At(0, 0))
                choice_ratio(At(0, 0))
                bias_relu(At(0, 1))
                choice_ratio(At(0, 1))
                times_gate(At(0, 0))
                with sc.Fori(1, TILES // 2) as h:
                    for c in (0, 1):
                        bias_relu(At(h, c))
                        choice_ratio(At(h, c))
                        times_gate(At(h, c - 1))
                bias_relu(At(TILES // 2, 0))
                choice_ratio(At(TILES // 2, 0))
                times_gate(At(TILES // 2, -1))
                times_gate(At(TILES // 2, 0))

            @block.vector
            def _(dve):
                V = nc.vector

                def rows_out(i):
                    dve.wait_ge(rT_done, i.g + 1)
                    wait(dve, in_done, (i.g - 1) * PAIRS)
                    V.tensor_copy(rT[:, i.par].rearrange("p k c s -> p (k c s)"), ps_rT(i.par)).then_inc(rT_ready, 1)

                def split(i, pair):
                    n = i.g * PAIRS + pair + 1
                    dve.wait_ge(hid_ready, n)
                    wait(dve, out_done, i.g - 1)
                    s = slice(pair * 2, pair * 2 + 2)
                    V.tensor_copy(hid_high[:, i.par, s, :], hid[:, s, :]).then_inc(split_high, 1)
                    dve.wait_ge(split_high, n)
                    V.tensor_tensor(hid_low[:, i.par, s, :], hid[:, s, :], hid_high[:, i.par, s, :],
                                    ALU.subtract).then_inc(split_low, 1)

                def gates(i):
                    dve.wait_ge(ratio_ready, i.g + 1)
                    wait(dve, added, (i.g - 1) * SUB * 16)
                    V.tensor_copy(token[:, i.par, :], field(i.par, ROW_TOKEN, U32))
                    V.tensor_scalar(is_first[:], field(i.par, ROW_FIRST, F32), tile_expert_f[:, bass.ds(i.g, 1)], None,
                                    ALU.is_equal).then_inc(meta_taken, 1)
                    V.tensor_scalar(norm[:], ratio[:], 1.0, None, ALU.add).then_inc(gate_step, 1)
                    dve.wait_ge(gate_step, i.g * 4 + 1)
                    V.reciprocal(norm[:], norm[:]).then_inc(gate_step, 1)
                    dve.wait_ge(gate_step, i.g * 4 + 2)
                    V.tensor_tensor(second[:], norm[:], ratio[:], ALU.mult).then_inc(gate_step, 1)
                    dve.wait_ge(gate_step, i.g * 4 + 3)
                    V.tensor_tensor(norm[:], norm[:], second[:], ALU.subtract).then_inc(gate_step, 1)
                    dve.wait_ge(gate_step, i.g * 4 + 4)
                    dve.wait_ge(meta_taken, i.g + 1)
                    V.tensor_tensor(norm[:], norm[:], is_first[:], ALU.mult).then_inc(norm_ready, 1)
                    dve.wait_ge(norm_ready, i.g + 1)
                    V.tensor_tensor(gate[:, i.par, :], norm[:], second[:], ALU.add).then_inc(gate_ready, 1)

                def add_bias(i):
                    e = expert_of(dve, i)
                    dve.wait_ge(out_done, i.g + 1)
                    wait(dve, gated, i.g * SUB)
                    for s in range(SUB):
                        last = V.scalar_tensor_tensor(yb[:, s, :], ps_out(i.par)[:, s, :], 1.0 / WSCALE,
                                                      b2[:, bass.ds(e * D, D)], ALU.mult, ALU.add)
                    last.then_inc(y_ready, 1)

                def splits(i):
                    for pair in range(PAIRS):
                        split(i, pair)

                dve.wait_ge(b2_loaded, 16)
                rows_out(At(0, 0))
                splits(At(0, 0))
                gates(At(0, 0))
                rows_out(At(0, 1))
                splits(At(0, 1))
                rows_out(At(1, 0))
                add_bias(At(0, 0))
                gates(At(0, 1))
                with dve.Fori(1, TILES // 2) as h:
                    for c in (0, 1):
                        splits(At(h, c))
                        rows_out(At(h, c + 1))
                        add_bias(At(h, c - 1))
                        gates(At(h, c))
                splits(At(TILES // 2, 0))
                add_bias(At(TILES // 2, -1))
                gates(At(TILES // 2, 0))
                add_bias(At(TILES // 2, 0))


def kernel(**inputs):
    import numpy as np
    import concourse.bacc as bacc
    from concourse.bass_utils import run_bass_kernel_spmd

    v = {name: np.asarray(a) for name, a in inputs.items()}
    adapter = {name[len("L0_cond_"):]: a for name, a in v.items() if name.startswith("L0_cond_")}
    moe = {name[len("L1_cond_"):]: a for name, a in v.items() if name.startswith("L1_cond_")}

    def columns(a):
        return a.reshape(-1, P).T

    w1 = moe["exp_w1"].reshape(EXPERTS, DC, P, FF).reshape(EXPERTS * DC, P, FF)
    w2 = moe["exp_w2"].reshape(EXPERTS, FC, P, D).transpose(0, 2, 1, 3).reshape(EXPERTS, P, DC, CHUNK)
    w2 = w2.transpose(0, 2, 1, 3).reshape(EXPERTS * DC, P, CHUNK)
    arrays = {
        "x": v["x"].reshape(TOKENS, D),
        "ids": v["itok_B_0_15"].reshape(1, ITEMS),
        "subject_ids": v["itok_B_6_14"].reshape(1, ITEMS),
        "down_w": adapter["down_W"].T.reshape(DC, P, A).transpose(1, 0, 2),
        "down_b": adapter["down_b"].reshape(A, 1),
        "up_w": adapter["up_W"].T,
        "up_b": adapter["up_b"].reshape(1, D),
        "adapter_w": adapter["expert_W"].reshape(ADAPTERS, A * A),
        "adapter_b": adapter["expert_b"],
        "domain_emb": adapter["domain_emb"],
        "gamma0": adapter["ln_gamma"].reshape(1, D),
        "beta0": adapter["ln_beta"].reshape(1, D),
        "subj_emb": moe["subj_emb"],
        "hyp_w1": moe["hyp_w1"],
        "hyp_w2": moe["hyp_w2"],
        "sty_w1": moe["sty_w1"],
        "sty_b1": moe["sty_b1"].reshape(SH // 2, 1),
        "sty_w2": moe["sty_w2"],
        "feature": np.concatenate([columns(moe[n]) for n in
                                   ("ln_g", "ln_b", "hyp_b1", "hyp_b2", "sty_b2", "exp_b1")], axis=1),
        "router_w": moe["router_w"].reshape(DC, P, EXPERTS).transpose(1, 0, 2),
        "expert_w": np.concatenate([w1, w2], axis=0),
        "exp_b2": moe["exp_b2"].reshape(1, EXPERTS * D),
    }
    arrays = {name: np.ascontiguousarray(a) for name, a in arrays.items()}

    nc = bacc.Bacc("TRN2", target_bir_lowering=False, num_devices=1)
    args = {name: nc.dram_tensor(name, a.shape, mybir.dt.from_np(a.dtype), kind="ExternalInput").ap()
            for name, a in arrays.items()}
    out = nc.dram_tensor("out", (TOKENS + P, D), F32, kind="ExternalOutput").ap()
    build(nc, **args, out=out)
    result = run_bass_kernel_spmd(nc, [arrays], core_ids=[0])
    return result.results[0]["out"][:TOKENS].reshape(ITEMS, T, D)
```

```python
from contextlib import ExitStack

import concourse.bass as bass
from concourse import mybir

F32 = mybir.dt.float32
F16 = mybir.dt.float16
I32 = mybir.dt.int32
U32 = mybir.dt.uint32
ALU = mybir.AluOpType
ACT = mybir.ActivationFunctionType
AX = mybir.AxisListType.X

P = 128
ITEMS, T, D = 64, 64, 256
A, ADAPTERS = 64, 16
SUBJECTS, SE, SH = 32, 64, 128
EXPERTS, FF = 8, 1024
TOKENS = ITEMS * T
DC = D // P
FC = FF // P
GROUP = 512
GROUPS = TOKENS // GROUP
GT = GROUP // P
GI = GROUP // T
SUB = 2
SLOTS = SUB * P
TILES = (2 * TOKENS + EXPERTS * (SLOTS - 1)) // SLOTS
QUEUE = TOKENS + SLOTS
IDLE = EXPERTS * QUEUE
NONE_ROW = ADAPTERS
CHUNK = 1024
CHUNKS = 2 * EXPERTS * DC * FF // CHUNK
CUTS = [4, 4, 4, 4, 2, 2, 2, 2, 4, 4]
assert sum(CUTS) == CHUNKS and len(CUTS) == GROUPS + 2
W2_AT = EXPERTS * DC * FF
LOOP_FROM = 2
STAGES = 4
WSCALE = 256.0

ROW_TOKEN, ROW_DIFF, ROW_FIRST, ROW = 2 * D, 2 * D + 2, 2 * D + 4, 2 * D + 8

LN_G, LN_B, HYP_B1, HYP_B2, STY_B2, B1 = 0, DC, 2 * DC, 2 * DC + 1, 2 * DC + 2, 4 * DC + 2
FEATURE_COLS = B1 + EXPERTS * FC


class At:

    def __init__(self, h, c=0):
        self.g = h * 2 + c
        self.par = c % 2
        self.half = h + c // 2


def wait(eng, sem, value):
    if not isinstance(value, int) or value > 0:
        eng.wait_ge(sem, value)


def wait_apart(eng, held, *waits):
    waits = [(sem, value if isinstance(value, int) else eng.to_reg(value)) for sem, value in waits]
    if not isinstance(waits[0][1], int):
        eng.wait_ge(held, 1)
    for sem, value in waits:
        wait(eng, sem, value)


def upto(g, n, most):
    return min(g + n, most) if isinstance(g, int) else g + n


def bcast(ap, axis, shape):
    return ap.unsqueeze(axis).broadcast_to(shape)


def spread(ap, partitions):
    return ap.partition_broadcast(partitions).rearrange("q o n -> q (o n)")


def build(nc, x, ids, subject_ids, down_w, down_b, up_w, up_b, adapter_w, adapter_b, domain_emb,
          gamma0, beta0, subj_emb, hyp_w1, hyp_w2, sty_w1, sty_b1, sty_w2, feature, router_w,
          expert_w, exp_b2, out):
    x_rows = x.rearrange("(g t p) d -> g p t d", t=GT, p=P)
    out_rows = out[0:TOKENS].rearrange("(g t p) d -> g p t d", t=GT, p=P)
    spare_rows = out[TOKENS:TOKENS + P]

    queues = nc.dram_tensor("queues", (IDLE + SLOTS, ROW // 2), U32, kind="Internal").ap()

    with ExitStack() as whole:
        def sem(name):
            return whole.enter_context(nc.semaphore(name))

        def keep(name, shape, dt):
            return whole.enter_context(nc.sbuf_tensor(name, shape, dt))

        w_high = keep("w_high", [P, CHUNKS * CHUNK], F16)
        w_low = keep("w_low", [P, CHUNKS * CHUNK], F16)
        feat = keep("feat", [P, FEATURE_COLS], F32)
        ident16 = keep("ident16", [P, P], F16)
        tile_expert = keep("tile_expert", [1, TILES], I32)
        tile_row = keep("tile_row", [1, TILES], I32)
        tile_expert_f = keep("tile_expert_f", [P, TILES], F32)
        banks = whole.enter_context(nc.psum_tensor("banks", [P, 8, 512], F32))

        dense(nc, sem, locals())
        experts(nc, sem, locals())


def dense(nc, sem, env):
    (x_rows, ids, subject_ids, down_w, down_b, up_w, up_b, adapter_w, adapter_b, domain_emb, gamma0,
     beta0, subj_emb, hyp_w1, hyp_w2, sty_w1, sty_b1, sty_w2, feature, router_w, expert_w, out_rows,
     spare_rows, queues) = (env[n] for n in (
         "x_rows", "ids", "subject_ids", "down_w", "down_b", "up_w", "up_b", "adapter_w",
         "adapter_b", "domain_emb", "gamma0", "beta0", "subj_emb", "hyp_w1", "hyp_w2", "sty_w1",
         "sty_b1", "sty_w2", "feature", "router_w", "expert_w", "out_rows", "spare_rows", "queues"))
    w_high, w_low, feat, ident16, tile_expert, tile_row, tile_expert_f, banks = (
        env[n] for n in ("w_high", "w_low", "feat", "ident16", "tile_expert", "tile_row",
                         "tile_expert_f", "banks"))

    with ExitStack() as ctx:
        def sb(name, shape, dt=F32):
            return ctx.enter_context(nc.sbuf_tensor(name, shape, dt))

        ident = sb("ident", [P, P])
        minus_half = sb("minus_half", [P, GI * DC])
        part_no = sb("part_no", [P, 1])
        expert_no = sb("expert_no", [P, EXPERTS])
        queue_start = sb("queue_start", [P, EXPERTS])
        earlier16 = sb("earlier16", [P, P], F16)
        ones16 = sb("ones16", [P, P], F16)
        dw = sb("dw", [P, DC, A])
        ab = sb("ab", [A, 2])
        uw = sb("uw", [A + 1, D])
        g0 = sb("g0", [P, D])
        b0 = sb("b0", [P, D])
        rw = sb("rw", [P, DC, EXPERTS])
        item_gamma = sb("item_gamma", [P, DC, ITEMS])
        item_beta = sb("item_beta", [P, DC, ITEMS])
        item_add = sb("item_add", [P, A])

        h_rows = sb("h_rows", [P, 2, GT, ROW], F16)
        stage = sb("stage", [P, STAGES, CHUNK])
        xb = sb("xb", [P, 2, GT, D])
        rb = sb("rb", [P, 2, GT, D])
        nb = sb("nb", [P, GT, D])
        xT = sb("xT", [P, DC, GROUP])
        hT = sb("hT", [P, DC, GROUP])
        act = sb("act", [A, GROUP])
        dom = sb("dom", [A + 1, GROUP])
        wnow = sb("wnow", [A, 2, GI * A])
        stats0 = sb("stats0", [P, GT, 6])
        mv0 = sb("mv0", [P, GT, 2])
        rs0 = sb("rs0", [P, GT])
        stats1 = sb("stats1", [P, GT, 6])
        mv1 = sb("mv1", [P, GT, 2])
        rs1 = sb("rs1", [P, GT])
        shift1 = sb("shift1", [P, GT])
        statsT = sb("statsT", [P, DC * GI, 6])
        msum = sb("msum", [P, DC * GI])
        mdiff = sb("mdiff", [P, DC * GI])
        var4 = sb("var4", [P, DC * GI])
        rsT = sb("rsT", [P, DC * GI])
        aff_a = sb("aff_a", [P, DC, GI])
        aff_c = sb("aff_c", [P, DC, GI])

        pad_row = sb("pad_row", [P, ROW], F16)
        tile_no = sb("tile_no", [P, TILES])
        tile_start = sb("tile_start", [P, TOKENS // SLOTS])
        zeros = sb("zeros", [P, EXPERTS])
        counts = sb("counts", [1, EXPERTS], I32)
        lg = sb("lg", [P, GT, EXPERTS])
        top = sb("top", [P, GT, 8])
        top_at = sb("top_at", [P, GT, 8], U32)
        choice = sb("choice", [P, GT, 2])
        mask = sb("mask", [P, GT, 2, EXPERTS])
        chosen = sb("chosen", [P, GT, EXPERTS], F16)
        chosen_sum = sb("chosen_sum", [P, GT, EXPERTS], F16)
        place = sb("place", [P, GT, EXPERTS])
        slot_f = sb("slot_f", [P, GT, 2])
        slot = sb("slot", [P, 2, GT, 2], U32)

        table = w_low[0:NONE_ROW + 1, 16 * CHUNK:24 * CHUNK].bitcast(F32)
        wsel = w_low[0:A, 24 * CHUNK:32 * CHUNK].bitcast(F32)
        wsel_pairs = wsel.rearrange("a (i q w) -> a w q i", q=A // 2, w=2)
        scratch = w_high[:, 24 * CHUNK:32 * CHUNK].bitcast(F32)
        at = [0]

        def scr(rows, cols):
            at[0] += cols
            return scratch[0:rows, at[0] - cols:at[0]]

        idf = scr(NONE_ROW + 1, ITEMS)
        sidf = scr(SUBJECTS, ITEMS)
        idc = scr(NONE_ROW + 1, ITEMS)
        hot_w = scr(NONE_ROW + 1, ITEMS)
        hot_e = scr(ADAPTERS, ITEMS)
        hot_s = scr(SUBJECTS, ITEMS)
        t_ab = scr(ADAPTERS, A)
        t_de = scr(ADAPTERS, A)
        t_se = scr(SUBJECTS, SE)
        hw1 = scr(SE, SH)
        hw2 = scr(SH, SH)
        sw1 = scr(SH, SH // 2)
        sw2 = scr(SH // 2, 2 * D)
        se_sb = scr(SE, ITEMS)
        hy1 = scr(SH, ITEMS)
        hy2 = scr(SH, ITEMS)
        st1 = scr(SH // 2, ITEMS)
        style = scr(P, DC * ITEMS)
        absz = scr(P, DC * ITEMS)
        expz = scr(P, DC * ITEMS)
        lnz = scr(P, DC * ITEMS)
        ids_i = scr(NONE_ROW + 1, ITEMS).bitcast(I32)
        sids_i = scr(SUBJECTS, ITEMS).bitcast(I32)

        zero_out = hT[:, 0, 0:D]
        earlier = hT[:, 1, 0:P]
        first_tokens = hT[:, 1, P:P + 2 * GT].rearrange("p (a t) -> p a t", t=GT)
        spare_no = hT[:, 1, P + 2 * GT:P + 2 * GT + 1]

        G = TILES * EXPERTS
        assert 3 * G + 2 * TILES + 8 * 16 + TOKENS // SLOTS * EXPERTS <= 2 * GT * D
        tabs = rb[:, :, :, :].rearrange("p a t d -> p (a t d)")

        def grid(k):
            return tabs[:, k * G:(k + 1) * G].rearrange("p (i e) -> p i e", e=EXPERTS)

        def line(k):
            return tabs[:, 3 * G + k * TILES:3 * G + (k + 1) * TILES]

        def per_expert(k):
            at = 3 * G + 2 * TILES + k * EXPERTS
            return tabs[:, at:at + EXPERTS]

        over = tabs[:, 3 * G + 2 * TILES + 8 * 16:3 * G + 2 * TILES + 8 * 16 + TOKENS // SLOTS * EXPERTS]
        def float_field(rows, at):
            return rows[:, :, at:at + 2].bitcast(F32).rearrange("p t o -> p (t o)")

        def token_field(rows, flat):
            field = rows[:, :, ROW_TOKEN:ROW_TOKEN + 2] if len(rows.shape) == 3 else rows[:, :, :, ROW_TOKEN:ROW_TOKEN + 2]
            return field.bitcast(I32).rearrange(flat)

        ps_x = banks[:, 0:2, :]
        ps_u = banks[:, 2:4, :].rearrange("p a b -> p (a b)").rearrange("p (t d) -> p t d", d=D)
        ps_h = banks[:, 4:6, :].rearrange("p a b -> p (a b)").rearrange("p (t d) -> p t d", d=D)
        ps_down = banks[0:A, 6, :]
        ps_lg = banks[:, 6, 0:GT * EXPERTS].rearrange("p (t e) -> p t e", e=EXPERTS)
        ps_dom = banks[0:A, 7, :]
        ps_rank = banks[:, 7, 0:GT * EXPERTS].rearrange("p (t e) -> p t e", e=EXPERTS)

        ids_loaded, table_loaded = sem("ids_loaded"), sem("table_loaded")
        early_loaded, late_loaded = sem("early_loaded"), sem("late_loaded")
        pool_consts, cleared_zero = sem("pool_consts"), sem("cleared_zero")
        rows_cleared, rows_numbered, filled = sem("rows_cleared"), sem("rows_numbered"), sem("filled")
        ids_float, hot_ready, select_done, select_copied = (
            sem("ids_float"), sem("hot_ready"), sem("select_done"), sem("select_copied"))
        net_done, net_ready, style_step, lnz_ready = (
            sem("net_done"), sem("net_ready"), sem("style_step"), sem("lnz_ready"))
        dom_row, spare_stored = sem("dom_row"), sem("spare_stored")
        x_loaded = [sem("x_loaded0"), sem("x_loaded1")]
        wnow_loaded = [sem("wnow_loaded0"), sem("wnow_loaded1")]
        x1_stored = [sem("x1_stored0"), sem("x1_stored1")]
        stage_loaded = [sem(f"stage_loaded{s}") for s in range(STAGES)]
        (xT_done, xT_ready, down_done, act_ready, adapt_done, dom_ready, up_done, st0_ready,
         mv0_ready, ve0_ready, rs0_ready, centred_ready, x1_ready, st1_ready, mv1_ready, ve1_ready,
         rs1_ready, shift1_ready, n_ready, nT_done, hT_ready) = (sem(n) for n in (
             "xT_done", "xT_ready", "down_done", "act_ready", "adapt_done", "dom_ready", "up_done",
             "st0_ready", "mv0_ready", "ve0_ready", "rs0_ready", "centred_ready",
             "x1_ready", "st1_ready", "mv1_ready", "ve1_ready", "rs1_ready", "shift1_ready",
             "n_ready", "nT_done", "hT_ready"))
        (stT_ready, item_step, var4_ready, rsT_ready, scaled_ready, h_ready, h_rest_ready, logits_done,
         logits_copied, back_done, high_ready, low_ready) = (sem(n) for n in (
             "stT_ready", "item_step", "var4_ready", "rsT_ready", "scaled_ready",
             "h_ready", "h_rest_ready", "logits_done", "logits_copied", "back_done", "high_ready", "low_ready"))
        aff_ready = [sem("aff_ready0"), sem("aff_ready1")]
        w_high_ready, w_low_ready = sem("w_high_ready"), sem("w_low_ready")
        (top_ready, top_at_ready, choice_ready, mask_ready, chosen_ready, rank_done, sum_ready,
         place_ready, picked_ready, slot_f_ready, slots_known) = (sem(n) for n in (
             "top_ready", "top_at_ready", "choice_ready", "mask_ready", "chosen_ready", "rank_done",
             "sum_ready", "place_ready", "picked_ready", "slot_f_ready", "slots_known"))
        scattered = [sem("scattered0"), sem("scattered1")]
        counted, counts_known, table_step = sem("counted"), sem("counts_known"), sem("table_step")
        N_EARLY, N_LATE = 8, 8
        N_POOL = 13
        SELECTS = A // 16

        def iterations(eng, body, first=LOOP_FROM, until=GROUPS // 2, after={}):
            for i in range(2 * first):
                body(At(i // 2, i % 2))
                if i in after:
                    after[i]()
            with eng.Fori(first, until) as h:
                body(At(h, 0))
                body(At(h, 1))
            for i in range(2 * until, GROUPS + 2):
                body(At(i // 2, i % 2))

        def back(i, n):
            if isinstance(i.g, int):
                g = i.g - n
                return At(g // 2, g % 2) if 0 <= g < GROUPS else None
            return At(i.half, i.par - n)

        def chunks(i):
            if isinstance(i.g, int):
                start = sum(CUTS[:i.g])
                return [(q, q % STAGES, q // STAGES) for q in range(start, start + CUTS[i.g])]
            start = sum(CUTS[:2 * LOOP_FROM]) + CUTS[2 * LOOP_FROM] * i.par
            return [((i.half - LOOP_FROM) * STAGES + q, q % STAGES, i.half - LOOP_FROM + q // STAGES)
                    for q in range(start, start + CUTS[2 * LOOP_FROM])]

        def fill_queues(eng, first):
            with eng.Fori(first * EXPERTS // 2, (first + 1) * EXPERTS // 2) as e:
                count = eng.value_load(counts[0:1, bass.ds(e, 1)], min_val=0, max_val=TOKENS)
                eng.dma_start(queues[bass.ds(e * QUEUE + count, SLOTS)].rearrange("(s p) d -> p s d", p=P),
                              bcast(pad_row[:].bitcast(U32), 1, [P, SUB, ROW // 2])).then_inc(filled, 16)

        with nc.Block() as block:

            @block.sync
            def _(sp):
                def of(rows, g):
                    return rows[g] if isinstance(g, int) else rows[bass.ds(g, 1)].rearrange("o p t d -> (o p) t d")

                def load_x(i):
                    sp.dma_start(xb[:, i.par], of(x_rows, i.g)).then_inc(x_loaded[i.par], 16)

                def load_adapters(i):
                    wait(sp, adapt_done, i.g - 1)
                    sp.dma_start(wnow[:, i.par], wsel[:, bass.ds(i.g * GI * A, GI * A)]).then_inc(wnow_loaded[i.par], 16)

                def load_weights(i, some=slice(None)):
                    for q, slot, turn in chunks(i)[some]:
                        wait(sp, w_low_ready, q - STAGES + 1)
                        src = expert_w[q] if isinstance(q, int) else expert_w[bass.ds(q, 1)].rearrange("o p c -> (o p) c")
                        sp.dma_start(stage[:, slot], src).then_inc(stage_loaded[slot], 16)

                sp.dma_start(ids_i, spread(ids, NONE_ROW + 1)).then_inc(ids_loaded, 16)
                sp.dma_start(sids_i, spread(subject_ids, SUBJECTS)).then_inc(ids_loaded, 16)
                sp.dma_start(table, adapter_w).then_inc(table_loaded, 16)
                load_x(At(0, 0))
                for dst, src in ((dw[:], down_w), (ab[:, 0:1], down_b), (ab[:, 1:2], sty_b1), (t_ab, adapter_b),
                                 (t_de, domain_emb), (t_se, subj_emb), (uw[0:A], up_w), (uw[A:A + 1], up_b)):
                    sp.dma_start(dst, src).then_inc(early_loaded, 16)
                load_weights(At(0, 0), slice(0, STAGES))
                load_x(At(0, 1))
                for dst, src in ((hw1, hyp_w1), (feat[:], feature), (hw2, hyp_w2), (sw1, sty_w1), (sw2, sty_w2),
                                 (g0[:], spread(gamma0, P)), (b0[:], spread(beta0, P)), (rw[:], router_w)):
                    sp.dma_start(dst, src).then_inc(late_loaded, 16)
                sp.wait_ge(select_copied, SELECTS)
                load_adapters(At(0, 0))
                sp.wait_ge(cleared_zero, 1)
                sp.dma_start(spare_rows, zero_out).then_inc(spare_stored, 16)
                sp.wait_ge(rows_numbered, 2)
                sp.dma_start(queues[IDLE:IDLE + SLOTS].rearrange("(s p) d -> p s d", p=P),
                             bcast(pad_row[:].bitcast(U32), 1, [P, SUB, ROW // 2])).then_inc(filled, 16)

                def body(i):
                    first = isinstance(i.g, int) and i.g == 0
                    if (s1 := back(i, 0)) is not None and not first:
                        load_adapters(s1)
                    load_weights(i, slice(STAGES if first else 0, None))
                    if (s2 := back(i, 1)) is not None:
                        if not isinstance(i.g, int) or i.g + 1 < GROUPS:
                            wait_apart(sp, ids_loaded, (up_done, s2.g + 1))
                            load_x(At(s2.half + 1, s2.par))
                        sp.wait_ge(x1_ready, s2.g + 1)
                        sp.dma_start(of(out_rows, s2.g), rb[:, s2.par]).then_inc(x1_stored[s2.par], 16)

                iterations(sp, body, until=GROUPS // 2 - 1)
                sp.wait_ge(counts_known, 1)
                fill_queues(sp, 0)
                for par in range(2):
                    sp.wait_ge(x1_stored[par], GROUPS // 2 * 16)
                sp.wait_ge(spare_stored, 16)
                sp.wait_ge(filled, (EXPERTS + 1) * 16)

            @block.gpsimd
            def _(pool):
                def iota(dst, pattern, base=0, channel=0):
                    return nc.gpsimd.iota(dst, pattern, base=base, channel_multiplier=channel,
                                          allow_small_or_imprecise_dtypes=True)

                iota(part_no[:], [[0, 1]], channel=1).then_inc(pool_consts, 1)
                nc.gpsimd.memset(ident[:], 0.0).then_inc(pool_consts, 1)
                pool.wait_ge(pool_consts, 2)
                nc.gpsimd.affine_select(out=ident[:], in_=ident[:], compare_op=ALU.not_equal, fill=1.0, base=0,
                                        pattern=[[-1, P]], channel_multiplier=1).then_inc(pool_consts, 1)
                nc.gpsimd.memset(minus_half[:], -0.5).then_inc(pool_consts, 1)
                nc.gpsimd.memset(item_add[:], 0.0).then_inc(pool_consts, 1)
                nc.gpsimd.memset(zero_out, 0.0).then_inc(cleared_zero, 1)
                nc.gpsimd.memset(earlier, 0.0).then_inc(pool_consts, 1)
                pool.wait_ge(pool_consts, 6)
                nc.gpsimd.affine_select(out=earlier, in_=earlier, compare_op=ALU.is_ge, fill=1.0, base=0,
                                        pattern=[[-1, P]], channel_multiplier=1).then_inc(pool_consts, 1)
                nc.gpsimd.tensor_copy(ident16[:], ident[:]).then_inc(pool_consts, 1)
                nc.gpsimd.memset(ones16[:], 1.0).then_inc(pool_consts, 1)
                pool.wait_ge(pool_consts, 7)
                nc.gpsimd.tensor_copy(earlier16[:], earlier).then_inc(pool_consts, 1)
                iota(expert_no[:], [[1, EXPERTS]]).then_inc(pool_consts, 1)
                iota(queue_start[:], [[QUEUE, EXPERTS]]).then_inc(pool_consts, 1)
                nc.gpsimd.memset(chosen_sum[:], 0.0).then_inc(pool_consts, 1)
                nc.gpsimd.memset(h_rows[:], 0.0).then_inc(rows_cleared, 1)
                nc.gpsimd.memset(pad_row[:], 0.0).then_inc(rows_cleared, 1)
                iota(first_tokens, [[GROUP, 2], [P, GT]], base=-2 * GROUP, channel=1).then_inc(rows_cleared, 1)
                iota(spare_no, [[0, 1]], base=TOKENS, channel=1).then_inc(rows_cleared, 1)
                iota(tile_no[:], [[1, TILES]]).then_inc(rows_cleared, 1)
                iota(tile_start[:], [[SLOTS, TOKENS // SLOTS]]).then_inc(rows_cleared, 1)
                nc.gpsimd.memset(zeros[:], 0.0).then_inc(rows_cleared, 1)

                def rstd(g, mv, mv_sem, rs, used_sem, ve_sem, rs_sem):
                    wait_apart(pool, select_copied, (mv_sem, g + 1), (used_sem, g))
                    nc.gpsimd.tensor_scalar(rs[:], mv[:, :, 1], 1e-5, None, ALU.add).then_inc(ve_sem, 1)
                    pool.wait_ge(ve_sem, g + 1)
                    nc.gpsimd.tensor_tensor(rs[:], rs[:], minus_half[:, 0:GT], ALU.pow).then_inc(rs_sem, 1)

                SENDS = [(t, k) for t in range(GT) for k in range(2)]

                def scatter(i, sends):
                    wait_apart(pool, select_copied, (slots_known, i.g + 1))
                    for t, k in sends:
                        nc.gpsimd.indirect_dma_start(
                            out=queues, out_offset=bass.IndirectOffsetOnAxis(ap=slot[:, i.par, t, k:k + 1], axis=0),
                            in_=h_rows[:, i.par, t, :].bitcast(U32), in_offset=None).then_inc(scattered[i.par], 16)

                def body(i):
                    s2, s3, s4 = back(i, 1), back(i, 2), back(i, 3)
                    if s2 is not None:
                        rstd(s2.g, mv0, mv0_ready, rs0, x1_ready, ve0_ready, rs0_ready)
                    if s4 is not None:
                        scatter(s4, SENDS[:3])
                    if s3 is not None:
                        pool.wait_ge(var4_ready, s3.g + 1)
                        for c in range(DC):
                            of_c = slice(c * GI, (c + 1) * GI)
                            nc.gpsimd.tensor_tensor(rsT[:, of_c], var4[:, of_c], minus_half[:, of_c],
                                                    ALU.pow).then_inc(rsT_ready, 1)
                    if s2 is not None:
                        rstd(s2.g, mv1, mv1_ready, rs1, n_ready, ve1_ready, rs1_ready)
                    if s4 is not None:
                        scatter(s4, SENDS[3:])

                pool.wait_ge(select_copied, SELECTS)
                iterations(pool, body)
                scatter(At(GROUPS // 2, -1), SENDS)
                for par in range(2):
                    pool.wait_ge(scattered[par], GROUPS // 2 * GT * 2 * 16)

            @block.tensor
            def _(pe):
                def item_rows():
                    pe.wait_ge(early_loaded, 16 * N_EARLY)
                    pe.wait_ge(hot_ready, 3)
                    nc.tensor.matmul(banks[0:ITEMS, 7, 0:A], hot_w[0:ADAPTERS], t_ab, start=True, stop=False)
                    nc.tensor.matmul(banks[0:ITEMS, 7, 0:A], hot_e, t_de, start=False, stop=True)
                    nc.tensor.matmul(banks[0:SE, 7, A:A + ITEMS], t_se, hot_s, start=True, stop=True).then_inc(net_done, 1)

                def select():
                    pe.wait_ge(table_loaded, 16)
                    for b in range(SELECTS):
                        wait(pe, select_copied, b - 1)
                        for k in range(8):
                            q = b * 8 + k
                            last = nc.tensor.matmul(banks[:, 4 + b % 2, k * ITEMS:(k + 1) * ITEMS],
                                                    table[:, q * 2 * A:(q + 1) * 2 * A], hot_w, start=True, stop=True)
                        last.then_inc(select_done, 1)

                def style_network():
                    pe.wait_ge(late_loaded, 16 * N_LATE)
                    pe.wait_ge(select_copied, SELECTS)
                    for w, src, bank, n, k in ((hw1, se_sb, 4, SH, 1), (hw2, hy1, 5, SH, 2), (sw1, hy2, 4, SH // 2, 3)):
                        pe.wait_ge(net_ready, k + 1)
                        nc.tensor.matmul(banks[0:n, bank, 0:ITEMS], w, src, start=True, stop=True).then_inc(net_done, 1)
                    pe.wait_ge(net_ready, 5)
                    for c in range(2 * DC):
                        last = nc.tensor.matmul(banks[:, 5, c * ITEMS:(c + 1) * ITEMS], sw2[:, c * P:(c + 1) * P],
                                                st1, start=True, stop=True)
                    last.then_inc(net_done, 1)
                    pe.wait_ge(net_ready, 6)

                def into_features(i):
                    pe.wait_ge(x_loaded[i.par], (i.half + 1) * 16)
                    for c in range(DC):
                        wait(pe, hT_ready, (i.g - 2) * DC + (c + 1))
                        for t in range(GT):
                            last = nc.tensor.transpose(ps_x[:, c, t * P:(t + 1) * P],
                                                       xb[:, i.par, t, c * P:(c + 1) * P], ident[:])
                        last.then_inc(xT_done, 1)

                def adapter(i):
                    if isinstance(i.g, int) and i.g == 0:
                        item_rows()
                        pe.wait_ge(dom_row, 2)
                        pe.wait_ge(net_ready, 2)
                    wait_apart(pe, dom_row, (dom_ready, i.g))
                    wait(pe, place_ready, i.g - 2)
                    nc.tensor.matmul(ps_dom, item_add[:], bcast(ident[:, bass.ds(i.g * GI, GI)], 2, [P, GI, T]),
                                     start=True, stop=False)
                    wait(pe, logits_copied, i.g - 2)
                    for c in range(DC):
                        pe.wait_ge(xT_ready, i.g * DC + (c + 1))
                        last = nc.tensor.matmul(ps_down, dw[:, c, :], xT[:, c, :], start=(c == 0), stop=(c == DC - 1))
                    last.then_inc(down_done, 1)
                    if isinstance(i.g, int) and i.g == 0:
                        select()
                        style_network()
                    wait_apart(pe, dom_row, (wnow_loaded[i.par], (i.half + 1) * 16), (act_ready, i.g + 1))
                    for b in range(GI):
                        last = nc.tensor.matmul(ps_dom[:, b * T:(b + 1) * T], wnow[:, i.par, b * A:(b + 1) * A],
                                                act[:, b * T:(b + 1) * T], start=False, stop=(b == GI - 1))
                    last.then_inc(adapt_done, 1)
                    pe.wait_ge(dom_ready, i.g + 1)
                    wait(pe, centred_ready, i.g * GT)
                    for t in range(GT):
                        nc.tensor.matmul(ps_u[:, t, :], dom[:, t * P:(t + 1) * P], uw[:], start=True, stop=False)
                        last = nc.tensor.matmul(ps_u[:, t, :], ident[:], xb[:, i.par, t, :], start=False, stop=True)
                    last.then_inc(up_done, 1)

                def route_and_back(i):
                    pe.wait_ge(h_ready, i.g + 1)
                    pe.wait_ge(h_rest_ready, i.g + 1)
                    pe.wait_ge(act_ready, upto(i.g, 3, GROUPS))
                    for t in range(GT):
                        for c in range(DC):
                            last = nc.tensor.matmul(ps_lg[:, t, :], hT[:, c, t * P:(t + 1) * P], rw[:, c, :],
                                                    start=(c == 0), stop=(c == DC - 1))
                    last.then_inc(logits_done, 1)
                    wait(pe, low_ready, i.g)
                    for t in range(GT):
                        for c in range(DC):
                            last = nc.tensor.transpose(ps_h[:, t, c * P:(c + 1) * P], hT[:, c, t * P:(t + 1) * P], ident[:])
                    last.then_inc(back_done, 1)

                def normed_into_features(i):
                    pe.wait_ge(n_ready, i.g + 1)
                    pe.wait_ge(xT_ready, min(i.g + 2, GROUPS) * DC if isinstance(i.g, int) else (i.g + 2) * DC)
                    for c in range(DC):
                        for t in range(GT):
                            last = nc.tensor.transpose(ps_x[:, c, t * P:(t + 1) * P], nb[:, t, c * P:(c + 1) * P], ident[:])
                        last.then_inc(nT_done, 1)

                def rank(i):
                    pe.wait_ge(chosen_ready, i.g + 1)
                    pe.wait_ge(dom_ready, upto(i.g, 3, GROUPS))
                    wait(pe, sum_ready, i.g)
                    nc.tensor.matmul(ps_rank, earlier16[:], chosen[:], start=True, stop=False)
                    for n in range(1, GT):
                        nc.tensor.matmul(ps_rank[:, n:GT, :], ones16[:], chosen[:, 0:GT - n, :], start=False, stop=False)
                    for t in range(GT):
                        last = nc.tensor.matmul(ps_rank, ones16[:], bcast(chosen_sum[:, t, :], 1, [P, GT, EXPERTS]),
                                                start=False, stop=(t == GT - 1))
                    last.then_inc(rank_done, 1)

                pe.wait_ge(pool_consts, N_POOL)

                def body(i):
                    s1, s2, s3 = back(i, 0), back(i, 1), back(i, 2)
                    if s1 is not None:
                        into_features(s1)
                        adapter(s1)
                    if s3 is not None:
                        route_and_back(s3)
                    if s2 is not None:
                        normed_into_features(s2)
                    if s3 is not None:
                        rank(s3)

                iterations(pe, body)
                pe.wait_ge(sum_ready, GROUPS)
                for t in range(GT):
                    last = nc.tensor.matmul(banks[:, 6, 0:EXPERTS], ones16[:], chosen_sum[:, t, :],
                                            start=(t == 0), stop=(t == GT - 1))
                last.then_inc(counted, 1)

            @block.scalar
            def _(sc):
                def softplus():
                    sc.wait_ge(net_ready, 6)
                    nc.scalar.activation(absz, style, ACT.Abs).then_inc(style_step, 1)
                    sc.wait_ge(style_step, 1)
                    nc.scalar.activation(expz, absz, ACT.Exp, scale=-1.0).then_inc(style_step, 1)
                    sc.wait_ge(style_step, 2)
                    nc.scalar.activation(lnz, expz, ACT.Ln, bias=1.0).then_inc(lnz_ready, 1)

                def cut_high(i, some):
                    for q, slot, turn in chunks(i)[some]:
                        sc.wait_ge(stage_loaded[slot], (turn + 1) * 16)
                        nc.scalar.activation(w_high[:, bass.ds(q * CHUNK, CHUNK)], stage[:, slot], ACT.Copy,
                                             scale=WSCALE).then_inc(w_high_ready, 1)

                def features_out(i):
                    for c in range(DC):
                        sc.wait_ge(xT_done, i.g * DC + (c + 1))
                        wait(sc, down_done, i.g)
                        nc.scalar.activation(xT[:, c, :], ps_x[:, c, :], ACT.Copy).then_inc(xT_ready, 1)

                def activate(i):
                    sc.wait_ge(down_done, i.g + 1)
                    wait(sc, adapt_done, i.g)
                    if isinstance(i.g, int) and i.g == 0:
                        sc.wait_ge(early_loaded, 16 * N_EARLY)
                    nc.scalar.activation(act[:], ps_down, ACT.Gelu, bias=ab[:, 0:1]).then_inc(act_ready, 1)

                def adapted(i):
                    sc.wait_ge(adapt_done, i.g + 1)
                    wait(sc, up_done, i.g)
                    nc.scalar.activation(dom[0:A], ps_dom, ACT.Copy).then_inc(dom_ready, 1)

                def item_norm(i):
                    sc.wait_ge(aff_ready[0], (i.g + 1) * 3)
                    for b in range(GI):
                        v = hT[:, 0, b * T:(b + 1) * T]
                        last = nc.scalar.activation(v, v, ACT.Identity, scale=aff_a[:, 0, b:b + 1],
                                                    bias=aff_c[:, 0, b:b + 1])
                    last.then_inc(h_ready, 1)

                def logits(i):
                    sc.wait_ge(logits_done, i.g + 1)
                    wait(sc, top_at_ready, i.g)
                    nc.scalar.activation(lg[:], ps_lg, ACT.Copy).then_inc(logits_copied, 1)

                def high(i):
                    sc.wait_ge(back_done, i.g + 1)
                    if isinstance(i.g, int) and i.g == 0:
                        sc.wait_ge(rows_numbered, 2)
                    wait(sc, scattered[i.par], i.half * GT * 2 * 16)
                    nc.scalar.activation(h_rows[:, i.par, :, 0:D], ps_h, ACT.Copy).then_inc(high_ready, 1)

                def layer_norm(i):
                    sc.wait_ge(shift1_ready, i.g + 1)
                    wait(sc, nT_done, i.g * DC)
                    for t in range(GT):
                        last = nc.scalar.activation(nb[:, t, :], rb[:, i.par, t, :], ACT.Identity,
                                                    scale=rs1[:, t:t + 1], bias=shift1[:, t:t + 1])
                    last.then_inc(n_ready, 1)
                    if isinstance(i.g, int) and i.g == 0:
                        sc.wait_ge(spare_stored, 16)
                        sc.wait_ge(late_loaded, 16 * N_LATE)

                def scale_features(i):
                    for c in range(DC):
                        sc.wait_ge(nT_done, i.g * DC + (c + 1))
                        wait(sc, back_done, i.g)
                        nc.scalar.activation(hT[:, c, :], ps_x[:, c, :], ACT.Identity,
                                             scale=feat[:, LN_G + c:LN_G + c + 1],
                                             bias=feat[:, LN_B + c:LN_B + c + 1]).then_inc(hT_ready, 1)

                def body(i):
                    s1, s2, s3 = back(i, 0), back(i, 1), back(i, 2)
                    if s1 is not None:
                        features_out(s1)
                    cut_high(i, slice(0, 2))
                    if s1 is not None:
                        activate(s1)
                    cut_high(i, slice(2, 3))
                    if s1 is not None:
                        adapted(s1)
                    cut_high(i, slice(3, None))
                    if s3 is not None:
                        item_norm(s3)
                    if s2 is not None:
                        layer_norm(s2)
                    if s3 is not None:
                        logits(s3)
                        high(s3)
                    if s2 is not None:
                        scale_features(s2)

                iterations(sc, body, after={0: softplus})
                sc.wait_ge(counts_known, 1)
                fill_queues(sc, 1)

            @block.vector
            def _(dve):
                V = nc.vector
                step = [0]

                def link(ins):
                    step[0] += 1
                    ins.then_inc(table_step, 1)
                    dve.wait_ge(table_step, step[0])

                V.memset(dom[A:A + 1, :], 1.0).then_inc(dom_row, 1)
                dve.wait_ge(ids_loaded, 32)
                dve.wait_ge(pool_consts, 1)
                link(V.tensor_copy(idf, ids_i))
                link(V.tensor_copy(sidf, sids_i))
                link(V.tensor_scalar(idc, idf, -1.0, float(NONE_ROW), ALU.max, ALU.min))
                link(V.tensor_scalar(hot_w, idc, 0.0, float(NONE_ROW + 1), ALU.is_lt, ALU.mult))
                link(V.tensor_tensor(idc, idc, hot_w, ALU.add))
                V.tensor_scalar(hot_w, idc, part_no[0:NONE_ROW + 1, 0:1], None, ALU.is_equal).then_inc(hot_ready, 1)
                link(V.tensor_scalar(idf, idf, 0.0, float(ADAPTERS - 1), ALU.max, ALU.min))
                V.tensor_scalar(hot_e, idf[0:ADAPTERS], part_no[0:ADAPTERS, 0:1], None, ALU.is_equal).then_inc(hot_ready, 1)
                link(V.tensor_scalar(sidf, sidf, 0.0, float(SUBJECTS - 1), ALU.max, ALU.min))
                V.tensor_scalar(hot_s, sidf, part_no[0:SUBJECTS, 0:1], None, ALU.is_equal).then_inc(hot_ready, 1)
                dve.wait_ge(net_done, 1)
                dve.wait_ge(pool_consts, N_POOL)
                V.tensor_copy(item_add[0:ITEMS], banks[0:ITEMS, 7, 0:A]).then_inc(dom_row, 1)
                V.tensor_copy(se_sb, banks[0:SE, 7, A:A + ITEMS]).then_inc(net_ready, 2)
                for b in range(SELECTS):
                    dve.wait_ge(select_done, b + 1)
                    for w in range(2):
                        last = V.tensor_copy(wsel_pairs[:, w, b * 8:(b + 1) * 8, :],
                                             banks[w * A:(w + 1) * A, 4 + b % 2, :].rearrange("a (q i) -> a q i", i=ITEMS))
                    last.then_inc(select_copied, 1)
                dve.wait_ge(rows_cleared, 7)
                V.tensor_copy(token_field(h_rows[:], "p a t o -> p a (t o)"), first_tokens).then_inc(rows_numbered, 1)
                V.tensor_copy(pad_row[:, ROW_TOKEN:ROW_TOKEN + 2].bitcast(I32), spare_no).then_inc(rows_numbered, 1)

                dve.wait_ge(late_loaded, 16 * N_LATE)
                dve.wait_ge(net_done, 2)
                V.tensor_scalar(hy1, banks[0:SH, 4, 0:ITEMS], feat[:, HYP_B1:HYP_B1 + 1], 0.0, ALU.add,
                                ALU.max).then_inc(net_ready, 1)
                dve.wait_ge(net_done, 3)
                V.tensor_scalar(hy2, banks[0:SH, 5, 0:ITEMS], feat[:, HYP_B2:HYP_B2 + 1], None,
                                ALU.add).then_inc(net_ready, 1)
                dve.wait_ge(net_done, 4)
                V.tensor_scalar(st1, banks[0:SH // 2, 4, 0:ITEMS], ab[:, 1:2], 0.0, ALU.add, ALU.max).then_inc(net_ready, 1)
                dve.wait_ge(net_done, 5)
                for c in range(DC):
                    V.tensor_scalar(style[:, c * ITEMS:(c + 1) * ITEMS], banks[:, 5, c * ITEMS:(c + 1) * ITEMS],
                                    feat[:, STY_B2 + c:STY_B2 + c + 1], None, ALU.add)
                for c in range(DC):
                    last = V.tensor_scalar(item_beta[:, c, :], banks[:, 5, (DC + c) * ITEMS:(DC + c + 1) * ITEMS],
                                           feat[:, STY_B2 + DC + c:STY_B2 + DC + c + 1], None, ALU.add)
                last.then_inc(net_ready, 1)

                def item_gammas():
                    dve.wait_ge(lnz_ready, 1)
                    gam = item_gamma[:].rearrange("p c i -> p (c i)")
                    link(V.scalar_tensor_tensor(gam, style, 0.0, lnz, ALU.max, ALU.add))
                    link(V.tensor_scalar(gam, gam, 1e-8, None, ALU.add))

                def moments_parts(src, stats, st_sem, used, g, tiles=slice(0, GT)):
                    wait(dve, used, g)
                    for t in range(tiles.start, tiles.stop):
                        V.bn_stats(stats[:, t, :], src[:, t, :]).then_inc(st_sem, 1)

                def moments(stats, st_sem, mv, mv_sem, g):
                    wait_apart(dve, pool_consts, (st_sem, (g + 1) * GT))
                    for t in range(GT):
                        last = V.bn_aggr(mv[:, t, :], stats[:, t, :])
                    last.then_inc(mv_sem, 1)

                def centre(i, t):
                    if t == 0:
                        dve.wait_ge(mv0_ready, i.g + 1)
                        wait(dve, x1_stored[i.par], i.half * 16)
                        wait(dve, n_ready, i.g - 1)
                    V.scalar_tensor_tensor(rb[:, i.par, t, :], ps_u[:, t, :], mv0[:, t, 0:1], g0[:], ALU.subtract,
                                           ALU.mult).then_inc(centred_ready, 1)

                def adapter_norm(i):
                    dve.wait_ge(rs0_ready, i.g + 1)
                    dve.wait_ge(centred_ready, (i.g + 1) * GT)
                    for t in range(GT):
                        v = rb[:, i.par, t, :]
                        last = V.scalar_tensor_tensor(v, v, rs0[:, t:t + 1], b0[:], ALU.mult, ALU.add)
                    last.then_inc(x1_ready, 1)

                def norm_shift(i):
                    dve.wait_ge(rs1_ready, i.g + 1)
                    wait(dve, n_ready, i.g)
                    V.scalar_tensor_tensor(shift1[:], mv1[:, :, 0], -1.0, rs1[:], ALU.mult, ALU.mult).then_inc(shift1_ready, 1)

                def item_parts(i, c):
                    dve.wait_ge(hT_ready, i.g * DC + (c + 1))
                    for b in range(GI):
                        last = V.bn_stats(statsT[:, c * GI + b, :], hT[:, c, b * T:(b + 1) * T])
                    last.then_inc(stT_ready, 1)

                def item_variance(i, k):
                    if k == 0:
                        dve.wait_ge(stT_ready, (i.g + 1) * DC)
                        V.tensor_tensor(msum[:], statsT[:, :, 1], statsT[:, :, 4], ALU.add)
                        V.tensor_tensor(mdiff[:], statsT[:, :, 1], statsT[:, :, 4], ALU.subtract)
                        V.tensor_tensor(var4[:], statsT[:, :, 2], statsT[:, :, 5], ALU.add).then_inc(item_step, 1)
                        return
                    dve.wait_ge(item_step, i.g * 3 + k)
                    if k == 1:
                        V.tensor_tensor(mdiff[:], mdiff[:], mdiff[:], ALU.mult).then_inc(item_step, 1)
                    if k == 2:
                        V.scalar_tensor_tensor(var4[:], var4[:], 4.0 / T, mdiff[:], ALU.mult, ALU.add).then_inc(item_step, 1)
                    if k == 3:
                        V.tensor_scalar(var4[:], var4[:], 0.25, 1e-8, ALU.mult, ALU.add).then_inc(var4_ready, 1)

                def item_scale(i, c, k):
                    items = bass.ds(i.g * GI, GI)
                    of_c = slice(c * GI, (c + 1) * GI)
                    if k == 0:
                        dve.wait_ge(rsT_ready, i.g * DC + (c + 1))
                        wait(dve, h_ready, i.g)
                        V.tensor_tensor(aff_a[:, c, :], rsT[:, of_c], item_gamma[:, c, items],
                                        ALU.mult).then_inc(aff_ready[c], 1)
                        return
                    dve.wait_ge(aff_ready[c], i.g * 3 + k)
                    if k == 1:
                        V.scalar_tensor_tensor(aff_c[:, c, :], msum[:, of_c], 0.5, aff_a[:, c, :], ALU.mult,
                                               ALU.mult).then_inc(aff_ready[c], 1)
                    if k == 2:
                        V.tensor_tensor(aff_c[:, c, :], item_beta[:, c, items], aff_c[:, c, :],
                                        ALU.subtract).then_inc(aff_ready[c], 1)

                def item_norm_rest(i, add):
                    v = hT[:, 1, :].rearrange("p (b t) -> p b t", t=T)
                    if not add:
                        dve.wait_ge(aff_ready[1], i.g * 3 + 1)
                        V.tensor_tensor(v, v, bcast(aff_a[:, 1, :], 2, [P, GI, T]), ALU.mult).then_inc(scaled_ready, 1)
                    else:
                        dve.wait_ge(scaled_ready, i.g + 1)
                        dve.wait_ge(aff_ready[1], (i.g + 1) * 3)
                        V.tensor_tensor(v, v, bcast(aff_c[:, 1, :], 2, [P, GI, T]), ALU.add).then_inc(h_rest_ready, 1)

                def cut_low(i, some):
                    for q, slot, turn in chunks(i)[some]:
                        dve.wait_ge(w_high_ready, q + 1)
                        w = bass.ds(q * CHUNK, CHUNK)
                        V.scalar_tensor_tensor(w_low[:, w], stage[:, slot], WSCALE, w_high[:, w], ALU.mult,
                                               ALU.subtract).then_inc(w_low_ready, 1)

                def best_two(i):
                    wait_apart(dve, pool_consts, (logits_copied, i.g + 1))
                    for t in range(GT):
                        last = V.max(top[:, t, :], lg[:, t, :])
                    last.then_inc(top_ready, 1)

                def their_experts(i):
                    wait_apart(dve, pool_consts, (top_ready, i.g + 1))
                    for t in range(GT):
                        last = V.max_index(top_at[:, t, :], top[:, t, :], lg[:, t, :])
                    last.then_inc(top_at_ready, 1)

                def choices(i):
                    dve.wait_ge(top_at_ready, i.g + 1)
                    V.tensor_copy(choice[:], top_at[:, :, 0:2]).then_inc(choice_ready, 1)

                def choice_masks(i):
                    dve.wait_ge(choice_ready, i.g + 1)
                    V.tensor_tensor(mask[:], bcast(expert_no[:].unsqueeze(1), 1, [P, GT, 2, EXPERTS]),
                                    bcast(choice[:], 3, [P, GT, 2, EXPERTS]), ALU.is_equal).then_inc(mask_ready, 1)

                def both_choices(i):
                    dve.wait_ge(mask_ready, i.g + 1)
                    V.tensor_tensor(chosen[:], mask[:, :, 0, :], mask[:, :, 1, :], ALU.add).then_inc(chosen_ready, 1)

                def low(i):
                    dve.wait_ge(high_ready, i.g + 1)
                    V.tensor_tensor(h_rows[:, i.par, :, D:2 * D], ps_h, h_rows[:, i.par, :, 0:D],
                                    ALU.subtract).then_inc(low_ready, 1)

                def row_fields(i):
                    dve.wait_ge(choice_ready, i.g + 1)
                    field = h_rows[:, i.par]
                    V.tensor_tensor(float_field(field, ROW_DIFF), top[:, :, 1], top[:, :, 0], ALU.subtract)
                    V.tensor_copy(float_field(field, ROW_FIRST), choice[:, :, 0])
                    tok = token_field(field, "p t o -> p (t o)")
                    V.tensor_scalar(tok, tok, float(2 * GROUP), None, ALU.add)

                def place_rows(i, k):
                    if k == 0:
                        dve.wait_ge(rank_done, i.g + 1)
                        V.tensor_tensor(place[:], ps_rank, bcast(queue_start[:], 1, [P, GT, EXPERTS]),
                                        ALU.add).then_inc(place_ready, 1)
                        V.tensor_tensor(chosen_sum[:], chosen_sum[:], chosen[:], ALU.add).then_inc(sum_ready, 1)
                    if k == 1:
                        dve.wait_ge(place_ready, i.g + 1)
                        V.tensor_tensor(mask[:], mask[:], bcast(place[:], 2, [P, GT, 2, EXPERTS]),
                                        ALU.mult).then_inc(picked_ready, 1)
                    if k == 2:
                        dve.wait_ge(picked_ready, i.g + 1)
                        V.tensor_reduce(slot_f[:], mask[:], AX, ALU.add).then_inc(slot_f_ready, 1)
                    if k == 3:
                        dve.wait_ge(slot_f_ready, i.g + 1)
                        V.tensor_copy(slot[:, i.par], slot_f[:]).then_inc(slots_known, 1)

                def body(i):
                    s1, s2, s3, s4 = (back(i, n) for n in range(4))

                    def step(group, work, *args):
                        if group is not None:
                            work(group, *args)

                    step(s4, place_rows, 0)
                    if s2 is not None:
                        dve.wait_ge(up_done, s2.g + 1)
                        moments_parts(ps_u, stats0, st0_ready, rs0_ready, s2.g)
                    step(s4, place_rows, 1)
                    if s2 is not None:
                        moments(stats0, st0_ready, mv0, mv0_ready, s2.g)
                    step(s4, place_rows, 2)
                    step(s3, item_parts, 0)
                    step(s4, place_rows, 3)
                    step(s3, item_parts, 1)
                    step(s2, centre, 0)
                    step(s3, item_variance, 0)
                    step(s2, centre, 1)
                    step(s3, item_variance, 1)
                    step(s2, centre, 2)
                    step(s3, item_variance, 2)
                    step(s2, centre, 3)
                    step(s3, item_variance, 3)
                    step(s2, adapter_norm)
                    step(s3, item_scale, 0, 0)
                    if s2 is not None:
                        dve.wait_ge(x1_ready, s2.g + 1)
                        moments_parts(rb[:, s2.par], stats1, st1_ready, rs1_ready, s2.g, slice(0, 1))
                    step(s3, item_scale, 0, 1)
                    if s2 is not None:
                        moments_parts(rb[:, s2.par], stats1, st1_ready, rs1_ready, s2.g, slice(1, 2))
                    step(s3, item_scale, 0, 2)
                    if s2 is not None:
                        moments_parts(rb[:, s2.par], stats1, st1_ready, rs1_ready, s2.g, slice(2, GT))
                    step(s3, item_scale, 1, 0)
                    if s2 is not None:
                        moments(stats1, st1_ready, mv1, mv1_ready, s2.g)
                    step(s3, item_scale, 1, 1)
                    step(s3, item_norm_rest, False)
                    step(s3, item_scale, 1, 2)
                    if s1 is not None:
                        wait_apart(dve, pool_consts, (wnow_loaded[s1.par], (s1.half + 1) * 16))
                    step(s3, item_norm_rest, True)
                    step(s2, norm_shift)
                    cut_low(i, slice(None))
                    step(s3, best_two)
                    step(s3, their_experts)
                    step(s3, choices)
                    step(s3, choice_masks)
                    step(s3, both_choices)
                    step(s3, low)
                    step(s3, row_fields)

                iterations(dve, body, after={0: item_gammas})
                for k in range(4):
                    place_rows(At(GROUPS // 2, -1), k)

                GRID = [P, TILES, EXPERTS]
                count, ntiles, tile_end, tile_first, offset = (per_expert(k) for k in range(5))
                dve.wait_ge(counted, 1)
                for par in range(2):
                    dve.wait_ge(x1_stored[par], GROUPS // 2 * 16)
                dve.wait_ge(nT_done, GROUPS * DC)
                V.tensor_copy(counts[:], banks[0:1, 6, 0:EXPERTS]).then_inc(counts_known, 1)
                link(V.tensor_copy(count, banks[:, 6, 0:EXPERTS]))
                over_e = over.rearrange("p (e k) -> p e k", e=EXPERTS)
                OVER = [P, EXPERTS, TOKENS // SLOTS]
                link(V.tensor_tensor(over_e, bcast(count, 2, OVER), bcast(tile_start[:], 1, OVER), ALU.is_gt))
                link(V.tensor_reduce(ntiles, over_e, AX, ALU.add))
                link(V.tensor_tensor_scan(tile_end, ntiles, zeros[:], 0.0, ALU.add, ALU.add))
                link(V.tensor_tensor(tile_first, tile_end, ntiles, ALU.subtract))
                link(V.tensor_tensor(grid(0), bcast(tile_no[:], 2, GRID), bcast(tile_first, 1, GRID), ALU.is_ge))
                link(V.tensor_reduce(line(0), grid(0), AX, ALU.add))
                link(V.tensor_scalar(tile_expert_f[:], line(0), -1.0, None, ALU.add))
                V.tensor_copy(tile_expert[:], tile_expert_f[0:1])
                link(V.scalar_tensor_tensor(offset, tile_first, -float(SLOTS), queue_start[:], ALU.mult, ALU.add))
                link(V.tensor_tensor(grid(1), bcast(tile_expert_f[:], 2, GRID), bcast(expert_no[:], 1, GRID), ALU.is_equal))
                link(V.tensor_tensor(grid(1), grid(1), bcast(offset, 1, GRID), ALU.mult))
                link(V.tensor_reduce(line(0), grid(1), AX, ALU.add))
                link(V.scalar_tensor_tensor(line(0), tile_no[:], float(SLOTS), line(0), ALU.mult, ALU.add))
                link(V.tensor_scalar(line(1), tile_no[:], tile_end[:, EXPERTS - 1:EXPERTS], None, ALU.is_lt))
                link(V.scalar_tensor_tensor(line(0), line(0), -float(IDLE), line(1), ALU.add, ALU.mult))
                V.tensor_scalar(tile_row[:], line(0)[0:1], float(IDLE), None, ALU.add)


def experts(nc, sem, env):
    queues, out, exp_b2 = env["queues"], env["out"], env["exp_b2"]
    w_high, w_low, feat, ident16, tile_expert, tile_row, tile_expert_f, banks = (
        env[n] for n in ("w_high", "w_low", "feat", "ident16", "tile_expert", "tile_row",
                         "tile_expert_f", "banks"))

    with ExitStack() as ctx:
        def sb(name, shape, dt=F32):
            return ctx.enter_context(nc.sbuf_tensor(name, shape, dt))

        b2 = sb("b2", [P, EXPERTS * D])
        rows = sb("rows", [P, 2, SUB, ROW], F16)
        rT = sb("rT", [P, 2, 2, DC, SLOTS], F16)
        hid = sb("hid", [P, FC, SLOTS])
        hid_high = sb("hid_high", [P, 2, FC, SLOTS], F16)
        hid_low = sb("hid_low", [P, 2, FC, SLOTS], F16)
        yb = sb("yb", [P, SUB, D])
        yg = sb("yg", [P, 2, SUB, D])
        token = sb("token", [P, 2, SUB], U32)
        gate = sb("gate", [P, 2, SUB])
        ratio = sb("ratio", [P, SUB])
        norm = sb("norm", [P, SUB])
        second = sb("second", [P, SUB])
        is_first = sb("is_first", [P, SUB])

        b2_loaded = sem("b2_loaded")
        rows_loaded = [sem("rows_loaded0"), sem("rows_loaded1")]
        rT_done, rT_ready, in_done, hid_ready, split_high, split_low, out_done, y_ready = (
            sem(n) for n in ("rT_done", "rT_ready", "in_done", "hid_ready", "split_high", "split_low",
                             "out_done", "y_ready"))
        ratio_ready, meta_taken, gate_step, norm_ready, gate_ready, gated, added = (
            sem(n) for n in ("ratio_ready", "meta_taken", "gate_step", "norm_ready", "gate_ready",
                             "gated", "added"))

        PAIRS = FC // 2

        def ps_in(c):
            return banks[:, c // 2, (c % 2) * SLOTS:(c % 2 + 1) * SLOTS]

        def ps_rT(par):
            return banks[:, 4 + par, :].bitcast(F16)

        def ps_out(par):
            return banks[:, 6 + par, :].rearrange("p (s d) -> p s d", d=D)

        def part_of(par, s, k, c):
            return rows[:, par, s, k * D + c * P:k * D + (c + 1) * P]

        def field(par, place, dt):
            return rows[:, par, :, place:place + 2].bitcast(dt).rearrange("p s o -> p (s o)")

        def expert_of(eng, i):
            return eng.value_load(tile_expert[0:1, bass.ds(i.g, 1)], min_val=0, max_val=EXPERTS - 1)

        with nc.Block() as block:

            @block.sync
            def _(sp):
                def load(i):
                    row = sp.value_load(tile_row[0:1, bass.ds(i.g, 1)], min_val=0, max_val=IDLE)
                    wait(sp, rT_done, i.g - 1)
                    wait(sp, meta_taken, i.g - 1)
                    sp.dma_start(rows[:, i.par].bitcast(U32), queues[bass.ds(row, SLOTS)].rearrange("(s p) d -> p s d", p=P)
                                 ).then_inc(rows_loaded[i.par], 16)

                load(At(0, 0))
                load(At(0, 1))
                sp.dma_start(b2[:], spread(exp_b2, P)).then_inc(b2_loaded, 16)
                with sp.Fori(1, TILES // 2) as h:
                    load(At(h, 0))
                    load(At(h, 1))
                load(At(TILES // 2, 0))

            @block.gpsimd
            def _(pool):
                def add_rows(i):
                    for s in range(SUB):
                        wait_apart(pool, b2_loaded, (gated, i.g * SUB + s + 1), (added, (i.g * SUB + s) * 16))
                        nc.gpsimd.indirect_dma_start(
                            out=out, out_offset=bass.IndirectOffsetOnAxis(ap=token[:, i.par, s:s + 1], axis=0),
                            in_=yg[:, i.par, s, :], in_offset=None, compute_op=ALU.add).then_inc(added, 16)

                add_rows(At(0, 0))
                add_rows(At(0, 1))
                with pool.Fori(1, TILES // 2) as h:
                    add_rows(At(h, 0))
                    add_rows(At(h, 1))
                add_rows(At(TILES // 2, 0))
                pool.wait_ge(added, TILES * SUB * 16)

            @block.tensor
            def _(pe):
                def transpose_rows(i):
                    pe.wait_ge(rows_loaded[i.par], (i.half + 1) * 16)
                    wait(pe, rT_ready, i.g - 1)
                    for k in range(2):
                        for c in range(DC):
                            for s in range(SUB):
                                at = (k * DC + c) * SLOTS + s * P
                                last = nc.tensor.transpose(ps_rT(i.par)[:, at:at + P],
                                                           part_of(i.par, s, k, c), ident16[:])
                    last.then_inc(rT_done, 1)

                held = [pe.alloc_register("even_expert"), pe.alloc_register("odd_expert")]

                def expert(i, load=False):
                    if load:
                        pe.reg_load(held[i.par], tile_expert[0:1, bass.ds(i.g, 1)])
                    return pe.snap(held[i.par], min_val=0, max_val=EXPERTS - 1)

                def layer_in(i):
                    e = expert(i, load=True)
                    pe.wait_ge(rT_ready, i.g + 1)
                    for c in range(FC):
                        if c % 2 == 0:
                            wait(pe, hid_ready, (i.g - 1) * PAIRS + c // 2 + 1)
                        n = 0
                        for k in range(DC):
                            at = bass.ds(e * (DC * FF) + (k * FF + c * P), P)
                            for w, v in ((w_high, 0), (w_high, 1), (w_low, 0)):
                                last = nc.tensor.matmul(ps_in(c), w[:, at], rT[:, i.par, v, k, :],
                                                        start=(n == 0), stop=(n == 3 * DC - 1))
                                n += 1
                        if c % 2 == 1:
                            last.then_inc(in_done, 1)

                def layer_out(i):
                    e = expert(i)
                    wait(pe, y_ready, i.g - 1)
                    for s in range(SUB):
                        n = 0
                        for c in range(FC):
                            if s == 0 and c % 2 == 0:
                                pe.wait_ge(split_low, i.g * PAIRS + c // 2 + 1)
                            at = bass.ds(e * (FC * D) + (W2_AT + c * D), D)
                            for w, v in ((w_high, hid_high), (w_high, hid_low), (w_low, hid_high)):
                                last = nc.tensor.matmul(ps_out(i.par)[:, s, :], v[:, i.par, c, s * P:(s + 1) * P],
                                                        w[:, at], start=(n == 0), stop=(n == 3 * FC - 1))
                                n += 1
                    last.then_inc(out_done, 1)

                transpose_rows(At(0, 0))
                layer_in(At(0, 0))
                transpose_rows(At(0, 1))
                layer_in(At(0, 1))
                transpose_rows(At(1, 0))
                layer_out(At(0, 0))
                with pe.Fori(1, TILES // 2) as h:
                    for c in (0, 1):
                        layer_in(At(h, c))
                        transpose_rows(At(h, c + 1))
                        layer_out(At(h, c - 1))
                layer_in(At(TILES // 2, 0))
                layer_out(At(TILES // 2, -1))
                layer_out(At(TILES // 2, 0))

            @block.scalar
            def _(sc):
                def bias_relu(i):
                    e = expert_of(sc, i)
                    for c in range(FC):
                        if c % 2 == 0:
                            sc.wait_ge(in_done, i.g * PAIRS + c // 2 + 1)
                            wait(sc, split_low, (i.g - 1) * PAIRS + c // 2 + 1)
                        last = nc.scalar.activation(hid[:, c, :], ps_in(c), ACT.Relu,
                                                    scale=1.0 / WSCALE, bias=feat[:, bass.ds(e * FC + (B1 + c), 1)])
                        if c % 2 == 1:
                            last.then_inc(hid_ready, 1)

                def choice_ratio(i):
                    sc.wait_ge(rows_loaded[i.par], (i.half + 1) * 16)
                    wait(sc, gate_ready, i.g)
                    nc.scalar.activation(ratio[:], field(i.par, ROW_DIFF, F32), ACT.Exp).then_inc(ratio_ready, 1)

                def times_gate(i):
                    sc.wait_ge(y_ready, i.g + 1)
                    sc.wait_ge(gate_ready, i.g + 1)
                    wait(sc, added, (i.g - 1) * SUB * 16)
                    for s in range(SUB):
                        nc.scalar.activation(yg[:, i.par, s, :], yb[:, s, :], ACT.Copy,
                                             scale=gate[:, i.par, s:s + 1]).then_inc(gated, 1)

                bias_relu(At(0, 0))
                choice_ratio(At(0, 0))
                bias_relu(At(0, 1))
                choice_ratio(At(0, 1))
                times_gate(At(0, 0))
                with sc.Fori(1, TILES // 2) as h:
                    for c in (0, 1):
                        bias_relu(At(h, c))
                        choice_ratio(At(h, c))
                        times_gate(At(h, c - 1))
                bias_relu(At(TILES // 2, 0))
                choice_ratio(At(TILES // 2, 0))
                times_gate(At(TILES // 2, -1))
                times_gate(At(TILES // 2, 0))

            @block.vector
            def _(dve):
                V = nc.vector

                def rows_out(i):
                    dve.wait_ge(rT_done, i.g + 1)
                    wait(dve, in_done, (i.g - 1) * PAIRS)
                    V.tensor_copy(rT[:, i.par].rearrange("p k c s -> p (k c s)"), ps_rT(i.par)).then_inc(rT_ready, 1)

                def split(i, pair):
                    n = i.g * PAIRS + pair + 1
                    dve.wait_ge(hid_ready, n)
                    wait(dve, out_done, i.g - 1)
                    s = slice(pair * 2, pair * 2 + 2)
                    V.tensor_copy(hid_high[:, i.par, s, :], hid[:, s, :]).then_inc(split_high, 1)
                    dve.wait_ge(split_high, n)
                    V.tensor_tensor(hid_low[:, i.par, s, :], hid[:, s, :], hid_high[:, i.par, s, :],
                                    ALU.subtract).then_inc(split_low, 1)

                def gates(i):
                    dve.wait_ge(ratio_ready, i.g + 1)
                    wait(dve, added, (i.g - 1) * SUB * 16)
                    V.tensor_copy(token[:, i.par, :], field(i.par, ROW_TOKEN, U32))
                    V.tensor_scalar(is_first[:], field(i.par, ROW_FIRST, F32), tile_expert_f[:, bass.ds(i.g, 1)], None,
                                    ALU.is_equal).then_inc(meta_taken, 1)
                    V.tensor_scalar(norm[:], ratio[:], 1.0, None, ALU.add).then_inc(gate_step, 1)
                    dve.wait_ge(gate_step, i.g * 4 + 1)
                    V.reciprocal(norm[:], norm[:]).then_inc(gate_step, 1)
                    dve.wait_ge(gate_step, i.g * 4 + 2)
                    V.tensor_tensor(second[:], norm[:], ratio[:], ALU.mult).then_inc(gate_step, 1)
                    dve.wait_ge(gate_step, i.g * 4 + 3)
                    V.tensor_tensor(norm[:], norm[:], second[:], ALU.subtract).then_inc(gate_step, 1)
                    dve.wait_ge(gate_step, i.g * 4 + 4)
                    dve.wait_ge(meta_taken, i.g + 1)
                    V.tensor_tensor(norm[:], norm[:], is_first[:], ALU.mult).then_inc(norm_ready, 1)
                    dve.wait_ge(norm_ready, i.g + 1)
                    V.tensor_tensor(gate[:, i.par, :], norm[:], second[:], ALU.add).then_inc(gate_ready, 1)

                def add_bias(i):
                    e = expert_of(dve, i)
                    dve.wait_ge(out_done, i.g + 1)
                    wait(dve, gated, i.g * SUB)
                    for s in range(SUB):
                        last = V.scalar_tensor_tensor(yb[:, s, :], ps_out(i.par)[:, s, :], 1.0 / WSCALE,
                                                      b2[:, bass.ds(e * D, D)], ALU.mult, ALU.add)
                    last.then_inc(y_ready, 1)

                def splits(i):
                    for pair in range(PAIRS):
                        split(i, pair)

                rows_out(At(0, 0))
                splits(At(0, 0))
                gates(At(0, 0))
                rows_out(At(0, 1))
                splits(At(0, 1))
                rows_out(At(1, 0))
                dve.wait_ge(b2_loaded, 16)
                add_bias(At(0, 0))
                gates(At(0, 1))
                with dve.Fori(1, TILES // 2) as h:
                    for c in (0, 1):
                        splits(At(h, c))
                        rows_out(At(h, c + 1))
                        add_bias(At(h, c - 1))
                        gates(At(h, c))
                splits(At(TILES // 2, 0))
                add_bias(At(TILES // 2, -1))
                gates(At(TILES // 2, 0))
                add_bias(At(TILES // 2, 0))


def kernel(**inputs):
    import numpy as np
    import concourse.bacc as bacc
    from concourse.bass_utils import run_bass_kernel_spmd

    v = {name: np.asarray(a) for name, a in inputs.items()}
    adapter = {name[len("L0_cond_"):]: a for name, a in v.items() if name.startswith("L0_cond_")}
    moe = {name[len("L1_cond_"):]: a for name, a in v.items() if name.startswith("L1_cond_")}

    def columns(a):
        return a.reshape(-1, P).T

    w1 = moe["exp_w1"].reshape(EXPERTS, DC, P, FF).reshape(EXPERTS * DC, P, FF)
    w2 = moe["exp_w2"].reshape(EXPERTS, FC, P, D).transpose(0, 2, 1, 3).reshape(EXPERTS, P, DC, CHUNK)
    w2 = w2.transpose(0, 2, 1, 3).reshape(EXPERTS * DC, P, CHUNK)
    arrays = {
        "x": v["x"].reshape(TOKENS, D),
        "ids": v["itok_B_0_15"].reshape(1, ITEMS),
        "subject_ids": v["itok_B_6_14"].reshape(1, ITEMS),
        "down_w": adapter["down_W"].T.reshape(DC, P, A).transpose(1, 0, 2),
        "down_b": adapter["down_b"].reshape(A, 1),
        "up_w": adapter["up_W"].T,
        "up_b": adapter["up_b"].reshape(1, D),
        "adapter_w": np.concatenate([adapter["expert_W"].reshape(ADAPTERS, A * A),
                                     np.eye(A, dtype=np.float32).reshape(1, A * A)]),
        "adapter_b": adapter["expert_b"],
        "domain_emb": adapter["domain_emb"],
        "gamma0": adapter["ln_gamma"].reshape(1, D),
        "beta0": adapter["ln_beta"].reshape(1, D),
        "subj_emb": moe["subj_emb"],
        "hyp_w1": moe["hyp_w1"],
        "hyp_w2": moe["hyp_w2"],
        "sty_w1": moe["sty_w1"],
        "sty_b1": moe["sty_b1"].reshape(SH // 2, 1),
        "sty_w2": moe["sty_w2"],
        "feature": np.concatenate([columns(moe[n]) for n in
                                   ("ln_g", "ln_b", "hyp_b1", "hyp_b2", "sty_b2", "exp_b1")], axis=1),
        "router_w": moe["router_w"].reshape(DC, P, EXPERTS).transpose(1, 0, 2),
        "expert_w": np.concatenate([w1, w2], axis=0),
        "exp_b2": moe["exp_b2"].reshape(1, EXPERTS * D),
    }
    arrays = {name: np.ascontiguousarray(a) for name, a in arrays.items()}

    nc = bacc.Bacc("TRN2", target_bir_lowering=False, num_devices=1)
    args = {name: nc.dram_tensor(name, a.shape, mybir.dt.from_np(a.dtype), kind="ExternalInput").ap()
            for name, a in arrays.items()}
    out = nc.dram_tensor("out", (TOKENS + P, D), F32, kind="ExternalOutput").ap()
    build(nc, **args, out=out)
    result = run_bass_kernel_spmd(nc, [arrays], core_ids=[0])
    return result.results[0]["out"][:TOKENS].reshape(ITEMS, T, D)
```
